# Optimizing a Trainium2 kernel written in Bass

```python
import numpy as np
import jax
import jax.numpy as jnp

def _softmax(x, axis=-1):
    return jax.nn.softmax(x, axis=axis)

def _gelu(x):
    return jax.nn.gelu(x, approximate=True)

def _silu(x):
    return jax.nn.silu(x)

def _sigmoid(x):
    return jax.nn.sigmoid(x)

def _layernorm(x, axis=-1, eps=1e-05):
    m = jnp.mean(x, axis=axis, keepdims=True)
    v = jnp.var(x, axis=axis, keepdims=True)
    return (x - m) / jnp.sqrt(v + eps)

def _scatter_add(tgt, idx, src, axis=0):
    return tgt.at[idx].add(src)

def _segment_sum(src, seg, n):
    return jax.ops.segment_sum(src, seg, n)
kernel_name = 'mk_gps_d1_gnn_r8_19b7ab'

def setup_inputs(seed: int=0):
    np.random.seed(seed)
    _w = jnp.asarray

    def _rec_inputs():
        import jax
        import jax.numpy as jnp
        _gk = jax.random.key(seed)
        x = -8.776e-05 + 1 * jax.random.normal(jax.random.fold_in(_gk, 1), (2500, 256), jnp.float32)
        _s = jax.random.randint(jax.random.fold_in(_gk, 2), (20000,), 0, 2500, jnp.int32)
        _d = jax.random.randint(jax.random.fold_in(_gk, 3), (20000,), 0, 2500, jnp.int32)
        _loop = jnp.arange(2500, dtype=jnp.int32)
        src = jnp.concatenate([_s, _d, _loop])
        dst = jnp.concatenate([_d, _s, _loop])
        _o = jnp.argsort(dst, stable=True)
        src = src[_o]
        dst = dst[_o]
        edge_attr_18 = 0.000318098 + 1.00013 * jax.random.normal(jax.random.fold_in(_gk, 12), (42500, 18), jnp.float32)
        edge_attr_256 = -8.513e-05 + 0.999844 * jax.random.normal(jax.random.fold_in(_gk, 13), (42500, 256), jnp.float32)
        edge_attr_54 = 0.000309991 + 1.00005 * jax.random.normal(jax.random.fold_in(_gk, 14), (42500, 54), jnp.float32)
        return (x, src, dst, edge_attr_18, edge_attr_256, edge_attr_54)
    x, src, dst, edge_attr_18, edge_attr_256, edge_attr_54 = _rec_inputs()

    def _L0_gnn_setup():
        import jax, jax.numpy as jnp
        import numpy as np
        N, E, C, MID = (2500, 40000, 256, 64)
        NR, NS = (6, 3)
        F1_IN = NR * NS * NS
        F2_IN = NR * NS
        G = 64
        EPS = 1e-05
        NEG_SLOPE = 0.1

        def leaky(v):
            return jnp.where(v > 0, v, NEG_SLOPE * v)
        key = jax.random.key(seed)
        ks = jax.random.split(key, 26)

        def w(k, shape):
            fan_in = shape[0]
            return jax.random.normal(k, shape, dtype=jnp.float32) / jnp.sqrt(jnp.float32(fan_in))
        return {'x': jax.random.normal(ks[0], (N, C), dtype=jnp.float32), 'gate_edge': jax.random.normal(ks[1], (E, C), dtype=jnp.float32), 'feature1': jax.random.normal(ks[2], (E, F1_IN), dtype=jnp.float32), 'feature2': jax.random.normal(ks[3], (E, F2_IN), dtype=jnp.float32), 'edge_index': jax.random.randint(ks[4], (2, E), 0, N, dtype=jnp.int32), 'batch': jnp.sort(jax.random.randint(ks[5], (N,), 0, G, dtype=jnp.int32)), 'w_f1a': w(ks[6], (F1_IN, MID)), 'w_f1b': w(ks[7], (MID, C)), 'w_f2a': w(ks[8], (F2_IN, MID)), 'w_f2b': w(ks[9], (MID, C)), 'c1_wl': w(ks[10], (C, C)), 'c1_bl': jnp.zeros((C,), jnp.float32), 'c1_wr': w(ks[11], (C, C)), 'c2_wl': w(ks[12], (C, C)), 'c2_bl': jnp.zeros((C,), jnp.float32), 'c2_wr': w(ks[13], (C, C)), 'lin1_w': w(ks[14], (C, C)), 'lin1_b': jnp.zeros((C,), jnp.float32), 'lin2_w': w(ks[15], (C, C)), 'lin2_b': jnp.zeros((C,), jnp.float32), 'cat_w': w(ks[16], (2 * C, C)), 'cat_b': jnp.zeros((C,), jnp.float32), 'gn_w': jnp.ones((C,), jnp.float32), 'gn_b': jnp.zeros((C,), jnp.float32), 'gn_ms': jnp.ones((C,), jnp.float32)}
    _L0_gnn_all = _L0_gnn_setup()
    _L0_gnn_in = {k: v for k, v in _L0_gnn_all.items() if k in ('w_f1a', 'w_f1b', 'w_f2a', 'w_f2b', 'c1_wl', 'c1_bl', 'c1_wr', 'c2_wl', 'c2_bl', 'c2_wr', 'lin1_w', 'lin1_b', 'lin2_w', 'lin2_b', 'cat_w', 'cat_b', 'gn_w', 'gn_b', 'gn_ms')}
    del _L0_gnn_all

    def _L0_mix_setup():
        import jax, jax.numpy as jnp
        import numpy as np
        D_MODEL = 256
        NUM_HEADS = 8
        DEPTH = D_MODEL // NUM_HEADS
        B, L = (32, 512)

        def _feature_map(x):
            return jax.nn.elu(x) + 1.0
        key = jax.random.key(seed)
        ks = jax.random.split(key, 9)
        sc = 1.0 / np.sqrt(D_MODEL)
        return {'x': jax.random.normal(ks[0], (B, L, D_MODEL), dtype=jnp.float32), 'wq': jax.random.normal(ks[1], (D_MODEL, D_MODEL), dtype=jnp.float32) * sc, 'bq': jnp.zeros((D_MODEL,), dtype=jnp.float32), 'wk': jax.random.normal(ks[2], (D_MODEL, D_MODEL), dtype=jnp.float32) * sc, 'bk': jnp.zeros((D_MODEL,), dtype=jnp.float32), 'wv': jax.random.normal(ks[3], (D_MODEL, D_MODEL), dtype=jnp.float32) * sc, 'bv': jnp.zeros((D_MODEL,), dtype=jnp.float32), 'wo': jax.random.normal(ks[4], (D_MODEL, D_MODEL), dtype=jnp.float32) * sc, 'bo': jnp.zeros((D_MODEL,), dtype=jnp.float32)}
    _L0_mix_all = _L0_mix_setup()
    _L0_mix_in = {k: v for k, v in _L0_mix_all.items() if k in ('wq', 'bq', 'wk', 'bk', 'wv', 'bv', 'wo', 'bo')}
    del _L0_mix_all

    def _L0_ffn_setup():
        import jax, jax.numpy as jnp
        import numpy as np
        B, N, D = (16, 512, 256)
        NUM_EXPERTS, TOP_K, HEADS = (4, 2, 4)
        N_EDGES = 131072
        LN_EPS = 1e-05

        def _layernorm(x, g, b):
            mu = x.mean(-1, keepdims=True)
            var = ((x - mu) ** 2).mean(-1, keepdims=True)
            return (x - mu) * jax.lax.rsqrt(var + LN_EPS) * g + b

        def _forward(x, edge_index, W_gat, att_src, att_dst, b_gat, ln_gamma, ln_beta, W1, b1, W2, b2):
            Bc, Nc, Dc = x.shape
            M = Bc * Nc
            x_flat = x.reshape(M, Dc)
            h = (x_flat @ W_gat).reshape(M, HEADS, NUM_EXPERTS)
            loops = jnp.arange(M, dtype=edge_index.dtype)
            src = jnp.concatenate([edge_index[0], loops])
            dst = jnp.concatenate([edge_index[1], loops])
            a_src = (h * att_src).sum(-1)
            a_dst = (h * att_dst).sum(-1)
            e = jax.nn.leaky_relu(a_src[src] + a_dst[dst], negative_slope=0.2)
            e_max = jax.ops.segment_max(e, dst, num_segments=M)
            ee = jnp.exp(e - e_max[dst])
            denom = jax.ops.segment_sum(ee, dst, num_segments=M)
            alpha = ee / (denom[dst] + 1e-16)
            msg = h[src] * alpha[:, :, None]
            agg = jax.ops.segment_sum(msg, dst, num_segments=M).reshape(M, HEADS * NUM_EXPERTS) + b_gat
            scores = _layernorm(agg, ln_gamma, ln_beta).reshape(M, HEADS, NUM_EXPERTS).mean(1)
            scores = scores.reshape(Bc, Nc, NUM_EXPERTS)
            topk_s, topk_i = jax.lax.top_k(scores, TOP_K)
            w = jax.nn.softmax(topk_s, axis=-1)
            out = jnp.zeros_like(x)
            for ei in range(NUM_EXPERTS):
                g = jnp.where(topk_i == ei, w, 0.0).sum(-1)
                hh = jax.nn.gelu(x @ W1[ei] + b1[ei], approximate=False)
                out = out + g[..., None] * (hh @ W2[ei] + b2[ei])
            return out
        key = jax.random.key(seed)
        ks = jax.random.split(key, 8)
        s = 0.05
        return {'x': jax.random.normal(ks[0], (B, N, D), jnp.float32), 'W_gat': jax.random.normal(ks[1], (D, HEADS * NUM_EXPERTS), jnp.float32) * s, 'att_src': jax.random.normal(ks[2], (HEADS, NUM_EXPERTS), jnp.float32) * s, 'att_dst': jax.random.normal(ks[3], (HEADS, NUM_EXPERTS), jnp.float32) * s, 'b_gat': jnp.zeros((HEADS * NUM_EXPERTS,), jnp.float32), 'ln_gamma': jnp.ones((HEADS * NUM_EXPERTS,), jnp.float32), 'ln_beta': jnp.zeros((HEADS * NUM_EXPERTS,), jnp.float32), 'W1': jax.random.normal(ks[4], (NUM_EXPERTS, D, 2 * D), jnp.float32) * s, 'b1': jnp.zeros((NUM_EXPERTS, 2 * D), jnp.float32), 'W2': jax.random.normal(ks[5], (NUM_EXPERTS, 2 * D, D), jnp.float32) * s, 'b2': jnp.zeros((NUM_EXPERTS, D), jnp.float32), 'edge_index': jax.random.randint(ks[6], (2, N_EDGES), 0, B * N, jnp.int32)}
    _L0_ffn_all = _L0_ffn_setup()
    _L0_ffn_in = {k: v for k, v in _L0_ffn_all.items() if k in ('W_gat', 'att_src', 'att_dst', 'b_gat', 'ln_gamma', 'ln_beta', 'W1', 'b1', 'W2', 'b2', 'edge_index')}
    del _L0_ffn_all
    return {'x': x, 'src': src, 'dst': dst, 'edge_attr_18': edge_attr_18, 'edge_attr_256': edge_attr_256, 'edge_attr_54': edge_attr_54, 'L0_gnn_w_f1a': _L0_gnn_in['w_f1a'], 'L0_gnn_w_f1b': _L0_gnn_in['w_f1b'], 'L0_gnn_w_f2a': _L0_gnn_in['w_f2a'], 'L0_gnn_w_f2b': _L0_gnn_in['w_f2b'], 'L0_gnn_c1_wl': _L0_gnn_in['c1_wl'], 'L0_gnn_c1_bl': _L0_gnn_in['c1_bl'], 'L0_gnn_c1_wr': _L0_gnn_in['c1_wr'], 'L0_gnn_c2_wl': _L0_gnn_in['c2_wl'], 'L0_gnn_c2_bl': _L0_gnn_in['c2_bl'], 'L0_gnn_c2_wr': _L0_gnn_in['c2_wr'], 'L0_gnn_lin1_w': _L0_gnn_in['lin1_w'], 'L0_gnn_lin1_b': _L0_gnn_in['lin1_b'], 'L0_gnn_lin2_w': _L0_gnn_in['lin2_w'], 'L0_gnn_lin2_b': _L0_gnn_in['lin2_b'], 'L0_gnn_cat_w': _L0_gnn_in['cat_w'], 'L0_gnn_cat_b': _L0_gnn_in['cat_b'], 'L0_gnn_gn_w': _L0_gnn_in['gn_w'], 'L0_gnn_gn_b': _L0_gnn_in['gn_b'], 'L0_gnn_gn_ms': _L0_gnn_in['gn_ms'], 'L0_mix_wq': _L0_mix_in['wq'], 'L0_mix_bq': _L0_mix_in['bq'], 'L0_mix_wk': _L0_mix_in['wk'], 'L0_mix_bk': _L0_mix_in['bk'], 'L0_mix_wv': _L0_mix_in['wv'], 'L0_mix_bv': _L0_mix_in['bv'], 'L0_mix_wo': _L0_mix_in['wo'], 'L0_mix_bo': _L0_mix_in['bo'], 'L0_ffn_W_gat': _L0_ffn_in['W_gat'], 'L0_ffn_att_src': _L0_ffn_in['att_src'], 'L0_ffn_att_dst': _L0_ffn_in['att_dst'], 'L0_ffn_b_gat': _L0_ffn_in['b_gat'], 'L0_ffn_ln_gamma': _L0_ffn_in['ln_gamma'], 'L0_ffn_ln_beta': _L0_ffn_in['ln_beta'], 'L0_ffn_W1': _L0_ffn_in['W1'], 'L0_ffn_b1': _L0_ffn_in['b1'], 'L0_ffn_W2': _L0_ffn_in['W2'], 'L0_ffn_b2': _L0_ffn_in['b2'], 'L0_ffn_edge_index': _L0_ffn_in['edge_index']}

def reference(x, src, dst, edge_attr_18, edge_attr_256, edge_attr_54, L0_gnn_w_f1a, L0_gnn_w_f1b, L0_gnn_w_f2a, L0_gnn_w_f2b, L0_gnn_c1_wl, L0_gnn_c1_bl, L0_gnn_c1_wr, L0_gnn_c2_wl, L0_gnn_c2_bl, L0_gnn_c2_wr, L0_gnn_lin1_w, L0_gnn_lin1_b, L0_gnn_lin2_w, L0_gnn_lin2_b, L0_gnn_cat_w, L0_gnn_cat_b, L0_gnn_gn_w, L0_gnn_gn_b, L0_gnn_gn_ms, L0_mix_wq, L0_mix_bq, L0_mix_wk, L0_mix_bk, L0_mix_wv, L0_mix_bv, L0_mix_wo, L0_mix_bo, L0_ffn_W_gat, L0_ffn_att_src, L0_ffn_att_dst, L0_ffn_b_gat, L0_ffn_ln_gamma, L0_ffn_ln_beta, L0_ffn_W1, L0_ffn_b1, L0_ffn_W2, L0_ffn_b2, L0_ffn_edge_index):
    import jax
    import jax.numpy as jnp

    def _L0_gnn_ref(x, gate_edge, feature1, feature2, edge_index, batch, w_f1a, w_f1b, w_f2a, w_f2b, c1_wl, c1_bl, c1_wr, c2_wl, c2_bl, c2_wr, lin1_w, lin1_b, lin2_w, lin2_b, cat_w, cat_b, gn_w, gn_b, gn_ms):
        import jax, jax.numpy as jnp
        import numpy as np
        N, E, C, MID = (2500, 40000, 256, 64)
        NR, NS = (6, 3)
        F1_IN = NR * NS * NS
        F2_IN = NR * NS
        G = 64
        EPS = 1e-05
        NEG_SLOPE = 0.1

        def leaky(v):
            return jnp.where(v > 0, v, NEG_SLOPE * v)
        src, dst = (edge_index[0], edge_index[1])
        f1 = feature1 @ w_f1a @ w_f1b * gate_edge
        h1 = jax.ops.segment_sum(x[src] * f1, dst, num_segments=N)
        h1 = h1 @ c1_wl + c1_bl + x @ c1_wr
        h1 = leaky(h1 @ lin1_w + lin1_b)
        _dead = feature2 @ w_f2a @ w_f2b
        f2 = f1 * gate_edge
        h2 = jax.ops.segment_sum(x[src] * f2, dst, num_segments=N)
        h2 = h2 @ c2_wl + c2_bl + x @ c2_wr
        h2 = leaky(h2 @ lin2_w + lin2_b)
        h = jnp.concatenate([h1, h2], axis=1) @ cat_w + cat_b
        cnt = jnp.maximum(jax.ops.segment_sum(jnp.ones((N,), h.dtype), batch, num_segments=G), 1.0)[:, None]
        mean = jax.ops.segment_sum(h, batch, num_segments=G) / cnt
        out = h - mean[batch] * gn_ms
        var = jax.ops.segment_sum(out * out, batch, num_segments=G) / cnt
        std = jnp.sqrt(var + EPS)[batch]
        return gn_w * out / std + gn_b

    def _L0_mix_ref(x, wq, bq, wk, bk, wv, bv, wo, bo):
        import jax, jax.numpy as jnp
        import numpy as np
        D_MODEL = 256
        NUM_HEADS = 8
        DEPTH = D_MODEL // NUM_HEADS
        B, L = (32, 512)

        def _feature_map(x):
            return jax.nn.elu(x) + 1.0
        b, l, _ = x.shape
        q = (x @ wq + bq).reshape(b, l, NUM_HEADS, DEPTH)
        k = (x @ wk + bk).reshape(b, l, NUM_HEADS, DEPTH)
        v = (x @ wv + bv).reshape(b, l, NUM_HEADS, DEPTH)
        q = _feature_map(q)
        k = _feature_map(k)
        kv = jnp.einsum('blhd,blhe->bhde', k, v)
        k_sum = jnp.sum(k, axis=1)
        qkv = jnp.einsum('blhd,bhde->blhe', q, kv)
        normalizer = jnp.einsum('blhd,bhd->blh', q, k_sum) + 1e-06
        out = qkv / normalizer[..., None]
        out = out.reshape(b, l, D_MODEL)
        return out @ wo + bo

    def _L0_ffn_ref(x, W_gat, att_src, att_dst, b_gat, ln_gamma, ln_beta, W1, b1, W2, b2, edge_index):
        import jax, jax.numpy as jnp
        import numpy as np
        B, N, D = (16, 512, 256)
        NUM_EXPERTS, TOP_K, HEADS = (4, 2, 4)
        N_EDGES = 131072
        LN_EPS = 1e-05

        def _layernorm(x, g, b):
            mu = x.mean(-1, keepdims=True)
            var = ((x - mu) ** 2).mean(-1, keepdims=True)
            return (x - mu) * jax.lax.rsqrt(var + LN_EPS) * g + b

        def _forward(x, edge_index, W_gat, att_src, att_dst, b_gat, ln_gamma, ln_beta, W1, b1, W2, b2):
            Bc, Nc, Dc = x.shape
            M = Bc * Nc
            x_flat = x.reshape(M, Dc)
            h = (x_flat @ W_gat).reshape(M, HEADS, NUM_EXPERTS)
            loops = jnp.arange(M, dtype=edge_index.dtype)
            src = jnp.concatenate([edge_index[0], loops])
            dst = jnp.concatenate([edge_index[1], loops])
            a_src = (h * att_src).sum(-1)
            a_dst = (h * att_dst).sum(-1)
            e = jax.nn.leaky_relu(a_src[src] + a_dst[dst], negative_slope=0.2)
            e_max = jax.ops.segment_max(e, dst, num_segments=M)
            ee = jnp.exp(e - e_max[dst])
            denom = jax.ops.segment_sum(ee, dst, num_segments=M)
            alpha = ee / (denom[dst] + 1e-16)
            msg = h[src] * alpha[:, :, None]
            agg = jax.ops.segment_sum(msg, dst, num_segments=M).reshape(M, HEADS * NUM_EXPERTS) + b_gat
            scores = _layernorm(agg, ln_gamma, ln_beta).reshape(M, HEADS, NUM_EXPERTS).mean(1)
            scores = scores.reshape(Bc, Nc, NUM_EXPERTS)
            topk_s, topk_i = jax.lax.top_k(scores, TOP_K)
            w = jax.nn.softmax(topk_s, axis=-1)
            out = jnp.zeros_like(x)
            for ei in range(NUM_EXPERTS):
                g = jnp.where(topk_i == ei, w, 0.0).sum(-1)
                hh = jax.nn.gelu(x @ W1[ei] + b1[ei], approximate=False)
                out = out + g[..., None] * (hh @ W2[ei] + b2[ei])
            return out
        return _forward(x, edge_index, W_gat, att_src, att_dst, b_gat, ln_gamma, ln_beta, W1, b1, W2, b2)
    edge_index = jnp.stack([src, dst])
    batch0 = jnp.zeros((2500,), jnp.int32)
    xn = _layernorm(x, axis=-1)
    x = x + _L0_gnn_ref(xn, edge_attr_256, edge_attr_54, edge_attr_18, edge_index, batch0, L0_gnn_w_f1a, L0_gnn_w_f1b, L0_gnn_w_f2a, L0_gnn_w_f2b, L0_gnn_c1_wl, L0_gnn_c1_bl, L0_gnn_c1_wr, L0_gnn_c2_wl, L0_gnn_c2_bl, L0_gnn_c2_wr, L0_gnn_lin1_w, L0_gnn_lin1_b, L0_gnn_lin2_w, L0_gnn_lin2_b, L0_gnn_cat_w, L0_gnn_cat_b, L0_gnn_gn_w, L0_gnn_gn_b, L0_gnn_gn_ms) + _L0_mix_ref(xn[None], L0_mix_wq, L0_mix_bq, L0_mix_wk, L0_mix_bk, L0_mix_wv, L0_mix_bv, L0_mix_wo, L0_mix_bo)[0]
    x = x + _L0_ffn_ref(_layernorm(x, axis=-1)[None], L0_ffn_W_gat, L0_ffn_att_src, L0_ffn_att_dst, L0_ffn_b_gat, L0_ffn_ln_gamma, L0_ffn_ln_beta, L0_ffn_W1, L0_ffn_b1, L0_ffn_W2, L0_ffn_b2, L0_ffn_edge_index)[0]
    return x

_drawn_inputs = setup_inputs


def setup_inputs(seed=0):
    import zlib

    import numpy as np

    out = dict(_drawn_inputs(seed))
    spreads = {'L0_gnn_c1_bl': (0.0, 0.713),
     'L0_gnn_c2_bl': (0.0, 0.408),
     'L0_gnn_lin1_b': (0.0, 0.719),
     'L0_gnn_lin2_b': (0.0, 0.656),
     'L0_gnn_cat_b': (0.0, 0.513),
     'L0_gnn_gn_w': (1.0, 0.2),
     'L0_gnn_gn_b': (0.0, 0.1),
     'L0_gnn_gn_ms': (1.0, 0.2),
     'L0_mix_bq': (0.0, 0.8),
     'L0_mix_bk': (0.0, 0.8),
     'L0_mix_bv': (0.0, 0.1),
     'L0_mix_bo': (0.0, 0.1),
     'L0_ffn_b_gat': (0.0, 0.1),
     'L0_ffn_ln_gamma': (1.0, 0.2),
     'L0_ffn_ln_beta': (0.0, 0.1),
     'L0_ffn_b1': (0.0, 0.1),
     'L0_ffn_b2': (0.0, 0.1)}
    factors = {'L0_mix_wq': 8.0, 'L0_mix_wk': 2.804, 'L0_ffn_att_dst': 3.247}
    for name, (base, spread) in spreads.items():
        noise = np.random.default_rng([zlib.crc32(name.encode()), seed]).standard_normal(out[name].shape)
        drawn = base * np.exp(spread * noise) if base else spread * noise
        out[name] = jnp.asarray(drawn.astype(out[name].dtype))
    for name, factor in factors.items():
        out[name] = (out[name] * factor).astype(out[name].dtype)
    return out
```

```python
from contextlib import ExitStack

import numpy as np
import concourse.bass as bass
from concourse import mybir

ALU = mybir.AluOpType
ACT = mybir.ActivationFunctionType
F32 = mybir.dt.float32
BF16 = mybir.dt.bfloat16
I32 = mybir.dt.int32
AX = mybir.AxisListType.X
RMAX = bass.bass_isa.ReduceOp.max

P = 128
N = 2500
C = 256
NB = 125
T = N // NB
NW = 500
NC = N // NW
BW = NW // NB

E1 = 42500
CT = 7
CH = P * CT
NCH = 48
WIN = 128
NWIN = NCH // 2
DEPTH = 3
BODY = 12

E2 = 131072
EC = E2 // P
HEADS, NEXP = 4, 4
HE = HEADS * NEXP
TS = HE + HEADS
TD = 2 * HEADS
G = 6
HG = 3
ROUNDS = NC * NEXP
SORTS = 4
KCAP = EC + 8
RB = 50
CNT = 52
CCOLS = CNT * ROUNDS
HID = 512
HM = HID // P
HALF = NW // 2
MAGIC = 12582912.0
EPS = 1e-5


class Steps:

    def __init__(self, eng, sem):
        self.eng, self.sem, self.base, self.k = eng, sem, 0, 0

    def did(self, ins):
        ins.then_inc(self.sem, 1)
        self.k += 1

    def settle(self):
        self.eng.wait_ge(self.sem, self.base + self.k)

    def then(self, ins):
        self.did(ins)
        self.settle()

    def restart(self, base):
        self.base, self.k = base, 0


def build(nc, x, src, dst, ea54, ea256, edges, wf1aT, wf1b, wlrT, lin, catw, vecs,
          wkv, bkv, wq, wo, wgat, atts, attd, bgat, lng, lnb,
          w1, b1, w2, b2, out):
    with ExitStack() as ctx:
        def sb(name, shape, dt=F32):
            return ctx.enter_context(nc.sbuf_tensor(name, shape, dt))

        def sem(name):
            return ctx.enter_context(nc.semaphore(name))

        psum = ctx.enter_context(nc.psum_tensor("psum", [P, 8, 512], F32))
        bank = [psum[:, i, :] for i in range(8)]

        xn_d = nc.dram_tensor("xn_rows", [N, C], F32).ap()
        tsrc_d = nc.dram_tensor("source_rows", [N, TS], F32).ap()
        tdst_d = nc.dram_tensor("dest_rows", [N, TD], F32).ap()
        agg_d = nc.dram_tensor("counts", [RB, RB], F32).ap()

        x_rows = sb("x_rows", [P, T, C])
        xT = sb("xT", [P, 2, N])
        ident = sb("ident", [P, P])
        ones = sb("ones", [P, P])
        iota = sb("iota", [P, P])
        hmask = sb("hmask", [P, P])
        stats = sb("stats", [P, T, 6])
        mv = sb("mv", [P, T, 2])
        sd = sb("sd", [P, T])
        rs = sb("rs", [P, T])
        epsc = sb("epsc", [P, 1])
        NCOL = 14
        cols = sb("cols", [P, 2 * NCOL])
        b1c = sb("b1c", [P, NEXP * HM])
        fbias = sb("fbias", [P, 4])
        srt = sb("srt", [P, 8])
        small = sb("small", [P, 2 * NWIN])
        ared = sb("ared", [P, 2 * NWIN])
        cellf = sb("cellf", [P, 8])
        celli = sb("celli", [P, 8], I32)
        basei = sb("basei", [1, NWIN], I32)
        basef = sb("basef", [1, NWIN])
        drel = sb("drel", [P, NCH, CT])
        drel_w = drel[:, :, :].rearrange("p (w s) t -> p w (s t)", s=2)
        srci = sb("srci", [P, DEPTH, CT], I32)
        shared = sb("shared", [P, KCAP + 2 * CCOLS])
        wlr = shared[:, 0:2048].rearrange("p (w k n) -> p w k n", w=4, k=2)
        linw = shared[:, 2048:3072].rearrange("p (b k n) -> p b k n", b=2, k=2)
        kbuf = shared[:, 0:KCAP]
        cnt_a = shared[:, KCAP:KCAP + CCOLS]
        cnt_b = shared[:, KCAP + CCOLS:KCAP + 2 * CCOLS]
        wsum = [shared[:, 4 * P * i:4 * P * i + 4 * P] for i in range(2)]

        LOW = 20856
        low = sb("low", [P, LOW])
        HIGH = 15400
        high = sb("high", [P, HIGH])

        def cut(buf, off, *shape, dt=None):
            n = int(np.prod(shape))
            v = buf[:, off:off + n]
            if dt is not None:
                v = v.bitcast(dt)
                if dt == BF16:
                    shape = shape[:-1] + (shape[-1] * 2,)
            if len(shape) == 1:
                return v
            names = "abcd"[:len(shape)]
            return v.rearrange(f"p ({' '.join(names)}) -> p {' '.join(names)}",
                               **{c: s for c, s in zip(names[1:], shape[1:])})

        HTW = N + WIN
        hT = cut(low, 0, 4, HTW)
        o = 4 * HTW
        mixT = cut(low, o, 2, N); o += 2 * N
        fw = cut(low, o, 4, 2, C); o += 4 * 2 * C
        cat = cut(low, o, 4, C); o += 4 * C
        wo_s = cut(low, o, 2, C); o += 2 * C
        wq_s = cut(low, o, 2, C); o += 2 * C
        wf = cut(low, o, C); o += C
        assert o <= LOW
        rows_n = cut(low, 0, T, C)
        m = T * C
        wkv_s = cut(low, m, 2, 512); m += 1024
        bkv_s = cut(low, m, 512); m += 512
        kraw = cut(low, m, 2, C); m += 512
        kexp = cut(low, m, 2, C); m += 512
        vrow = cut(low, m, 2, 2, P + 1); m += 4 * (P + 1)
        kvbd = cut(low, m, 2, 2, P); m += 512
        assert m <= 4 * HTW
        m = 0
        qraw = cut(low, m, 2, NW); m += 2 * NW
        qexp = cut(low, m, 2, NW); m += 2 * NW
        nrm = cut(low, m, 2, NW); m += 2 * NW
        att = cut(low, m, 2, NW); m += 2 * NW
        assert m <= T * C
        Y = cut(low, 0, T, NEXP, C)
        o = 0
        msgs = [cut(high, o + i * CT * 2 * C, CT, 2 * C) for i in range(DEPTH)]; o += DEPTH * CT * 2 * C
        gath = [m[:, :, 0:C] for m in msgs]
        gate = [m[:, :, C:2 * C] for m in msgs]
        sel = [cut(high, o + i * CT * WIN, CT, WIN) for i in range(2)]; o += 2 * CT * WIN
        FEAT = o
        feat = [cut(high, o + i * CH, CT, P) for i in range(2)]
        o += 2 * CH
        assert o <= HIGH, o
        W1s = [cut(high, i * 2048, 2, HID) for i in range(2)]
        W2s = [cut(high, i * 2048 + 1024, HM, C) for i in range(2)]
        o = 4096
        HT = cut(high, o, 2, N)
        rows2 = cut(high, o, T, C); o += T * C
        ybuf = cut(high, o, NW); ysq = cut(high, o, NW); o += NW
        L = cut(high, o, 4, NW); o += 4 * NW
        esrc = cut(high, o, EC, dt=I32); ekey = cut(high, o, EC); o += EC
        edst = cut(high, o, EC, dt=I32); o += EC
        emask = cut(high, o, EC); o += EC
        assert o <= HIGH, o
        o = 4096 + T * C
        tab = cut(high, o, T, 24); o += T * 24
        td = cut(high, o, T, TD); o += T * TD
        b2b = cut(high, o, NEXP * C); o += NEXP * C
        kI = cut(high, o, G, dt=I32); o += 8
        sI = cut(high, o, G, dt=I32); o += 8
        dI = cut(high, o, G, dt=I32); o += 8
        dG = cut(high, o, G, dt=I32); o += 8
        hi_ = cut(high, o, G); o += 8
        lo_ = cut(high, o, G); o += 8
        GA = cut(high, o, G, TS); o += G * TS
        GB = cut(high, o, G, TD); o += G * TD
        z = cut(high, o, G, HEADS); o += G * HEADS
        ez = cut(high, o, G, HEADS); o += G * HEADS
        V = cut(high, o, G, TS); o += G * TS
        OH = cut(high, o, G, T); o += G * T
        last = cut(high, o, 24); o += 24
        bgb = cut(high, o, 3 * HE); o += 3 * HE
        wg = cut(high, o, 2, 24); o += 48
        attb = cut(high, o, 2 * HE); o += 2 * HE
        mx = cut(high, o, 16); o += 16
        mall = cut(high, o, 16); o += 16
        GATS = o
        o = 4096
        hid = [cut(high, o + i * HM * HALF, HM, HALF) for i in range(2)]; o += 2 * HM * HALF
        outer = [cut(high, o + i * HG * T * TS, HG, T, TS) for i in range(2)]; o += 2 * HG * T * TS
        assert o <= 4096 + T * C, o
        o = GATS
        lo1 = [cut(high, o + i * HG * P, HG, P) for i in range(2)]; o += 2 * HG * P
        oa = cut(high, o, CNT, RB // 2, dt=BF16); o += CNT * RB // 2
        ob = cut(high, o, CNT, RB // 2, dt=BF16); o += CNT * RB // 2
        zeros = cut(high, o, 400); o += 400
        assert o <= HIGH, o
        o = 0
        agg = cut(high, o, T, TS); o += T * TS
        f1 = cut(high, o, T, HE); o += T * HE
        f2 = cut(high, o, T, HE); o += T * HE
        es = cut(high, o, T, HEADS); o += T * HEADS
        el = cut(high, o, T, HEADS); o += T * HEADS
        cn = cut(high, o, T); o += T
        sc = cut(high, o, T, 4); o += T * 4
        rk = cut(high, o, T, 4); o += T * 4
        gg = cut(high, o, T, 4); o += T * 4
        cc = cut(high, o, 64); o += 64
        t1 = cut(high, o, T); o += T
        t2 = cut(high, o, T); o += T
        assert o <= 4096

        def col(i, mm):
            return cols[:, 2 * i + mm:2 * i + mm + 1]

        (CBL1, CBL2, CLB1, CLB2, CCAT, CGW, CGB, CGM, CBQ, CBO, CMU, CA, CBB, CVAR) = range(NCOL)

        s_x = sem("x_loaded")
        s_w = [sem(f"weights_loaded{i}") for i in range(3)]
        s_cst = sem("constants_made")
        s_pool = sem("pool_steps")
        s_vec = sem("vector_steps")
        s_vec2 = sem("vector_steps_second_half")
        s_mark = sem("waits_passed")
        s_act = sem("scalar_steps")
        s_fold = sem("folds_multiplied")
        s_foldc = sem("folds_copied")
        s_st = sem("stats_ready")
        s_sd = sem("deviation_ready")
        s_xn = sem("rows_normalised")
        s_xnd = sem("rows_stored")
        s_tp = sem("rows_transposed")
        s_tc = sem("transposes_copied")
        s_kv = sem("kv_multiplied")
        s_kvu = sem("kv_taken")
        s_km = sem("k_clipped")
        s_ke = sem("k_exponent")
        s_pk = sem("k_feature_ready")
        s_kvs = sem("kv_summed")
        s_bd = sem("kv_masked")
        s_q = sem("q_multiplied")
        s_qr = sem("q_taken")
        s_qm = sem("q_clipped")
        s_qe = sem("q_exponent")
        s_pq = sem("q_feature_ready")
        s_qn = sem("attention_multiplied")
        s_at = sem("attention_normalised")
        s_wo = sem("mix_multiplied")
        s_mix = sem("mix_taken")
        s_dl = sem("destinations_loaded")
        s_dm = sem("windows_measured")
        s_ar = sem("reduced_over_partitions")
        s_base = sem("window_bases_ready")
        s_gate = [sem(f"gate_loaded{i}") for i in range(DEPTH)]
        s_idx = [sem(f"indices_loaded{i}") for i in range(DEPTH)]
        s_feat = [sem(f"features_loaded{i}") for i in range(2)]
        s_gath = [sem(f"sources_gathered{i}") for i in range(DEPTH)]
        s_lin = sem("filters_multiplied")
        s_linf = sem("filters_taken")
        s_m1 = sem("first_messages_ready")
        s_msg = sem("messages_ready")
        s_nb = sem("windows_moved")
        s_scat = sem("messages_summed")
        s_wcp = sem("window_copied")
        s_wt = sem("window_transposed")
        s_acc = sem("window_added")
        s_fz = sem("padding_cleared")
        s_el = sem("second_edges_loaded")
        s_de = sem("dense_multiplied")
        s_da = sem("dense_biased")
        s_dL = sem("dense_leaky")
        s_cp = sem("cat_multiplied")
        s_ct = sem("cat_taken")
        s_gs = sem("graphnorm_squares")
        s_gv = sem("graphnorm_steps")
        s_gq = sem("graphnorm_root")
        s_yT = sem("sum_by_feature_ready")
        s_yb = sem("sum_transposed")
        s_x1 = sem("sum_rows_ready")
        s_w1 = [sem(f"expert_weights_loaded{i}") for i in range(2)]
        s_gl = sem("gat_vectors_loaded")
        s_wg = sem("gat_weights_ready")
        s_tt = sem("tables_multiplied")
        s_tm = sem("logits_reduced")
        s_tb = sem("tables_ready")
        s_ts = sem("tables_stored")
        s_last = sem("last_source_loaded")
        s_ki = sem("round_indices_ready")
        s_gg = sem("round_gathered")
        s_z = sem("logits_ready")
        s_ez = sem("exponents_ready")
        s_out = sem("outer_ready")
        s_sc = sem("outer_summed")
        s_cnt = sem("counts_ready")
        s_cs = sem("counts_summed")
        s_zero = sem("sums_cleared")
        s_h1 = sem("hidden_multiplied")
        s_h2 = sem("hidden_ready")
        s_y = sem("expert_multiplied")
        s_yt = sem("expert_taken")
        s_wfree = sem("expert_weights_free")
        s_cst2 = sem("counts_copied")
        s_cd = sem("counts_stored")
        s_cl = sem("counts_loaded")
        s_a1 = sem("last_exponents")
        s_fin = sem("rows_finished")
        s_o = sem("output_stored")

        x_v = x.rearrange("(t p) c -> p t c", p=NB)
        out_v = out.rearrange("(t p) c -> p t c", p=NB)
        xn_v = xn_d.rearrange("(t p) c -> p t c", p=NB)

        block = ctx.enter_context(nc.Block())

        def over(v, *shape):
            return v.unsqueeze(len(shape) - 1).broadcast_to(shape)

        @block.sync
        def _(sp):
            for g in range(NC):
                sp.dma_start(x_rows[0:NB, BW * g:BW * g + BW, :], x_v[:, BW * g:BW * g + BW, :]).then_inc(s_x, 16)
            sp.dma_start(drel[:, :, :].bitcast(I32), dst.rearrange("c p t -> p c t")).then_inc(s_dl, 16)
            sp.dma_start(wlr, wlrT.rearrange("w (k p) n -> p w k n", p=P)).then_inc(s_w[0], 16)
            sp.dma_start(linw, lin.rearrange("b (k p) n -> p b k n", p=P)).then_inc(s_w[0], 16)
            sp.dma_start(high[0:64, 0:54], wf1aT).then_inc(s_w[0], 16)
            sp.dma_start(high[0:64, 64:64 + C], wf1b).then_inc(s_w[0], 16)
            sp.dma_start(cols[:, 0:2 * CMU], vecs).then_inc(s_w[0], 16)
            sp.dma_start(b1c[:, :], b1).then_inc(s_w[0], 16)
            sp.dma_start(wkv_s, wkv.rearrange("(k p) n -> p k n", p=P)).then_inc(s_w[1], 16)
            sp.dma_start(bkv_s, bkv.partition_broadcast(P)).then_inc(s_w[1], 16)
            sp.dma_start(wq_s, wq.rearrange("(k p) n -> p k n", p=P)).then_inc(s_w[1], 16)
            sp.dma_start(wo_s, wo.rearrange("(k p) n -> p k n", p=P)).then_inc(s_w[1], 16)
            sp.dma_start(cat, catw.rearrange("(k p) n -> p k n", p=P)).then_inc(s_w[1], 16)
            for g in range(NC):
                sp.wait_ge(s_xn, BW * (g + 1))
                sp.dma_start(xn_v[:, BW * g:BW * g + BW, :], rows_n[0:NB, BW * g:BW * g + BW, :]).then_inc(s_xnd, 16)
            sp.wait_ge(s_base, 1)
            npass = sp.value_load(celli[0:1, 0:1], min_val=1, max_val=N // WIN + 1)
            sp.wait_ge(s_fold, 3)
            sp.wait_ge(s_fz, 1)
            with sp.Fori(0, npass) as p:
                with sp.Fori(0, NCH // 6) as i:
                    for j in range(6):
                        q = p * NCH + i * 6 + j
                        c = i * 6 + j
                        sp.wait_ge(s_lin, q * 2 + 2)
                        sp.dma_start(feat[j % 2][0:54], ea54[bass.ds(c, 1)].rearrange("o f t p -> (o f) t p")
                                     ).then_inc(s_feat[j % 2], 16)
                        sp.wait_ge(s_scat, q + 1)
                        sp.dma_start(srci[:, j % DEPTH, :], src[bass.ds(c, 1)].rearrange("o p t -> (o p) t")
                                     ).then_inc(s_idx[j % DEPTH], 16)
                        sp.dma_start(gate[j % DEPTH], ea256[bass.ds(c, 1)].rearrange("o p (t c) -> (o p) t c", t=CT)
                                     ).then_inc(s_gate[j % DEPTH], 16)
            sp.wait_ge(s_scat, npass * NCH + DEPTH)
            sp.dma_start(esrc, edges[0].rearrange("(p c) -> p c", p=P)).then_inc(s_el, 16)
            sp.dma_start(edst, edges[1].rearrange("(p c) -> p c", p=P)).then_inc(s_el, 16)
            for e in range(2):
                sp.dma_start(W1s[e], w1[e].rearrange("(k p) n -> p k n", p=P)).then_inc(s_w1[e], 16)
                sp.dma_start(W2s[e], w2[e].rearrange("(k p) n -> p k n", p=P)).then_inc(s_w1[e], 16)
            sp.wait_ge(s_yT, 1)
            sp.dma_start(wg[:, :, 0:HE], wgat.rearrange("(k p) n -> p k n", p=P)).then_inc(s_gl, 16)
            sp.dma_start(attb[:, 0:HE], atts.partition_broadcast(P)).then_inc(s_gl, 16)
            sp.dma_start(attb[:, HE:2 * HE], attd.partition_broadcast(P)).then_inc(s_gl, 16)
            for i, v in enumerate((bgat, lng, lnb)):
                sp.dma_start(bgb[:, HE * i:HE * i + HE], v.partition_broadcast(P)).then_inc(s_gl, 16)
            sp.dma_start(b2b, b2.rearrange("e c -> (e c)").partition_broadcast(P)).then_inc(s_gl, 16)
            sp.wait_ge(s_tb, 1)
            sp.dma_start(tsrc_d.rearrange("(t p) c -> p t c", p=NB), tab[0:NB, :, 0:TS]).then_inc(s_ts, 16)
            sp.wait_ge(s_tb, 2)
            sp.dma_start(tdst_d.rearrange("(t p) c -> p t c", p=NB), td[0:NB]).then_inc(s_ts, 16)
            sp.wait_ge(s_ts, 32)
            sp.dma_start(last[:, 0:TS], tsrc_d[N - 1, :].partition_broadcast(P)).then_inc(s_last, 16)
            for e in range(2, NEXP):
                sp.wait_ge(s_y, 2 + 2 * NC * (e - 1))
                sp.dma_start(W1s[e % 2], w1[e].rearrange("(k p) n -> p k n", p=P)).then_inc(s_w1[e % 2], 16)
                sp.dma_start(W2s[e % 2], w2[e].rearrange("(k p) n -> p k n", p=P)).then_inc(s_w1[e % 2], 16)
            sp.wait_ge(s_cst2, 1)
            sp.dma_start(agg_d, cc[0:RB, 0:RB]).then_inc(s_cd, 16)
            sp.wait_ge(s_cd, 16)
            sp.dma_start(cn[0:NB], agg_d.rearrange("a b -> (a b)").rearrange("(t p) -> p t", p=NB),
                         allow_slow_non_contiguous=True).then_inc(s_cl, 16)
            for g in range(NC):
                sp.wait_ge(s_fin, g + 1)
                sp.dma_start(out_v[:, BW * g:BW * g + BW, :], x_rows[0:NB, BW * g:BW * g + BW, :]).then_inc(s_o, 16)
            sp.wait_ge(s_o, 16 * NC)

        @block.gpsimd
        def _(pool):
            pool.memset(ident[:, :], 0.0).then_inc(s_pool, 1)
            pool.wait_ge(s_pool, 1)
            pool.affine_select(out=ident[:, :], in_=ident[:, :], compare_op=ALU.not_equal, fill=1.0, base=0,
                               pattern=[[-1, P]], channel_multiplier=1).then_inc(s_cst, 1)
            pool.iota(iota[:, :], pattern=[[1, P]], base=0, channel_multiplier=0,
                      allow_small_or_imprecise_dtypes=True).then_inc(s_cst, 1)
            pool.wait_ge(s_dm, 1)
            pool.partition_all_reduce(ared[:, :], small[:, :], P, RMAX).then_inc(s_ar, 1)
            pool.wait_ge(s_xnd, 16 * NC)
            pool.wait_ge(s_base, 1)
            npass = pool.value_load(celli[0:1, 0:1], min_val=1, max_val=N // WIN + 1)
            with pool.Fori(0, npass) as p:
                with pool.Fori(0, NCH // DEPTH) as i:
                    for j in range(DEPTH):
                        pool.wait_ge(s_idx[j], (p * (NCH // DEPTH) + i) * 16 + 16)
                        pool.sem_inc(s_mark, 1)
                        for t in range(CT):
                            pool.indirect_dma_start(
                                gath[j][:, t, :], None, xn_d,
                                bass.IndirectOffsetOnAxis(ap=srci[:, j, t:t + 1], axis=0)).then_inc(s_gath[j], 16)
            pool.wait_ge(s_dm, 2)
            pool.partition_all_reduce(ared[:, 0:1], small[:, 0:1], P, RMAX).then_inc(s_ar, 1)
            pool.wait_ge(s_tm, 1)
            pool.partition_all_reduce(mall[0:NB, 0:4], mx[0:NB, 0:4], NB, RMAX).then_inc(s_ar, 1)
            pool.wait_ge(s_ts, 32)
            rem = pool.value_load(celli[0:1, 2:3], min_val=1, max_val=(EC - G * ROUNDS) // G + 1)

            def gathers(r):
                pool.wait_ge(s_ki, r + 1)
                pool.sem_inc(s_mark, 1)
                for t in range(G):
                    pool.indirect_dma_start(GA[:, t, :], None, tsrc_d,
                                            bass.IndirectOffsetOnAxis(ap=sI[:, t:t + 1], axis=0)).then_inc(s_gg, 16)
                    pool.indirect_dma_start(GB[:, t, :], None, tdst_d,
                                            bass.IndirectOffsetOnAxis(ap=dG[:, t:t + 1], axis=0)).then_inc(s_gg, 16)

            with pool.Fori(0, ROUNDS) as r:
                gathers(r)
            with pool.Fori(0, rem) as r:
                gathers(r + ROUNDS)

        @block.tensor
        def _(pe):
            pe.wait_ge(s_w[0], 16 * 6)
            pe.matmul(bank[0][0:54, 0:C], high[0:64, 0:54], high[0:64, 64:64 + C],
                      start=True, stop=True).then_inc(s_fold, 1)
            for w in range(4):
                for mm in range(2):
                    for k in range(2):
                        ins = pe.matmul(bank[1 + w][:, C * mm:C * mm + C], wlr[:, w, k, P * mm:P * mm + P],
                                        linw[:, w // 2, k, :], start=(k == 0), stop=(k == 1))
            ins.then_inc(s_fold, 1)
            for b in range(2):
                for mm in range(2):
                    for k in range(2):
                        ins = pe.matmul(bank[5][:, 2 * b + mm:2 * b + mm + 1], linw[:, b, k, P * mm:P * mm + P],
                                        col(CBL1 + b, k), start=(k == 0), stop=(k == 1))
            ins.then_inc(s_fold, 1)
            pe.wait_ge(s_cst, 1)

            def turn_rows(rows, ready0, used0):
                for g in range(NC):
                    pe.wait_ge(s_xn, ready0 + BW * (g + 1))
                    for k in range(2):
                        u = used0 + 2 * g + k
                        if u >= 4:
                            pe.wait_ge(s_tc, u - 3)
                        for b in range(BW):
                            ins = pe.transpose(bank[u % 4][:, NB * b:NB * b + NB],
                                               rows[0:NB, BW * g + b, P * k:P * k + P], ident[0:NB, 0:NB])
                        ins.then_inc(s_tp, 1)

            pe.wait_ge(s_foldc, 2)
            turn_rows(rows_n, 0, 0)
            pe.wait_ge(s_w[1], 16 * 5)

            def kv_sum(t):
                pe.wait_ge(s_pk, t + 1)
                for c in range(2):
                    ins = pe.matmul(bank[6 + c][:, 0:P + 1], kraw[0:NB, t % 2, P * c:P * c + P],
                                    vrow[0:NB, t % 2, c, :], start=(t == 0), stop=(t == T - 1))
                ins.then_inc(s_kvs, 1)

            for t in range(T):
                pe.wait_ge(s_tc, 2 * (t // BW) + 2)
                if t >= 2:
                    pe.wait_ge(s_kvu, t - 1)
                else:
                    pe.wait_ge(s_foldc, 3)
                for k in range(2):
                    ins = pe.matmul(bank[4 + t % 2][0:NB, :], xT[:, k, NB * t:NB * t + NB], wkv_s[:, k, :],
                                    start=(k == 0), stop=(k == 1))
                ins.then_inc(s_kv, 1)
                if t >= 1:
                    kv_sum(t - 1)
            kv_sum(T - 1)
            pe.wait_ge(s_tc, 2 * NC)
            with pe.Fori(0, NC) as n:
                for c in range(2):
                    for k in range(2):
                        ins = pe.matmul(bank[c][:, 0:NW], wq_s[:, k, P * c:P * c + P], xT[:, k, bass.ds(n * NW, NW)],
                                        start=(k == 0), stop=(k == 1))
                    ins.then_inc(s_q, 1)
                pe.wait_ge(s_bd, 1)
                for c in range(2):
                    pe.wait_ge(s_pq, n * 2 + c + 1)
                    pe.matmul(bank[2 + 2 * c][:, 0:NW], kvbd[:, c, 0, :], qraw[:, c, :], start=True, stop=True)
                    pe.matmul(bank[3 + 2 * c][:, 0:NW], kvbd[:, c, 1, :], qraw[:, c, :],
                              start=True, stop=True).then_inc(s_qn, 1)
                pe.wait_ge(s_at, n * 2 + 2)
                for mm in range(2):
                    for k in range(2):
                        ins = pe.matmul(bank[6 + mm][:, 0:NW], wo_s[:, k, P * mm:P * mm + P], att[:, k, :],
                                        start=(k == 0), stop=(k == 1))
                    ins.then_inc(s_wo, 1)
            pe.wait_ge(s_mix, 2 * NC)

            pe.wait_ge(s_base, 1)
            npass = pe.value_load(celli[0:1, 0:1], min_val=1, max_val=N // WIN + 1)

            def filters(q, use, j):
                pe.wait_ge(s_feat[j % 2], use * 16)
                for h, tiles in enumerate((range(0, 4), range(4, CT))):
                    pe.wait_ge(s_linf, q * 2 + (h + 1))
                    for t in tiles:
                        ins = pe.matmul(bank[2 + t // 2][:, C * (t % 2):C * (t % 2) + C],
                                        feat[j % 2][:, t, :], wf, start=True, stop=True)
                    ins.then_inc(s_lin, 1)

            def sums(q, j):
                w = j // 2
                if j % 2 == 0:
                    pe.wait_ge(s_wcp, (q >> 1) + 1)
                for h, tiles in enumerate((range(0, 4), range(4, CT))):
                    pe.wait_ge(s_msg, q * 2 + (h + 1))
                    for t in tiles:
                        ins = pe.matmul(bank[w % 2], sel[j % 2][:, t, :], msgs[j % DEPTH][:, t, :],
                                        start=(j % 2 == 0 and t == 0), stop=(j % 2 == 1 and t == CT - 1),
                                        skip_group_check=True)
                ins.then_inc(s_scat, 1)

            def turn_window(v, w):
                pe.wait_ge(s_wcp, v + 3)
                pe.wait_ge(s_acc, v + 1)
                for f in range(4):
                    ins = pe.transpose(bank[6 + w % 2][:, P * f:P * f + P], wsum[w % 2][:, P * f:P * f + P],
                                       ident[:, :])
                ins.then_inc(s_wt, 1)

            with pe.Fori(0, npass) as p:
                for j in range(2):
                    filters(p * NCH + j, p * (NCH // 2) + 1, j)
                with pe.Fori(0, NCH // BODY - 1) as i:
                    for j in range(BODY):
                        sums(p * NCH + i * BODY + j, j)
                        filters(p * NCH + i * BODY + (j + 2), p * (NCH // 2) + i * (BODY // 2) + (j // 2 + 2), j)
                        if j % 2:
                            turn_window(p * NWIN + i * (BODY // 2) + j // 2, j // 2)
                for j in range(BODY):
                    c = NCH - BODY + j
                    sums(p * NCH + c, j)
                    if c + 2 < NCH:
                        filters(p * NCH + (c + 2), p * (NCH // 2) + (c // 2 + 2), j)
                    if j % 2:
                        turn_window(p * NWIN + c // 2, j // 2)

            pe.wait_ge(s_acc, npass * NWIN + 2)
            pe.sem_inc(s_mark, 1)
            with pe.Fori(0, NC) as n:
                for b in range(2):
                    for mm in range(2):
                        u = 2 * b + mm
                        pe.wait_ge(s_da, n * 4 + (u + 1))
                        for k in range(2):
                            pe.matmul(bank[u][:, 0:NW], fw[:, 2 * b, k, P * mm:P * mm + P],
                                      hT[:, 2 * b + k, bass.ds(n * NW, NW)], start=(k == 0), stop=False)
                        for k in range(2):
                            ins = pe.matmul(bank[u][:, 0:NW], fw[:, 2 * b + 1, k, P * mm:P * mm + P],
                                            xT[:, k, bass.ds(n * NW, NW)], start=False, stop=(k == 1))
                        ins.then_inc(s_de, 1)
                pe.wait_ge(s_dL, n * 4 + 4)
                for mm in range(2):
                    pe.wait_ge(s_ct, n * 2 + (mm + 1))
                    for k in range(4):
                        ins = pe.matmul(bank[4 + mm][:, 0:NW], cat[:, k, P * mm:P * mm + P], L[:, k, :],
                                        start=(k == 0), stop=(k == 3))
                    ins.then_inc(s_cp, 1)
            pe.wait_ge(s_yT, 1)
            for t in range(T):
                if t >= 4:
                    pe.wait_ge(s_x1, t - 3)
                for k in range(2):
                    ins = pe.transpose(bank[t % 4][0:NB, P * k:P * k + P], mixT[:, k, NB * t:NB * t + NB], ident[:, :])
                ins.then_inc(s_yb, 1)
            pe.wait_ge(s_x1, T)
            turn_rows(rows2, T, 2 * NC)
            pe.wait_ge(s_tc, 4 * NC)
            pe.wait_ge(s_wg, 1)
            for t in range(T):
                for k in range(2):
                    ins = pe.matmul(bank[4][0:NB, 24 * t:24 * t + 24], xT[:, k, NB * t:NB * t + NB], wg[:, k, :],
                                    start=(k == 0), stop=(k == 1))
            ins.then_inc(s_tt, 1)
            pe.wait_ge(s_zero, 1)
            pe.matmul(bank[6][0:NB, 0:T * TS], zeros[:, 0:NB], zeros[:, 0:T * TS], start=True, stop=True,
                      skip_group_check=True)
            pe.matmul(bank[7][0:RB, 0:RB], zeros[:, 0:RB], zeros[:, 0:RB], start=True, stop=True,
                      skip_group_check=True)
            pe.wait_ge(s_tb, 2)
            rem = pe.value_load(celli[0:1, 2:3], min_val=1, max_val=(EC - G * ROUNDS) // G + 1)

            def edge_sums(r):
                for h in range(2):
                    pe.wait_ge(s_out, r * 2 + (h + 1))
                    for t in range(HG):
                        ins = pe.matmul(bank[6][0:NB, 0:T * TS], lo1[h][:, t, 0:NB],
                                        outer[h][:, t].rearrange("p a b -> p (a b)"), start=False, stop=True,
                                        skip_group_check=True)
                    ins.then_inc(s_sc, 1)

            for e in range(NEXP):
                pe.wait_ge(s_w1[e % 2], 32 * (e // 2 + 1))
                with pe.Fori(0, NC) as n:
                    r = n + e * NC
                    for h in range(2):
                        for mm in range(HM):
                            pe.wait_ge(s_h2, r * 8 + (h * 4 + mm + 1))
                            for k in range(2):
                                ins = pe.matmul(bank[mm][:, 0:HALF],
                                                W1s[e % 2][:, k, P * mm:P * mm + P],
                                                xT[:, k, bass.ds(n * NW + h * HALF, HALF)],
                                                start=(k == 0), stop=(k == 1))
                            ins.then_inc(s_h1, 1)
                    for h in range(2):
                        pe.wait_ge(s_h2, r * 8 + (h * 4 + 8))
                        pe.wait_ge(s_yt, r * 2 + (h + 1))
                        for b in range(2):
                            for k in range(HM):
                                ins = pe.matmul(bank[4 + h][0:NB, C * b:C * b + C], hid[h][:, k, NB * b:NB * b + NB],
                                                W2s[e % 2][:, k, :], start=(k == 0), stop=(k == HM - 1))
                        ins.then_inc(s_y, 1)
                    pe.wait_ge(s_cnt, r + 1)
                    for t in range(CNT):
                        ins = pe.matmul(bank[7][0:RB, 0:RB], oa[:, t, :], ob[:, t, :],
                                        start=False, stop=True, skip_group_check=True)
                    ins.then_inc(s_cs, 1)
                    edge_sums(r)
            with pe.Fori(0, rem) as r:
                edge_sums(r + ROUNDS)

        @block.scalar
        def _(act):
            act.sem_inc(s_linf, 2)
            act.sem_inc(s_lin, 4)
            act.sem_inc(s_scat, DEPTH)
            act.sem_inc(s_wcp, 2)
            act.sem_inc(s_acc, 2)
            act.sem_inc(s_wt, 2)
            act.sem_inc(s_sc, 2)
            act.sem_inc(s_cs, 1)
            act.sem_inc(s_yt, 2)
            act.sem_inc(s_y, 2)
            act.sem_inc(s_h2, 4)
            act.sem_inc(s_da, 4)
            act.sem_inc(s_ct, 2)
            act.sem_inc(s_cp, 2)
            act.sem_inc(s_qn, 2)

            def deviation(k):
                act.wait_ge(s_st, k)
                act.activation(sd[0:NB, :], mv[0:NB, :, 1], ACT.Sqrt, bias=epsc[0:NB, :]).then_inc(s_sd, 1)

            act.wait_ge(s_fold, 1)
            act.wait_ge(s_fz, 1)
            act.copy(wf[0:54, :], bank[0][0:54, 0:C]).then_inc(s_foldc, 1)
            act.wait_ge(s_fold, 3)
            for w in range(4):
                ins = act.copy(fw[:, w, :, :].rearrange("p a b -> p (a b)"), bank[1 + w])
            ins.then_inc(s_foldc, 1)
            deviation(1)

            def turned(used0):
                for g in range(NC):
                    for k in range(2):
                        u = used0 + 2 * g + k
                        act.wait_ge(s_tp, u + 1)
                        act.copy(xT[:, k, NW * g:NW * g + NW], bank[u % 4][:, 0:NW]).then_inc(s_tc, 1)

            turned(0)
            for t in range(T):
                act.wait_ge(s_km, t + 1)
                act.activation(kexp[0:NB, t % 2, :], kexp[0:NB, t % 2, :], ACT.Exp).then_inc(s_ke, 1)
            act.wait_ge(s_xnd, 16 * NC)
            with act.Fori(0, NC) as n:
                act.wait_ge(s_qn, n * 2 + 2)
                for c in range(2):
                    act.wait_ge(s_q, n * 2 + (c + 1))
                    act.activation(qraw[:, c, :], bank[c][:, 0:NW], ACT.Identity, bias=col(CBQ, c)).then_inc(s_qr, 1)
                for c in range(2):
                    act.wait_ge(s_qm, n * 2 + (c + 1))
                    act.activation(qexp[:, c, :], qexp[:, c, :], ACT.Exp).then_inc(s_qe, 1)
                for mm in range(2):
                    act.wait_ge(s_wo, n * 2 + (mm + 1))
                    act.activation(mixT[:, mm, bass.ds(n * NW, NW)], bank[6 + mm][:, 0:NW], ACT.Identity,
                                   bias=col(CBO, mm)).then_inc(s_mix, 1)
            act.wait_ge(s_base, 1)
            npass = act.value_load(celli[0:1, 0:1], min_val=1, max_val=N // WIN + 1)
            with act.Fori(0, npass) as p:
                with act.Fori(0, NWIN // 2) as i:
                    for w in range(2):
                        v = p * NWIN + i * 2 + w
                        act.wait_ge(s_scat, p * NCH + i * 4 + (2 * w + 2 + DEPTH))
                        act.wait_ge(s_wt, v + 1)
                        act.copy(wsum[w], bank[w]).then_inc(s_wcp, 1)
            act.wait_ge(s_scat, npass * NCH + DEPTH)
            with act.Fori(0, NC) as n:
                act.wait_ge(s_cp, n * 2 + 2)
                for u in range(4):
                    act.wait_ge(s_de, n * 4 + (u + 1))
                    act.activation(L[:, u, :], bank[u][:, 0:NW], ACT.Identity,
                                   bias=fbias[:, u:u + 1]).then_inc(s_da, 1)
                for mm in range(2):
                    act.wait_ge(s_cp, n * 2 + (mm + 3))
                    act.activation(HT[:, mm, bass.ds(n * NW, NW)], bank[4 + mm][:, 0:NW], ACT.Identity,
                                   bias=col(CCAT, mm)).then_inc(s_ct, 1)
            act.wait_ge(s_gv, 1)
            for mm in range(2):
                act.activation(hT[:, mm, 0:N], HT[:, mm, :], ACT.Square, bias=col(CMU, mm),
                               accum_out=col(CVAR, mm)).then_inc(s_gs, 1)
            act.wait_ge(s_gs, 2)
            act.activation(cols[:, 2 * CVAR:2 * CVAR + 2], cols[:, 2 * CVAR:2 * CVAR + 2], ACT.Sqrt,
                           bias=epsc[:, :], scale=1.0 / N).then_inc(s_gq, 1)
            deviation(2)
            turned(2 * NC)

            def exponents(r):
                act.wait_ge(s_z, r + 1)
                act.activation(ez, z, ACT.Exp).then_inc(s_ez, 1)

            for e in range(NEXP):
                with act.Fori(0, NC) as n:
                    r = n + e * NC
                    for h in range(2):
                        act.wait_ge(s_y, r * 2 + (h + 1))
                        for mm in range(HM):
                            act.wait_ge(s_h1, r * 8 + (h * 4 + mm + 1))
                            act.activation(hid[h][:, mm, :], bank[mm][:, 0:HALF],
                                           ACT.Gelu, bias=b1c[:, e * HM + mm:e * HM + mm + 1]).then_inc(s_h2, 1)
                        if h == 0:
                            exponents(r)
            act.wait_ge(s_tb, 2)
            rem = act.value_load(celli[0:1, 2:3], min_val=1, max_val=(EC - G * ROUNDS) // G + 1)
            with act.Fori(0, rem) as r:
                exponents(r + ROUNDS)
            act.wait_ge(s_a1, 1)
            act.activation(es[0:NB], es[0:NB], ACT.Exp).then_inc(s_ez, 1)
            act.activation(el[0:NB], el[0:NB], ACT.Exp).then_inc(s_ez, 1)
            act.wait_ge(s_a1, 2)
            act.activation(sd[0:NB, :], sc[0:NB, :, 0], ACT.Sqrt, bias=epsc[0:NB, :]).then_inc(s_ez, 1)
            act.wait_ge(s_a1, 3)
            act.activation(gg[0:NB], gg[0:NB], ACT.Exp).then_inc(s_ez, 1)

        @block.vector
        def _(dve):
            st = Steps(dve, s_vec)
            TT, TS1, STT = dve.tensor_tensor, dve.tensor_scalar, dve.scalar_tensor_tensor
            st.did(dve.memset(epsc[:, :], EPS))
            st.did(dve.memset(hmask[:, :], 0.0))
            st.did(dve.memset(vrow[:, :, :, P:P + 1], 1.0))
            st.settle()
            for g in range(4):
                st.did(dve.memset(hmask[32 * g:32 * g + 32, 32 * g:32 * g + 32], 1.0))

            st.did(dve.memset(wf, 0.0))
            st.settle()
            dve.memset(cut(high, FEAT, 2 * CH), 0.0).then_inc(s_fz, 1)

            dve.wait_ge(s_dl, 16)
            st.then(dve.tensor_copy(drel[:, :, :], drel[:, :, :].bitcast(I32)))
            st.did(dve.tensor_reduce(small[:, 0:NWIN], drel_w, AX, ALU.min))
            dve.tensor_reduce(small[:, NWIN:2 * NWIN], drel_w, AX, ALU.max)
            st.settle()
            dve.tensor_scalar(small[:, 0:NWIN], small[:, 0:NWIN], -1.0, None, ALU.mult).then_inc(s_dm, 1)

            def normalise(rows, out_rows, k):
                for t in range(T):
                    if k == 0:
                        dve.wait_ge(s_x, 16 * (t // BW + 1)) if t % BW == 0 and False else None
                    st.did(dve.bn_stats(stats[0:NB, t, :], rows[0:NB, t, :]))
                st.settle()
                for t in range(T):
                    ins = dve.bn_aggr(mv[0:NB, t, :], stats[0:NB, t, :])
                ins.then_inc(s_st, 1)
                dve.wait_ge(s_sd, k + 1)
                st.then(dve.reciprocal(rs[0:NB, :], sd[0:NB, :]))
                for t in range(T):
                    TS1(out_rows[0:NB, t, :], rows[0:NB, t, :], mv[0:NB, t, 0:1], rs[0:NB, t:t + 1],
                        ALU.subtract, ALU.mult).then_inc(s_xn, 1)

            dve.wait_ge(s_x, 16 * NC)
            normalise(x_rows, rows_n, 0)
            dve.wait_ge(s_fold, 3)
            TT(fbias[:, :], bank[5][:, 0:4], cols[:, 2 * CLB1:2 * CLB1 + 4], ALU.add).then_inc(s_foldc, 1)

            dve.wait_ge(s_ar, 1)
            st.did(TT(drel_w, drel_w, over(ared[:, 0:NWIN], P, NWIN, 2 * CT), ALU.add))
            st.then(TT(small[:, 0:NWIN], ared[:, NWIN:2 * NWIN], ared[:, 0:NWIN], ALU.add))
            st.then(dve.tensor_reduce(cellf[:, 0:1], small[:, 0:NWIN], AX, ALU.max))
            st.then(dve.tensor_copy(celli[:, 0:1], cellf[:, 0:1]))
            st.then(TS1(celli[:, 1:2], celli[:, 0:1], WIN.bit_length() - 1, None, ALU.arith_shift_right))
            st.did(TS1(celli[:, 0:1], celli[:, 1:2], 1.0, None, ALU.add))
            st.did(TS1(basef[:, :], ared[0:1, 0:NWIN], -1.0, None, ALU.mult))
            st.settle()
            dve.tensor_copy(basei[:, :], basef[:, :]).then_inc(s_base, 1)

            dve.wait_ge(s_w[1], 16 * 5)

            def key_map(t):
                dve.wait_ge(s_ke, t + 1)
                STT(kraw[0:NB, t % 2, :], kraw[0:NB, t % 2, :], 0.0, kexp[0:NB, t % 2, :],
                    ALU.max, ALU.add).then_inc(s_pk, 1)

            for t in range(T):
                dve.wait_ge(s_kv, t + 1)
                if t >= 2:
                    dve.wait_ge(s_kvs, t - 1)
                st.did(TT(kraw[0:NB, t % 2, :], bank[4 + t % 2][0:NB, 0:C], bkv_s[0:NB, 0:C], ALU.add))
                TT(vrow[0:NB, t % 2, :, 0:P], bank[4 + t % 2][0:NB, C:2 * C].rearrange("p (c n) -> p c n", c=2),
                   bkv_s[0:NB, C:2 * C].rearrange("p (c n) -> p c n", c=2), ALU.add).then_inc(s_kvu, 1)
                st.settle()
                TS1(kexp[0:NB, t % 2, :], kraw[0:NB, t % 2, :], 0.0, None, ALU.min).then_inc(s_km, 1)
                if t >= 1:
                    key_map(t - 1)
            key_map(T - 1)
            dve.wait_ge(s_kvs, T)
            st.settle()
            for c in range(2):
                st.did(TT(kvbd[:, c, 0, :], bank[6 + c][:, 0:P], hmask[:, :], ALU.mult))
                ins = TS1(kvbd[:, c, 1, :], hmask[:, :], bank[6 + c][:, P:P + 1], None, ALU.mult)
            ins.then_inc(s_bd, 1)
            dve.wait_ge(s_xnd, 16 * NC)
            v0 = st.k
            with dve.Fori(0, NC) as n:
                st.restart(n * 4 + v0)
                for c in range(2):
                    dve.wait_ge(s_qr, n * 2 + (c + 1))
                    TS1(qexp[:, c, :], qraw[:, c, :], 0.0, None, ALU.min).then_inc(s_qm, 1)
                for c in range(2):
                    dve.wait_ge(s_qe, n * 2 + (c + 1))
                    STT(qraw[:, c, :], qraw[:, c, :], 0.0, qexp[:, c, :], ALU.max, ALU.add).then_inc(s_pq, 1)
                for c in range(2):
                    dve.wait_ge(s_qn, n * 2 + (c + 3))
                    st.then(TS1(nrm[:, c, :], bank[3 + 2 * c][:, 0:NW], 1e-6, None, ALU.add))
                    st.then(dve.reciprocal(nrm[:, c, :], nrm[:, c, :]))
                    TT(att[:, c, :], bank[2 + 2 * c][:, 0:NW], nrm[:, c, :], ALU.mult).then_inc(s_at, 1)
            st.restart(v0 + 4 * NC)

            npass = dve.value_load(celli[0:1, 0:1], min_val=1, max_val=N // WIN + 1)
            dve.wait_ge(s_mix, 2 * NC)
            st.then(dve.memset(low[:, 0:4 * HTW], 0.0))
            dve.wait_ge(s_cst, 2)
            v0 = st.base + st.k
            halves = (slice(0, 4), slice(4, CT))
            banks = (psum[:, 2:4, :].rearrange("p b (t c) -> p (b t) c", c=C),
                     psum[:, 4:6, :].rearrange("p b (t c) -> p (b t) c", c=C)[:, 0:CT - 4, :])

            def chunk(p, c, use, j):
                d, q = j % DEPTH, p * NCH + c
                dve.wait_ge(s_scat, q + 2)
                TT(sel[j % 2], over(drel[:, bass.ds(c, 1), :].rearrange("p o t -> p (o t)"), P, CT, WIN),
                   iota[:, 0:WIN].unsqueeze(1).broadcast_to((P, CT, WIN)), ALU.is_equal)
                dve.wait_ge(s_gate[d], use * 16)
                dve.wait_ge(s_gath[d], use * (16 * CT))
                for h, ts in enumerate(halves):
                    dve.wait_ge(s_lin, q * 2 + (h + 5))
                    TT(gath[d][:, ts, :], banks[h], gath[d][:, ts, :], ALU.mult).then_inc(s_linf, 1)
                for h, ts in enumerate(halves):
                    dve.wait_ge(s_linf, q * 2 + (h + 3))
                    TT(gath[d][:, ts, :], gath[d][:, ts, :], gate[d][:, ts, :], ALU.mult).then_inc(s_m1, 1)
                for h, ts in enumerate(halves):
                    dve.wait_ge(s_m1, q * 2 + (h + 1))
                    TT(gate[d][:, ts, :], gath[d][:, ts, :], gate[d][:, ts, :], ALU.mult).then_inc(s_msg, 1)

            def add_window(p, c, w):
                v = p * NWIN + c
                dve.wait_ge(s_wt, v + 3)
                dve.wait_ge(s_acc, v + 2)
                dve.sem_inc(s_mark, 1)
                at = dve.value_load(basei[0:1, bass.ds(c, 1)], min_val=0, max_val=N)
                TT(hT[:, :, bass.ds(at, WIN)], hT[:, :, bass.ds(at, WIN)],
                   bank[6 + w % 2].rearrange("p (f w) -> p f w", f=4), ALU.add).then_inc(s_acc, 1)

            U3 = NCH // DEPTH
            with dve.Fori(0, npass) as p:
                for j in range(BODY):
                    chunk(p, j, p * U3 + (j // DEPTH + 1), j)
                    if j % 2 and j > 1:
                        add_window(p, j // 2 - 1, j // 2 - 1)
                with dve.Fori(1, NCH // BODY) as i:
                    for j in range(BODY):
                        chunk(p, i * BODY + j, p * U3 + i * (BODY // DEPTH) + (j // DEPTH + 1), j)
                        if j % 2:
                            add_window(p, i * (BODY // 2) + (j // 2 - 1), j // 2 - 1)
                add_window(p, NWIN - 1, NWIN - 1)
                st.restart(v0 + p * 2)
                st.did(TS1(drel[:, :, :], drel[:, :, :], float(-WIN), None, ALU.add))
                st.then(TS1(basef[:, :], basef[:, :], float(WIN), float(N), ALU.add, ALU.min))
                dve.tensor_copy(basei[:, :], basef[:, :]).then_inc(s_nb, 1)
                dve.wait_ge(s_nb, p + 1)
            v0 = npass * 2 + v0

            st.restart(v0)
            dve.wait_ge(s_el, 32)
            st.did(dve.memset(shared[:, :], 0.0))
            st.then(TS1(emask, edst, float(N), None, ALU.is_lt))
            A, B = cnt_a[:, 0:EC], cnt_b[:, 0:EC]
            st.then(STT(A, esrc, float(N - 1), emask, ALU.is_ge, ALU.mult))
            st.did(TT(emask, emask, A, ALU.subtract))
            st.then(STT(ekey, edst, 4096.0, esrc, ALU.mult, ALU.add))
            st.did(STT(ekey, ekey, 1.0, emask, ALU.add, ALU.mult))
            dve.tensor_reduce(small[:, 0:1], emask, AX, ALU.add).then_inc(s_dm, 1)
            st.then(STT(B, edst, 1.0, A, ALU.add, ALU.mult))
            st.then(TS1(cnt_a, cnt_b, -0.5, 1.0 / RB, ALU.add, ALU.mult))
            st.then(TS1(cnt_a, cnt_a, -0.5, MAGIC, ALU.add, ALU.add))
            st.then(TS1(cnt_a, cnt_a, -MAGIC, None, ALU.add))
            st.then(STT(cnt_b, cnt_a, -float(RB), cnt_b, ALU.mult, ALU.add))
            st.then(TS1(cnt_b, cnt_b, -1.0, None, ALU.add))
            dve.wait_ge(s_ar, 2)
            S0 = 8 * SORTS * NC
            st.did(TS1(cellf[:, 1:2], ared[:, 0:1], 1.0 / 8, -(S0 - 7.5) / 8 - 0.5, ALU.mult, ALU.add))
            st.then(TS1(cellf[:, 2:3], ared[:, 0:1], 1.0 / G, -(G * ROUNDS - G + 0.5) / G - 0.5, ALU.mult, ALU.add))
            st.then(TS1(cellf[:, 1:3], cellf[:, 1:3], MAGIC, None, ALU.add))
            st.then(TS1(cellf[:, 1:3], cellf[:, 1:3], -MAGIC, 1.0, ALU.add, ALU.max))
            st.then(dve.tensor_copy(celli[:, 1:3], cellf[:, 1:3]))
            dve.sem_inc(s_mark, 1)
            srem = dve.value_load(celli[0:1, 1:2], min_val=1, max_val=EC // 8 - SORTS * NC)
            v0 = v0 + st.k

            def sort_step(s):
                st.did(dve.max(srt[:, :], ekey))
                st.settle()
                dve.sem_inc(s_mark, 1)
                st.did(dve.match_replace(ekey, srt[:, :], ekey, 0.0))
                st.then(dve.tensor_copy(kbuf[:, bass.ds(s * 8, 8)], srt[:, :]))
                dve.sem_inc(s_mark, 1)

            with dve.Fori(0, NC) as n:
                st.restart(n * (3 * SORTS) + v0)
                for u in range(4):
                    dve.wait_ge(s_da, n * 4 + (u + 5))
                    STT(L[:, u, :], L[:, u, :], 0.1, L[:, u, :], ALU.mult, ALU.max).then_inc(s_dL, 1)
                for s in range(SORTS):
                    sort_step(n * SORTS + s)
            v0 = v0 + 3 * SORTS * NC
            with dve.Fori(0, srem) as s:
                st.restart(s * 3 + v0)
                sort_step(s + SORTS * NC)
            st.restart(srem * 3 + v0)
            st.settle()
            dve.sem_inc(s_mark, 1)
            st = Steps(dve, s_vec2)
            dve.wait_ge(s_ct, 2 * NC + 2)
            st.then(dve.tensor_reduce(cols[:, 2 * CA:2 * CA + 2], HT, AX, ALU.add))
            STT(cols[:, 2 * CMU:2 * CMU + 2], cols[:, 2 * CA:2 * CA + 2], -1.0 / N, cols[:, 2 * CGM:2 * CGM + 2],
                ALU.mult, ALU.mult).then_inc(s_gv, 1)
            dve.wait_ge(s_gv, 1)
            dve.wait_ge(s_gq, 1)
            st.then(dve.reciprocal(cols[:, 2 * CA:2 * CA + 2], cols[:, 2 * CVAR:2 * CVAR + 2]))
            st.then(TT(cols[:, 2 * CA:2 * CA + 2], cols[:, 2 * CA:2 * CA + 2], cols[:, 2 * CGW:2 * CGW + 2], ALU.mult))
            st.then(TT(cols[:, 2 * CBB:2 * CBB + 2], cols[:, 2 * CA:2 * CA + 2], cols[:, 2 * CMU:2 * CMU + 2], ALU.mult))
            st.then(TT(cols[:, 2 * CBB:2 * CBB + 2], cols[:, 2 * CBB:2 * CBB + 2], cols[:, 2 * CGB:2 * CGB + 2], ALU.add))
            for mm in range(2):
                st.did(TS1(HT[:, mm, :], HT[:, mm, :], col(CA, mm), col(CBB, mm), ALU.mult, ALU.add))
            st.settle()
            dve.wait_ge(s_mix, 2 * NC)
            TT(mixT, HT, mixT, ALU.add).then_inc(s_yT, 1)
            for t in range(T):
                dve.wait_ge(s_yb, t + 1)
                TT(x_rows[0:NB, t, :], bank[t % 4][0:NB, 0:C], x_rows[0:NB, t, :], ALU.add).then_inc(s_x1, 1)
            dve.wait_ge(s_x1, T)
            dve.wait_ge(s_yT, 1)
            normalise(x_rows, rows2, 1)
            dve.wait_ge(s_gl, 16 * 7)
            for i in range(2):
                for k in range(2):
                    st.did(TT(V.rearrange("p a b -> p (a b)")[:, (2 * i + k) * HE:(2 * i + k + 1) * HE], wg[:, k, 0:HE],
                              attb[:, HE * i:HE * i + HE], ALU.mult))
            st.settle()
            for i in range(2):
                for k in range(2):
                    ins = dve.tensor_reduce(wg[:, k, HE + 4 * i:HE + 4 * i + 4],
                                            V.rearrange("p a b -> p (a b)")[:, (2 * i + k) * HE:(2 * i + k + 1) * HE]
                                            .rearrange("p (h e) -> p h e", h=HEADS), AX, ALU.add)
            ins.then_inc(s_wg, 1)
            dve.memset(zeros, 0.0).then_inc(s_zero, 1)
            dve.wait_ge(s_tt, 1)
            dve.tensor_copy(tab[0:NB], bank[4][0:NB, 0:24 * T].rearrange("p (t c) -> p t c", t=T)).then_inc(s_tb, 1)
            dve.wait_ge(s_tb, 1)
            dve.tensor_reduce(mx[0:NB, 0:4], tab[0:NB, :, HE:TS].rearrange("p t h -> p h t"), AX, ALU.max).then_inc(s_tm, 1)
            st.did(dve.tensor_copy(td[0:NB, :, 0:4], tab[0:NB, :, TS:24]))
            dve.wait_ge(s_ar, 3)
            st.then(TT(td[0:NB, :, 4:8], tab[0:NB, :, TS:24],
                       mall[0:NB, 0:4].unsqueeze(1).broadcast_to((NB, T, 4)), ALU.add))
            STT(td[0:NB, :, 4:8], td[0:NB, :, 4:8], 0.2, td[0:NB, :, 4:8], ALU.mult, ALU.max).then_inc(s_tb, 1)
            dve.wait_ge(s_tb, 2)
            rem = dve.value_load(celli[0:1, 2:3], min_val=1, max_val=(EC - G * ROUNDS) // G + 1)

            def indices(r):
                st.then(TS1(kI, kbuf[:, bass.ds(r * G, G)], -1.0, None, ALU.add))
                st.did(TS1(sI, kI, 4095, None, ALU.bitwise_and))
                st.then(TS1(dI, kI, 12, None, ALU.arith_shift_right))
                st.did(TS1(sI, sI, float(N - 1), None, ALU.min))
                st.did(TS1(hi_, dI, 0.5, 1.0 / NB, ALU.add, ALU.mult))
                st.then(TS1(dG, dI, 0.0, None, ALU.max))
                dve.sem_inc(s_ki, 1) if False else None
                st.then(TS1(hi_, hi_, -0.5, MAGIC, ALU.add, ALU.add))
                st.then(TS1(hi_, hi_, -MAGIC, None, ALU.add))
                STT(lo_, hi_, -float(NB), dI, ALU.mult, ALU.add).then_inc(s_ki, 1)

            def edge_round(r, v, more):
                st.restart(v)
                dve.wait_ge(s_gg, r * (32 * G) + 32 * G)
                st.then(TT(z, GA[:, :, HE:TS], GB[:, :, 0:4], ALU.add))
                st.then(STT(z, z, 0.2, z, ALU.mult, ALU.max))
                TT(z, z, GB[:, :, 4:8], ALU.subtract).then_inc(s_z, 1)
                dve.wait_ge(s_ki, r + 1)
                st.did(TT(OH, over(hi_, P, G, T), iota[:, 0:T].unsqueeze(1).broadcast_to((P, G, T)), ALU.is_equal))
                for h in range(2):
                    dve.wait_ge(s_sc, r * 2 + (h + 1))
                    st.did(TT(lo1[h][:, :, 0:NB], over(lo_[:, HG * h:HG * h + HG], P, HG, NB),
                              iota[:, 0:NB].unsqueeze(1).broadcast_to((P, HG, NB)), ALU.is_equal))
                dve.wait_ge(s_ez, r + 1)
                st.did(TT(V[:, :, 0:HE].rearrange("p t (h e) -> p t h e", h=HEADS),
                          GA[:, :, 0:HE].rearrange("p t (h e) -> p t h e", h=HEADS),
                          over(ez, P, G, HEADS, NEXP), ALU.mult))
                st.then(dve.tensor_copy(V[:, :, HE:TS], ez))
                k5 = st.k
                if more:
                    indices(r + 1)
                for h in range(2):
                    for t in range(HG):
                        pass
                    TT(outer[h], over(OH[:, HG * h:HG * h + HG, :], P, HG, T, TS),
                       V[:, HG * h:HG * h + HG, :].unsqueeze(2).broadcast_to((P, HG, T, TS)), ALU.mult).then_inc(s_out, 1)
                return st.k

            IK, RK = 8, 0
            dve.wait_ge(s_tp, 4 * NC)
            indices(0)
            v0 = st.k
            per = 2 + 1 + 2 + 2 + IK
            for e in range(NEXP):
                with dve.Fori(0, NC) as n:
                    r = n + e * NC
                    got = edge_round(r, n * per + (v0 + e * NC * per if isinstance(v0, int) else v0 + e * NC * per), True)
                    assert got == per, got
                    dve.wait_ge(s_cs, r + 1)
                    TT(oa, over(cnt_a[:, bass.ds(r * CNT, CNT)], P, CNT, RB),
                       iota[:, 0:RB].unsqueeze(1).broadcast_to((P, CNT, RB)), ALU.is_equal)
                    TT(ob, over(cnt_b[:, bass.ds(r * CNT, CNT)], P, CNT, RB),
                       iota[:, 0:RB].unsqueeze(1).broadcast_to((P, CNT, RB)), ALU.is_equal).then_inc(s_cnt, 1)
                    for h in range(2):
                        dve.wait_ge(s_y, r * 2 + (h + 3))
                        TT(Y[0:NB, bass.ds(n * BW + 2 * h, 2), e, :], bank[4 + h][0:NB, :].rearrange("p (b c) -> p b c", b=2),
                           b2b[0:NB, C * e:C * e + C].unsqueeze(1).broadcast_to((NB, 2, C)), ALU.add).then_inc(s_yt, 1)
            v0 = v0 + ROUNDS * per
            dve.wait_ge(s_cs, ROUNDS + 1)
            dve.wait_ge(s_y, 2 * ROUNDS + 2)
            dve.tensor_copy(cc[0:RB, 0:RB], bank[7][0:RB, 0:RB]).then_inc(s_cst2, 1)
            with dve.Fori(0, rem) as r:
                edge_round(r + ROUNDS, r * per + v0, True) if False else edge_round(r + ROUNDS, r * per + v0, True)
            v0 = rem * per + v0
            st.restart(v0)

            dve.wait_ge(s_last, 16)
            R = slice(0, NB)
            st.did(TT(es[R], tab[R, :, HE:TS], tab[R, :, TS:24], ALU.add))
            st.then(TT(el[R], tab[R, :, TS:24], last[R, HE:TS].unsqueeze(1).broadcast_to((NB, T, 4)), ALU.add))
            st.did(STT(es[R], es[R], 0.2, es[R], ALU.mult, ALU.max))
            st.then(STT(el[R], el[R], 0.2, el[R], ALU.mult, ALU.max))
            st.did(TT(es[R], es[R], td[R, :, 4:8], ALU.subtract))
            TT(el[R], el[R], td[R, :, 4:8], ALU.subtract).then_inc(s_a1, 1)
            dve.wait_ge(s_sc, rem * 2 + (2 * ROUNDS + 2))
            st.did(dve.tensor_copy(agg[R], bank[6][R, 0:T * TS].rearrange("p (t c) -> p t c", t=T)))
            dve.wait_ge(s_ez, rem + (ROUNDS + 2))
            dve.wait_ge(s_cl, 16)
            st.did(TT(el[R], el[R], over(cn[R], NB, T, 4), ALU.mult))
            h4 = lambda v: v.rearrange("p t (h e) -> p t h e", h=HEADS)
            st.then(TT(h4(f1[R]), h4(tab[R, :, 0:HE]), over(es[R], NB, T, HEADS, NEXP), ALU.mult))
            st.did(TT(es[R], es[R], el[R], ALU.add))
            st.then(TT(h4(f2[R]), last[R, 0:HE].unsqueeze(1).broadcast_to((NB, T, HE)).rearrange("p t (h e) -> p t h e", h=HEADS),
                       over(el[R], NB, T, HEADS, NEXP), ALU.mult))
            st.did(TT(agg[R, :, 0:HE], agg[R, :, 0:HE], f1[R], ALU.add))
            st.then(TT(agg[R, :, HE:TS], agg[R, :, HE:TS], es[R], ALU.add))
            st.did(TT(agg[R, :, 0:HE], agg[R, :, 0:HE], f2[R], ALU.add))
            st.then(TS1(es[R], agg[R, :, HE:TS], 1e-16, None, ALU.add))
            st.then(dve.reciprocal(es[R], es[R]))
            st.then(TT(h4(f1[R]), h4(agg[R, :, 0:HE]), over(es[R], NB, T, HEADS, NEXP), ALU.mult))

            def by_value(i):
                return bgb[R, HE * i:HE * i + HE].unsqueeze(1).broadcast_to((NB, T, HE))

            st.then(TT(f1[R], f1[R], by_value(0), ALU.add))
            st.then(dve.tensor_reduce(t1[R], f1[R], AX, ALU.add))
            st.then(TS1(t1[R], t1[R], -1.0 / HE, None, ALU.mult))
            st.then(TT(f1[R], f1[R], over(t1[R], NB, T, HE), ALU.add))
            st.then(TT(f2[R], f1[R], f1[R], ALU.mult))
            st.then(dve.tensor_reduce(t2[R], f2[R], AX, ALU.add))
            TS1(sc[R, :, 0], t2[R], 1.0 / HE, None, ALU.mult).then_inc(s_a1, 1)
            dve.wait_ge(s_ez, rem + (ROUNDS + 3))
            st.then(dve.reciprocal(t1[R], sd[R, :]))
            st.then(TT(f1[R], f1[R], over(t1[R], NB, T, HE), ALU.mult))
            st.then(TT(f1[R], f1[R], by_value(1), ALU.mult))
            st.then(TT(f1[R], f1[R], by_value(2), ALU.add))
            st.then(dve.tensor_reduce(sc[R], f1[R].rearrange("p t (h e) -> p t e h", h=HEADS), AX, ALU.add))
            st.did(TS1(sc[R], sc[R], 1.0 / HEADS, None, ALU.mult))
            st.then(dve.memset(rk[R], 0.0))
            for i in range(4):
                for j in range(i + 1, 4):
                    st.then(TT(t2[R], sc[R, :, i], sc[R, :, j], ALU.is_ge))
                    st.did(TT(rk[R, :, j], rk[R, :, j], t2[R], ALU.add))
                    st.did(TT(rk[R, :, i], rk[R, :, i], t2[R], ALU.subtract))
                    st.settle()
            for i in range(4):
                st.did(TS1(rk[R, :, i], rk[R, :, i], float(3 - i), None, ALU.add))
            st.then(dve.tensor_reduce(t1[R], sc[R], AX, ALU.max))
            TT(gg[R], sc[R], over(t1[R], NB, T, 4), ALU.subtract).then_inc(s_a1, 1)
            dve.wait_ge(s_ez, rem + (ROUNDS + 4))
            st.then(STT(gg[R], rk[R], 1.5, gg[R], ALU.is_lt, ALU.mult))
            st.then(dve.tensor_reduce(t1[R], gg[R], AX, ALU.add))
            st.then(dve.reciprocal(t1[R], t1[R]))
            st.then(TT(gg[R], gg[R], over(t1[R], NB, T, 4), ALU.mult))
            dve.wait_ge(s_yt, 2 * ROUNDS + 2)
            for g in range(NC):
                for e in range(NEXP):
                    for b in range(BW):
                        t = g * BW + b
                        ins = STT(x_rows[R, t, :], Y[R, t, e, :], gg[R, t, e:e + 1], x_rows[R, t, :], ALU.mult, ALU.add)
                        if e == NEXP - 1 and b == BW - 1:
                            ins.then_inc(s_fin, 1)
                        else:
                            st.did(ins)
                    if e < NEXP - 1:
                        st.settle()


def kernel(**a):
    import concourse.bacc as _bacc
    from concourse.bass_utils import run_bass_kernel_spmd as _run

    a = {k: np.asarray(v) for k, v in a.items()}
    EP = NCH * CH

    def pad(v, fill):
        return np.concatenate([v, np.full((EP - E1,) + v.shape[1:], fill, v.dtype)])

    arrays = {
        "x": a["x"],
        "src": pad(a["src"], 0).reshape(NCH, P, CT),
        "dst": pad(a["dst"], N - 1).reshape(NCH, P, CT),
        "ea54": pad(a["edge_attr_54"], 0).reshape(NCH, P, CT, 54).transpose(0, 3, 2, 1),
        "ea256": pad(a["edge_attr_256"], 0).reshape(NCH, P, CT * C),
        "edges": a["L0_ffn_edge_index"],
        "wf1aT": a["L0_gnn_w_f1a"].T,
        "wf1b": a["L0_gnn_w_f1b"],
        "wlrT": np.stack([a[f"L0_gnn_{k}"].T for k in ("c1_wl", "c1_wr", "c2_wl", "c2_wr")]),
        "lin": np.stack([a["L0_gnn_lin1_w"], a["L0_gnn_lin2_w"]]),
        "catw": a["L0_gnn_cat_w"],
        "vecs": np.concatenate([a[f"L0_{k}"].reshape(2, P) for k in (
            "gnn_c1_bl", "gnn_c2_bl", "gnn_lin1_b", "gnn_lin2_b", "gnn_cat_b", "gnn_gn_w", "gnn_gn_b",
            "gnn_gn_ms", "mix_bq", "mix_bo")]).T,
        "wkv": np.concatenate([a["L0_mix_wk"], a["L0_mix_wv"]], axis=1),
        "bkv": np.concatenate([a["L0_mix_bk"], a["L0_mix_bv"]]),
        "wq": a["L0_mix_wq"], "wo": a["L0_mix_wo"],
        "wgat": a["L0_ffn_W_gat"], "atts": a["L0_ffn_att_src"].reshape(HE), "attd": a["L0_ffn_att_dst"].reshape(HE),
        "bgat": a["L0_ffn_b_gat"], "lng": a["L0_ffn_ln_gamma"], "lnb": a["L0_ffn_ln_beta"],
        "w1": a["L0_ffn_W1"], "b1": a["L0_ffn_b1"].reshape(NEXP * HM, P).T, "w2": a["L0_ffn_W2"], "b2": a["L0_ffn_b2"],
    }
    arrays = {f"in_{k}": np.ascontiguousarray(v) for k, v in arrays.items()}
    nc = _bacc.Bacc("TRN2", target_bir_lowering=False, num_devices=1)
    aps = {k[3:]: nc.dram_tensor(k, v.shape, mybir.dt.from_np(v.dtype), kind="ExternalInput").ap()
           for k, v in arrays.items()}
    out = nc.dram_tensor("out_rows", (N, C), F32, kind="ExternalOutput").ap()
    build(nc, out=out, **aps)
    r = _run(nc, [arrays], core_ids=[0])
    return r.results[0]["out_rows"]
```

```python
from contextlib import ExitStack

import numpy as np
import concourse.bass as bass
from concourse import mybir

ALU = mybir.AluOpType
ACT = mybir.ActivationFunctionType
F32 = mybir.dt.float32
BF16 = mybir.dt.bfloat16
I32 = mybir.dt.int32
F22 = mybir.dt.float32r
AX = mybir.AxisListType.X
RMAX = bass.bass_isa.ReduceOp.max

P = 128
N = 2500
C = 256
NB = 125
T = N // NB
NW = 500
NC = N // NW
BW = NW // NB

E1 = 42500
CT = 7
CH = P * CT
NCH = 48
WIN = 128
NWIN = NCH // 2
DEPTH = 3
KV = 4
IDX = 6
AHEAD = 2
BODY = 12

E2 = 131072
EC = E2 // P
HEADS, NEXP = 4, 4
HE = HEADS * NEXP
TS = HE + HEADS
TD = 2 * HEADS
G = 8
ROUNDS = NC * (NEXP - 1)
DW = 500
DH = N // DW
QT = 18
SAFE = 16.0
SORTS = 4
KCAP = EC + 4 * G
RB = 50
CCOLS = 4 * QT * ROUNDS
HID = 512
HM = HID // P
HALF = NW // 2
MAGIC = 12582912.0
EPS = 1e-5


class Steps:

    def __init__(self, eng, sem):
        self.eng, self.sem, self.base, self.k = eng, sem, 0, 0

    def did(self, ins):
        ins.then_inc(self.sem, 1)
        self.k += 1

    def settle(self):
        self.eng.wait_ge(self.sem, self.base + self.k)

    def then(self, ins):
        self.did(ins)
        self.settle()

    def restart(self, base):
        self.base, self.k = base, 0


def build(nc, x, src, dst, ea54, ea256, edges, wf1aT, wf1b, wlrT, lin, catw, vecs,
          wkv, bkv, wq, wo, wgat, atts, attd, bgat, lng, lnb,
          w1, b1, w2, b2, out):
    with ExitStack() as ctx:
        def sb(name, shape, dt=F32):
            return ctx.enter_context(nc.sbuf_tensor(name, shape, dt))

        def sem(name):
            return ctx.enter_context(nc.semaphore(name))

        psum = ctx.enter_context(nc.psum_tensor("psum", [P, 8, 512], F32))
        bank = [psum[:, i, :] for i in range(8)]

        xn_d = nc.dram_tensor("xn_rows", [N, C], F32).ap()
        tsrc_d = nc.dram_tensor("source_rows", [N, TS], F32).ap()
        tdst_d = nc.dram_tensor("dest_rows", [N, TD], F32).ap()
        agg_d = nc.dram_tensor("counts", [RB, RB], F32).ap()
        smax_d = nc.dram_tensor("segment_maxima", [N, HEADS], F32).ap()

        x_rows = sb("x_rows", [P, T, C])
        xT = sb("xT", [P, 2, N])
        ident = sb("ident", [P, P])
        iota = sb("iota", [P, DW])
        hmask = sb("hmask", [P, P])
        stats = sb("stats", [P, T, 6])
        mv = sb("mv", [P, T, 2])
        sd = sb("sd", [P, T])
        rs = sb("rs", [P, T])
        epsc = sb("epsc", [P, 1])
        tinyc = sb("tinyc", [P, 1])
        onec = sb("onec", [P, 1])
        gstat = sb("gstat", [P, 2, NC, 6])
        gmv = sb("gmv", [P, 2, 2])
        NCOL = 14
        cols = sb("cols", [P, 2 * NCOL])
        b1c = sb("b1c", [P, NEXP * HM])
        fbias = sb("fbias", [P, 4])
        srt = sb("srt", [P, 8])
        small = sb("small", [P, 2 * NWIN])
        ared = sb("ared", [P, 2 * NWIN])
        cellf = sb("cellf", [P, 8])
        celli = sb("celli", [P, 8], I32)
        basei = sb("basei", [1, NWIN], I32)
        basef = sb("basef", [1, NWIN])
        nrel = sb("nrel", [P, NCH, CT])
        nrel_w = nrel[:, :, :].rearrange("p (w s) t -> p w (s t)", s=2)
        srci = sb("srci", [P, IDX, CT], I32)
        shared = sb("shared", [P, KCAP + 2 * CCOLS])
        wlr = shared[:, 0:2048].rearrange("p (w k n) -> p w k n", w=4, k=2)
        linw = shared[:, 2048:3072].rearrange("p (b k n) -> p b k n", b=2, k=2)
        kbuf = shared[:, 0:KCAP]
        cnt_a = shared[:, KCAP:KCAP + CCOLS]
        cnt_b = shared[:, KCAP + CCOLS:KCAP + 2 * CCOLS]
        wsum = [shared[:, 4 * P * i:4 * P * i + 4 * P] for i in range(2)]
        fraw = shared[:, 8 * P:8 * P + 2 * CH]
        feat = [fraw[:, CH * i:CH * i + CH].rearrange("p (t e) -> p t e", t=CT) for i in range(2)]
        parts = sb("parts", [P, 2 * CH], F22)
        upper, lower = (parts[:, CH * i:CH * i + CH].rearrange("p (t e) -> p t e", t=CT) for i in range(2))
        wf = sb("filter_parts", [P, C], F22)
        TU = 2 * DH * TS + DW
        values = [parts[:, TU * i:TU * i + 2 * DH * TS].rearrange("p (k d v) -> p k d v", k=2, d=DH) for i in range(2)]
        digit = [parts[:, TU * i + 2 * DH * TS:TU * i + TU] for i in range(2)]

        LOW = 20608
        low = sb("low", [P, LOW])
        HIGH = 13440
        high = sb("high", [P, HIGH])

        def cut(buf, off, *shape, dt=None):
            n = int(np.prod(shape))
            v = buf[:, off:off + n]
            if dt is not None:
                v = v.bitcast(dt)
                if dt == BF16:
                    shape = shape[:-1] + (shape[-1] * 2,)
            if len(shape) == 1:
                return v
            names = "abcd"[:len(shape)]
            return v.rearrange(f"p ({' '.join(names)}) -> p {' '.join(names)}",
                               **{c: s for c, s in zip(names[1:], shape[1:])})

        HTW = N + WIN
        hT = cut(low, 0, 4, HTW)
        o = 4 * HTW
        mixT = cut(low, o, 2, N); o += 2 * N
        fw = cut(low, o, 4, 2, C); o += 4 * 2 * C
        cat = cut(low, o, 4, C); o += 4 * C
        wo_s = cut(low, o, 2, C); o += 2 * C
        wq_s = cut(low, o, 2, C); o += 2 * C
        assert o <= LOW
        rows_n = cut(low, 0, T, C)
        m = T * C
        wkv_s = cut(low, m, 2, 512); m += 1024
        bkv_s = cut(low, m, 512); m += 512
        kraw = cut(low, m, KV, C); m += KV * C
        kexp = cut(low, m, KV, C); m += KV * C
        vrow = cut(low, m, KV, 2, P + 1); m += KV * 2 * (P + 1)
        KVB = m
        kvbd = cut(low, m, 2, 2, P); m += 512
        assert m <= 4 * HTW
        m = 0
        qraw = cut(low, m, 2, NW); m += 2 * NW
        qrel = cut(low, m, 2, NW); m += 2 * NW
        qexp = cut(low, m, 2, NW); m += 2 * NW
        nrm = cut(low, m, 2, NW); m += 2 * NW
        att = cut(low, m, 2, NW); m += 2 * NW
        QB = m
        assert m <= T * C
        Y = cut(low, 0, T, NEXP, C)
        smt = cut(low, 0, N, HEADS)
        smf = cut(low, 0, N * HEADS)
        smr = cut(low, N * HEADS, N * HEADS)
        smo = cut(low, N * HEADS, N)
        niota = cut(low, N * HEADS + N, N)
        o = 0
        msgs = [cut(high, o + i * CT * 2 * C, CT, 2 * C) for i in range(DEPTH)]; o += DEPTH * CT * 2 * C
        gath = [m[:, :, 0:C] for m in msgs]
        gate = [m[:, :, C:2 * C] for m in msgs]
        sel = [cut(high, o + i * CT * WIN, CT, WIN) for i in range(2)]; o += 2 * CT * WIN
        wraw, wupper = cut(high, 1024, C), cut(high, 2048, C).bitcast(F22)
        assert o <= HIGH, o
        W1s = [cut(high, i * 2048, 2, HID) for i in range(2)]
        W2s = [cut(high, i * 2048 + 1024, HM, C) for i in range(2)]
        o = 4096
        HT = cut(high, o, 2, N)
        rows2 = cut(high, o, T, C); o += T * C
        L = cut(high, o, 4, NW); o += 4 * NW
        SORTED = HIGH - EC
        assert o <= SORTED
        esrc = cut(high, SORTED, EC, dt=I32); ekey = cut(high, SORTED, EC)
        edst = cut(high, 2048, EC, dt=I32)
        emask = cut(high, 2048 + EC, EC)
        assert o <= HIGH, o
        o = 4096 + T * C
        tab = cut(high, o, T, 24); o += T * 24
        td = cut(high, o, T, TD); o += T * TD
        b2b = cut(high, o, NEXP * C); o += NEXP * C
        kI = cut(high, o, G, dt=I32); o += G
        dI = cut(high, o, G, dt=I32); o += G
        index = cut(high, o, 2, G, dt=I32); o += 2 * G
        nindex = cut(high, o, 2, G, dt=I32); o += 2 * G
        digits = cut(high, o, 2, G); o += 2 * G
        ndigits = cut(high, o, 2, G); o += 2 * G
        lcur = cut(high, o, G); o += G
        WA = cut(high, o, G, TS); o += G * TS
        WB = cut(high, o, G, TD); o += G * TD
        GA = cut(high, o, G, TS); o += G * TS
        GB = cut(high, o, G, TD); o += G * TD
        z = cut(high, o, G, HEADS); o += G * HEADS
        ez = cut(high, o, G, HEADS); o += G * HEADS
        V = cut(high, o, G, TS); o += G * TS
        VP = cut(high, o, G, 2, TS); o += G * 2 * TS
        OH = cut(high, o, G, DH); o += G * DH
        es = cut(high, o, T, HEADS); o += T * HEADS
        el = cut(high, o, T, HEADS); o += T * HEADS
        last = cut(high, o, 24); o += 24
        bgb = cut(high, o, 3 * HE); o += 3 * HE
        wg = cut(high, o, 2, 24); o += 48
        attb = cut(high, o, 2 * HE); o += 2 * HE
        mx = cut(high, o, 16); o += 16
        mall = cut(high, o, 16); o += 16
        GATS = o
        assert GATS <= SORTED
        o = 4096
        ssrc = cut(high, o, EC, dt=I32); o += EC
        sdst = cut(high, o, EC, dt=I32); o += EC
        sidx = cut(high, o, 1, dt=I32); o += 1
        sdf = cut(high, o, 1); o += 1
        srow = cut(high, o, TS); o += TS
        srel = cut(high, o, HEADS); o += HEADS
        smx = cut(high, o, T, HEADS); o += T * HEADS
        o = 4096
        hid = [cut(high, o + i * HM * HALF, HM, HALF) for i in range(2)]; o += 2 * HM * HALF
        oa = [cut(high, o + i * QT * RB // 2, QT, RB // 2, dt=BF16) for i in range(2)]; o += QT * RB
        ob = [cut(high, o + i * QT * RB // 2, QT, RB // 2, dt=BF16) for i in range(2)]; o += QT * RB
        assert o <= 4096 + T * C, o
        o = GATS
        zeros = cut(high, o, DW); o += DW
        assert o <= HIGH, o
        o = 0
        agg = cut(high, o, T, TS); o += T * TS
        f1 = cut(high, o, T, HE); o += T * HE
        f2 = cut(high, o, T, HE); o += T * HE
        vsum = cut(high, o, DW); o += DW
        cn = cut(high, o, T); o += T
        sc = cut(high, o, T, 4); o += T * 4
        rk = cut(high, o, T, 4); o += T * 4
        gg = cut(high, o, T, 4); o += T * 4
        cc = cut(high, o, 64); o += 64
        t1 = cut(high, o, T); o += T
        t2 = cut(high, o, T); o += T
        assert o <= 2048

        def col(i, mm):
            return cols[:, 2 * i + mm:2 * i + mm + 1]

        (CBL1, CBL2, CLB1, CLB2, CCAT, CGW, CGB, CGM, CBQ, CBO, CMU, CA, CBB, CVAR) = range(NCOL)

        s_x = [sem(f"x_loaded{g}") for g in range(NC)]
        s_w = [sem(f"weights_loaded{i}") for i in range(3)]
        s_cst = sem("constants_made")
        s_pool = sem("pool_steps")
        s_vec = sem("vector_steps")
        s_vec2 = sem("vector_steps_second_half")
        s_mark = sem("waits_passed")
        s_act = sem("scalar_steps")
        s_fold = sem("folds_multiplied")
        s_foldc = sem("folds_copied")
        s_st = sem("stats_ready")
        s_sd = sem("deviation_ready")
        s_xn = sem("rows_normalised")
        s_xnd = sem("rows_stored")
        s_tp = sem("rows_transposed")
        s_tc = sem("transposes_copied")
        s_kv = sem("kv_multiplied")
        s_kvu = sem("kv_taken")
        s_km = sem("k_biased")
        s_ke = sem("k_exponent")
        s_pk = sem("k_feature_ready")
        s_kvs = sem("kv_summed")
        s_bd = sem("kv_masked")
        s_q = sem("q_multiplied")
        s_qe = sem("q_exponent")
        s_pq = sem("q_feature_ready")
        s_qn = sem("attention_multiplied")
        s_nr = sem("normaliser_taken")
        s_at = sem("attention_normalised")
        s_wo = sem("mix_multiplied")
        s_mix = sem("mix_taken")
        s_dl = sem("destinations_loaded")
        s_dm = sem("windows_measured")
        s_ar = sem("reduced_over_partitions")
        s_base = sem("window_bases_ready")
        s_gate = [sem(f"gate_loaded{i}") for i in range(DEPTH)]
        s_idx = [sem(f"indices_loaded{i}") for i in range(IDX)]
        s_feat = [sem(f"features_loaded{i}") for i in range(2)]
        s_gath = [sem(f"sources_gathered{i}") for i in range(DEPTH)]
        s_upper = sem("upper_parts_ready")
        s_split = sem("features_split")
        s_sel = sem("windows_selected")
        s_lin = sem("filters_multiplied")
        s_linf = sem("filters_taken")
        s_m1 = sem("first_messages_ready")
        s_msg = sem("messages_ready")
        s_nb = sem("windows_moved")
        s_scat = sem("messages_summed")
        s_wcp = sem("window_copied")
        s_wt = sem("window_transposed")
        s_acc = sem("window_added")
        s_fz = sem("padding_cleared")
        s_el = sem("second_edges_loaded")
        s_de = sem("dense_multiplied")
        s_da = sem("dense_biased")
        s_dL = sem("dense_leaky")
        s_cp = sem("cat_multiplied")
        s_ct = sem("cat_taken")
        s_gs = sem("graphnorm_squares")
        s_gv = sem("graphnorm_steps")
        s_gq = sem("graphnorm_root")
        s_gn = sem("graphnorm_applied")
        s_gc = sem("graphnorm_coefficients")
        s_yT = sem("sum_by_feature_ready")
        s_yb = sem("sum_transposed")
        s_x1 = sem("sum_rows_ready")
        s_w1 = [sem(f"expert_weights_loaded{i}") for i in range(2)]
        s_gl = sem("gat_vectors_loaded")
        s_wg = sem("gat_weights_ready")
        s_tt = sem("tables_multiplied")
        s_tm = sem("logits_reduced")
        s_tb = sem("tables_ready")
        s_ts = sem("tables_stored")
        s_wide = sem("span_compared")
        s_se = sem("slow_edges_loaded")
        s_sv = sem("slow_vector_steps")
        s_si = sem("slow_sources_ready")
        s_sg = sem("slow_sources_gathered")
        s_sm = sem("slow_maxima_by_partition")
        s_sr = sem("slow_maxima_reduced")
        s_sd2 = sem("slow_maxima_stored")
        s_sl = sem("slow_maxima_loaded")
        s_last = sem("last_source_loaded")
        s_ki = sem("round_indices_ready")
        s_gg = sem("round_gathered")
        s_z = sem("logits_ready")
        s_ez = sem("exponents_ready")
        s_out = sem("outer_ready")
        s_sc = sem("outer_summed")
        s_cnt = sem("counts_ready")
        s_cs = sem("counts_summed")
        s_zero = sem("sums_cleared")
        s_h1 = sem("hidden_multiplied")
        s_h2 = sem("hidden_ready")
        s_y = sem("expert_multiplied")
        s_yt = sem("expert_taken")
        s_yc = sem("last_expert_taken")
        s_yl = sem("last_expert_biased")
        s_vc = sem("value_sums_copied")
        s_vt = sem("value_sums_transposed")
        s_cst2 = sem("counts_copied")
        s_cd = sem("counts_stored")
        s_cl = sem("counts_loaded")
        s_a1 = sem("last_arguments")
        s_ow = sem("last_functions")
        s_fin = sem("rows_finished")
        s_o = sem("output_stored")

        x_v = x.rearrange("(t p) c -> p t c", p=NB)
        out_v = out.rearrange("(t p) c -> p t c", p=NB)
        xn_v = xn_d.rearrange("(t p) c -> p t c", p=NB)

        block = ctx.enter_context(nc.Block())

        def over(v, *shape):
            return v.unsqueeze(len(shape) - 1).broadcast_to(shape)

        @block.sync
        def _(sp):
            for g in range(NC):
                sp.dma_start(x_rows[0:NB, BW * g:BW * g + BW, :], x_v[:, BW * g:BW * g + BW, :]).then_inc(s_x[g], 16)
            sp.dma_start(nrel[:, :, :].bitcast(I32), dst.rearrange("c p t -> p c t")).then_inc(s_dl, 16)
            sp.dma_start(wlr, wlrT.rearrange("w (k p) n -> p w k n", p=P)).then_inc(s_w[0], 16)
            sp.dma_start(linw, lin.rearrange("b (k p) n -> p b k n", p=P)).then_inc(s_w[0], 16)
            sp.dma_start(high[0:64, 0:54], wf1aT).then_inc(s_w[0], 16)
            sp.dma_start(high[0:64, 64:64 + C], wf1b).then_inc(s_w[0], 16)
            sp.dma_start(cols[:, 0:2 * CMU], vecs).then_inc(s_w[0], 16)
            sp.dma_start(b1c[:, :], b1).then_inc(s_w[0], 16)
            sp.dma_start(wkv_s, wkv.rearrange("(k p) n -> p k n", p=P)).then_inc(s_w[1], 16)
            sp.dma_start(bkv_s, bkv.partition_broadcast(P)).then_inc(s_w[1], 16)
            sp.dma_start(wq_s, wq.rearrange("(k p) n -> p k n", p=P)).then_inc(s_w[1], 16)
            sp.dma_start(wo_s, wo.rearrange("(k p) n -> p k n", p=P)).then_inc(s_w[1], 16)
            sp.dma_start(cat, catw.rearrange("(k p) n -> p k n", p=P)).then_inc(s_w[1], 16)
            for g in range(NC):
                sp.wait_ge(s_xn, BW * (g + 1))
                sp.dma_start(xn_v[:, BW * g:BW * g + BW, :], rows_n[0:NB, BW * g:BW * g + BW, :]).then_inc(s_xnd, 16)
            sp.wait_ge(s_base, 1)
            npass = sp.value_load(celli[0:1, 0:1], min_val=1, max_val=N // WIN + 1)
            sp.wait_ge(s_fold, 3)
            sp.wait_ge(s_fz, 1)
            for j in range(AHEAD):
                sp.dma_start(srci[:, j, :], src[j]).then_inc(s_idx[j], 16)
            with sp.Fori(0, npass) as p:
                with sp.Fori(0, NCH // IDX) as i:
                    for j in range(IDX):
                        q = p * NCH + i * IDX + j
                        c = i * IDX + j
                        sp.wait_ge(s_split, q + 1)
                        for at in (0, 64):
                            sp.dma_start(feat[j % 2][at:at + 54],
                                         ea54[bass.ds(c, 1)].rearrange("o f t p -> (o f) t p")
                                         ).then_inc(s_feat[j % 2], 16)
                        sp.wait_ge(s_scat, q + 1)
                        a = (j + AHEAD) % IDX
                        sp.dma_start(srci[:, a, :], src[bass.ds(c + AHEAD, 1)].rearrange("o p t -> (o p) t")
                                     ).then_inc(s_idx[a], 16)
                        sp.dma_start(gate[j % DEPTH], ea256[bass.ds(c, 1)].rearrange("o p (t c) -> (o p) t c", t=CT)
                                     ).then_inc(s_gate[j % DEPTH], 16)
            sp.wait_ge(s_scat, npass * NCH + DEPTH)
            sp.dma_start(esrc, edges[0].rearrange("(p c) -> p c", p=P)).then_inc(s_el, 16)
            sp.dma_start(edst, edges[1].rearrange("(p c) -> p c", p=P)).then_inc(s_el, 16)
            for e in range(2):
                if e == 1:
                    sp.wait_ge(s_dm, 3)
                sp.dma_start(W1s[e], w1[e].rearrange("(k p) n -> p k n", p=P)).then_inc(s_w1[e], 16)
                sp.dma_start(W2s[e], w2[e].rearrange("(k p) n -> p k n", p=P)).then_inc(s_w1[e], 16)
            sp.wait_ge(s_yT, NC)
            sp.dma_start(wg[:, :, 0:HE], wgat.rearrange("(k p) n -> p k n", p=P)).then_inc(s_gl, 16)
            sp.dma_start(attb[:, 0:HE], atts.partition_broadcast(P)).then_inc(s_gl, 16)
            sp.dma_start(attb[:, HE:2 * HE], attd.partition_broadcast(P)).then_inc(s_gl, 16)
            for i, v in enumerate((bgat, lng, lnb)):
                sp.dma_start(bgb[:, HE * i:HE * i + HE], v.partition_broadcast(P)).then_inc(s_gl, 16)
            sp.dma_start(b2b, b2.rearrange("e c -> (e c)").partition_broadcast(P)).then_inc(s_gl, 16)
            sp.wait_ge(s_tb, 1)
            sp.dma_start(tsrc_d.rearrange("(t p) c -> p t c", p=NB), tab[0:NB, :, 0:TS]).then_inc(s_ts, 16)
            sp.wait_ge(s_wide, 1)
            wide = sp.value_load(celli[0:1, 3:4], min_val=0, max_val=1)
            with sp.If(wide):
                sp.dma_start(ssrc, edges[0].rearrange("(p c) -> p c", p=P)).then_inc(s_se, 16)
                sp.dma_start(sdst, edges[1].rearrange("(p c) -> p c", p=P)).then_inc(s_se, 16)
                sp.wait_ge(s_sr, 1)
                sp.dma_start(smax_d.rearrange("n h -> (n h)").unsqueeze(0), smr[0:1, :]).then_inc(s_sd2, 16)
                sp.wait_ge(s_sd2, 16)
                sp.dma_start(smx[0:NB], smax_d.rearrange("(t p) h -> p t h", p=NB)).then_inc(s_sl, 16)
            sp.wait_ge(s_tb, 2)
            sp.dma_start(tdst_d.rearrange("(t p) c -> p t c", p=NB), td[0:NB]).then_inc(s_ts, 16)
            sp.wait_ge(s_ts, 32)
            sp.dma_start(last[:, 0:TS], tsrc_d[N - 1, :].partition_broadcast(P)).then_inc(s_last, 16)
            for e in range(2, NEXP):
                sp.wait_ge(s_y, 2 + 2 * NC * (e - 1))
                sp.dma_start(W1s[e % 2], w1[e].rearrange("(k p) n -> p k n", p=P)).then_inc(s_w1[e % 2], 16)
                sp.dma_start(W2s[e % 2], w2[e].rearrange("(k p) n -> p k n", p=P)).then_inc(s_w1[e % 2], 16)
            sp.wait_ge(s_cst2, 1)
            sp.dma_start(agg_d, cc[0:RB, 0:RB]).then_inc(s_cd, 16)
            sp.wait_ge(s_cd, 16)
            sp.dma_start(cn[0:NB], agg_d.rearrange("a b -> (a b)").rearrange("(t p) -> p t", p=NB),
                         allow_slow_non_contiguous=True).then_inc(s_cl, 16)
            for g in range(NC):
                sp.wait_ge(s_fin, g + 1)
                sp.dma_start(out_v[:, BW * g:BW * g + BW, :], x_rows[0:NB, BW * g:BW * g + BW, :]).then_inc(s_o, 16)
            sp.wait_ge(s_o, 16 * NC)

        @block.gpsimd
        def _(pool):
            pool.memset(ident[:, :], 0.0).then_inc(s_pool, 1)
            pool.wait_ge(s_pool, 1)
            pool.affine_select(out=ident[:, :], in_=ident[:, :], compare_op=ALU.not_equal, fill=1.0, base=0,
                               pattern=[[-1, P]], channel_multiplier=1).then_inc(s_cst, 1)
            pool.iota(iota[:, :], pattern=[[1, DW]], base=0, channel_multiplier=0,
                      allow_small_or_imprecise_dtypes=True).then_inc(s_cst, 1)
            pool.wait_ge(s_dm, 1)
            pool.partition_all_reduce(ared[:, :], small[:, :], P, RMAX).then_inc(s_ar, 1)
            pool.wait_ge(s_xnd, 16 * NC)
            pool.wait_ge(s_base, 1)
            npass = pool.value_load(celli[0:1, 0:1], min_val=1, max_val=N // WIN + 1)
            with pool.Fori(0, npass) as p:
                with pool.Fori(0, NCH // IDX) as i:
                    for j in range(IDX):
                        pool.wait_ge(s_idx[j], (p * (NCH // IDX) + i) * 16 + 16)
                        pool.wait_ge(s_scat, p * NCH + i * IDX + (j + 1))
                        pool.sem_inc(s_mark, 1)
                        for t in range(CT):
                            pool.indirect_dma_start(
                                gath[j % DEPTH][:, t, :], None, xn_d,
                                bass.IndirectOffsetOnAxis(ap=srci[:, j, t:t + 1], axis=0)
                            ).then_inc(s_gath[j % DEPTH], 16)
            pool.wait_ge(s_dm, 2)
            pool.partition_all_reduce(ared[:, 0:1], small[:, 0:1], P, RMAX).then_inc(s_ar, 1)
            pool.wait_ge(s_tm, 1)
            pool.partition_all_reduce(mall[:, 0:8], mx[:, 0:8], P, RMAX).then_inc(s_ar, 1)
            pool.wait_ge(s_wide, 1)
            wide = pool.value_load(celli[0:1, 3:4], min_val=0, max_val=1)
            with pool.If(wide):
                pool.wait_ge(s_ts, 16)
                with pool.Fori(0, EC) as c:
                    pool.wait_ge(s_si, c + 1)
                    pool.sem_inc(s_mark, 1)
                    pool.indirect_dma_start(srow, None, tsrc_d,
                                            bass.IndirectOffsetOnAxis(ap=sidx, axis=0)).then_inc(s_sg, 16)
                pool.wait_ge(s_sm, 1)
                pool.partition_all_reduce(smr, smf, P, RMAX).then_inc(s_sr, 1)
            pool.wait_ge(s_ts, 32)
            rem = pool.value_load(celli[0:1, 2:3], min_val=1, max_val=(EC - G * ROUNDS) // G + 1)

            def gathers(r):
                pool.wait_ge(s_ki, r + 1)
                pool.sem_inc(s_mark, 1)
                for t in range(G):
                    pool.indirect_dma_start(GA[:, t, :], None, tsrc_d,
                                            bass.IndirectOffsetOnAxis(ap=index[:, 0, t:t + 1], axis=0)).then_inc(s_gg, 16)
                    pool.indirect_dma_start(GB[:, t, :], None, tdst_d,
                                            bass.IndirectOffsetOnAxis(ap=index[:, 1, t:t + 1], axis=0)).then_inc(s_gg, 16)

            with pool.Fori(0, ROUNDS) as r:
                gathers(r)
            with pool.Fori(0, rem) as r:
                gathers(r + ROUNDS)
            with pool.Fori(0, NC) as n:
                for h in range(2):
                    pool.wait_ge(s_yc, n * 2 + (h + 1))
                    v = Y[0:NB, bass.ds(n * BW + 2 * h, 2), NEXP - 1, :]
                    pool.tensor_tensor(v, v, b2b[0:NB, C * (NEXP - 1):].unsqueeze(1).broadcast_to((NB, 2, C)),
                                       ALU.add).then_inc(s_yl, 1)

        @block.tensor
        def _(pe):
            pe.wait_ge(s_w[0], 16 * 6)
            pe.matmul(bank[0][0:54, 0:C], high[0:64, 0:54], high[0:64, 64:64 + C],
                      start=True, stop=True).then_inc(s_fold, 1)
            for w in range(4):
                for mm in range(2):
                    for k in range(2):
                        ins = pe.matmul(bank[1 + w][:, C * mm:C * mm + C], wlr[:, w, k, P * mm:P * mm + P],
                                        linw[:, w // 2, k, :], start=(k == 0), stop=(k == 1))
            ins.then_inc(s_fold, 1)
            for b in range(2):
                for mm in range(2):
                    for k in range(2):
                        ins = pe.matmul(bank[5][:, 2 * b + mm:2 * b + mm + 1], linw[:, b, k, P * mm:P * mm + P],
                                        col(CBL1 + b, k), start=(k == 0), stop=(k == 1))
            ins.then_inc(s_fold, 1)
            pe.wait_ge(s_cst, 1)

            def turn_rows(rows, g, ready, used, banks):
                pe.wait_ge(s_xn, ready + BW * (g + 1))
                for k in range(2):
                    u = used + 2 * g + k
                    if 2 * g + k >= len(banks):
                        pe.wait_ge(s_tc, u - len(banks) + 1)
                    for b in range(BW):
                        ins = pe.transpose(banks[(2 * g + k) % len(banks)][:, NB * b:NB * b + NB],
                                           rows[0:NB, BW * g + b, P * k:P * k + P], ident[0:NB, 0:NB])
                    ins.then_inc(s_tp, 1)

            pe.wait_ge(s_foldc, 2)
            for g in range(NC):
                turn_rows(rows_n, g, 0, 0, bank[0:4])
            pe.wait_ge(s_w[1], 16 * 5)

            def kv_sum(t):
                pe.wait_ge(s_pk, t + 1)
                for c in range(2):
                    ins = pe.matmul(bank[6 + c][:, 0:P + 1], kexp[0:NB, t % KV, P * c:P * c + P],
                                    vrow[0:NB, t % KV, c, :], start=(t == 0), stop=(t == T - 1))
                ins.then_inc(s_kvs, 1)

            pe.wait_ge(s_foldc, 3)
            for t in range(T):
                pe.wait_ge(s_tc, 2 * NC if t >= 2 else 2)
                if t >= KV:
                    pe.wait_ge(s_kvu, t - KV + 1)
                for k in range(2):
                    ins = pe.matmul(bank[(4, 5, 2, 3)[t % KV]][0:NB, :], xT[:, k, NB * t:NB * t + NB], wkv_s[:, k, :],
                                    start=(k == 0), stop=(k == 1))
                ins.then_inc(s_kv, 1)
                if t >= 2:
                    kv_sum(t - 2)
            kv_sum(T - 2)
            kv_sum(T - 1)

            def queries(n):
                for c in range(2):
                    for k in range(2):
                        ins = pe.matmul(bank[c][:, 0:NW], wq_s[:, k, P * c:P * c + P], xT[:, k, bass.ds(n * NW, NW)],
                                        start=(k == 0), stop=(k == 1))
                    ins.then_inc(s_q, 1)

            def attend(n):
                for c in range(2):
                    pe.wait_ge(s_pq, n * 2 + (c + 1))
                    pe.wait_ge(s_at, n * 2 + (c + 1))
                    pe.matmul(bank[2 + 2 * c][:, 0:NW], kvbd[:, c, 0, :], qraw[:, c, :], start=True, stop=True)
                    pe.matmul(bank[3 + 2 * c][:, 0:NW], kvbd[:, c, 1, :], qraw[:, c, :],
                              start=True, stop=True).then_inc(s_qn, 1)

            def mix(n):
                pe.wait_ge(s_at, n * 2 + 4)
                pe.wait_ge(s_mix, n * 2 + 2)
                for mm in range(2):
                    for k in range(2):
                        ins = pe.matmul(bank[6 + mm][:, 0:NW], wo_s[:, k, P * mm:P * mm + P], att[:, k, :],
                                        start=(k == 0), stop=(k == 1))
                    ins.then_inc(s_wo, 1)

            queries(0)
            pe.wait_ge(s_bd, 1)
            with pe.Fori(0, NC - 1) as n:
                attend(n)
                queries(n + 1)
                mix(n)
            attend(NC - 1)
            mix(NC - 1)
            pe.wait_ge(s_mix, 2 * NC + 2)

            pe.wait_ge(s_base, 1)
            npass = pe.value_load(celli[0:1, 0:1], min_val=1, max_val=N // WIN + 1)

            def filters(q, j):
                pe.wait_ge(s_split, q + 3)
                for h, tiles in enumerate((range(0, 4), range(4, CT))):
                    pe.wait_ge(s_linf, q * 2 + (h + 1))
                    for t in tiles:
                        for k, part in enumerate((upper, lower)):
                            ins = pe.matmul(bank[2 + t // 2][:, C * (t % 2):C * (t % 2) + C],
                                            part[:, t, :], wf[:, :],
                                            start=(k == 0), stop=(k == 1))
                    ins.then_inc(s_lin, 1)

            def sums(q, j):
                w = j // 2
                if j % 2 == 0:
                    pe.wait_ge(s_wcp, (q >> 1) + 1)
                pe.wait_ge(s_sel, q + 1)
                for h, tiles in enumerate((range(0, 4), range(4, CT))):
                    pe.wait_ge(s_msg, q * 2 + (h + 1))
                    for t in tiles:
                        ins = pe.matmul(bank[w % 2], sel[j % 2][:, t, :], msgs[j % DEPTH][:, t, :],
                                        start=(j % 2 == 0 and t == 0), stop=(j % 2 == 1 and t == CT - 1),
                                        skip_group_check=True)
                ins.then_inc(s_scat, 1)

            def turn_window(v, w):
                pe.wait_ge(s_wcp, v + 3)
                pe.wait_ge(s_acc, v + 1)
                for f in range(4):
                    ins = pe.transpose(bank[6 + w % 2][:, P * f:P * f + P], wsum[w % 2][:, P * f:P * f + P],
                                       ident[:, :])
                ins.then_inc(s_wt, 1)

            with pe.Fori(0, npass) as p:
                for j in range(2):
                    filters(p * NCH + j, j)
                with pe.Fori(0, NCH // BODY - 1) as i:
                    for j in range(BODY):
                        sums(p * NCH + i * BODY + j, j)
                        filters(p * NCH + i * BODY + (j + 2), j)
                        if j % 2:
                            turn_window(p * NWIN + i * (BODY // 2) + j // 2, j // 2)
                for j in range(BODY):
                    c = NCH - BODY + j
                    sums(p * NCH + c, j)
                    if c + 2 < NCH:
                        filters(p * NCH + (c + 2), j)
                    if j % 2:
                        turn_window(p * NWIN + c // 2, j // 2)

            pe.wait_ge(s_acc, npass * NWIN + 2)
            pe.sem_inc(s_mark, 1)
            with pe.Fori(0, NC) as n:
                for b in range(2):
                    for mm in range(2):
                        u = 2 * b + mm
                        pe.wait_ge(s_da, n * 4 + (u + 1))
                        for k in range(2):
                            pe.matmul(bank[u][:, 0:NW], fw[:, 2 * b, k, P * mm:P * mm + P],
                                      hT[:, 2 * b + k, bass.ds(n * NW, NW)], start=(k == 0), stop=False)
                        for k in range(2):
                            ins = pe.matmul(bank[u][:, 0:NW], fw[:, 2 * b + 1, k, P * mm:P * mm + P],
                                            xT[:, k, bass.ds(n * NW, NW)], start=False, stop=(k == 1))
                        ins.then_inc(s_de, 1)
                pe.wait_ge(s_dL, n * 4 + 4)
                for mm in range(2):
                    pe.wait_ge(s_ct, n * 2 + (mm + 1))
                    for k in range(4):
                        ins = pe.matmul(bank[4 + mm][:, 0:NW], cat[:, k, P * mm:P * mm + P], L[:, k, :],
                                        start=(k == 0), stop=(k == 3))
                    ins.then_inc(s_cp, 1)
            def turn_back(g):
                pe.wait_ge(s_yT, g + 1)
                for t in range(BW * g, BW * g + BW):
                    if t >= 4:
                        pe.wait_ge(s_x1, t - 3)
                    for k in range(2):
                        ins = pe.transpose(bank[t % 4][0:NB, P * k:P * k + P], mixT[:, k, NB * t:NB * t + NB],
                                           ident[:, :])
                    ins.then_inc(s_yb, 1)

            def table(g):
                pe.wait_ge(s_tc, 2 * NC + 2 * g + 2)
                for t in range(BW * g, BW * g + BW):
                    for k in range(2):
                        ins = pe.matmul(bank[4][0:NB, 24 * t:24 * t + 24], xT[:, k, NB * t:NB * t + NB], wg[:, k, :],
                                        start=(k == 0), stop=(k == 1))
                return ins

            pe.wait_ge(s_ct, 2 * NC + 2)
            turn_back(0)
            turn_back(1)
            for g in range(1, NC + 1):
                if g + 1 < NC:
                    turn_back(g + 1)
                turn_rows(rows2, g - 1, T, 2 * NC, bank[5:8])
                if g == 2:
                    pe.wait_ge(s_wg, 1)
                if g >= 2:
                    table(g - 2)
            table(NC - 1).then_inc(s_tt, 1)
            pe.wait_ge(s_zero, 1)
            pe.matmul(bank[6][0:DH * TS, 0:DW], zeros[:, 0:DH * TS], zeros, start=True, stop=True,
                      skip_group_check=True)
            pe.matmul(bank[7][0:RB, 0:RB], zeros[:, 0:RB], zeros[:, 0:RB], start=True, stop=True,
                      skip_group_check=True)

            def tile_sums(r, i):
                pe.wait_ge(s_out, r * G + (i + 1))
                for k in range(2):
                    ins = pe.matmul(bank[6][0:DH * TS, 0:DW], values[i % 2][:, k].rearrange("p d v -> p (d v)"),
                                    digit[i % 2], start=False, stop=True, skip_group_check=True)
                ins.then_inc(s_sc, 1)

            def quarter(r, k):
                pe.wait_ge(s_cnt, r * 4 + (k + 1))
                for t in range(QT):
                    ins = pe.matmul(bank[7][0:RB, 0:RB], oa[k % 2][:, t, :], ob[k % 2][:, t, :],
                                    start=False, stop=True, skip_group_check=True)
                ins.then_inc(s_cs, 1)
                tile_sums(r, 2 * k)
                tile_sums(r, 2 * k + 1)

            def hidden(e, n, r, h):
                for mm in range(HM):
                    pe.wait_ge(s_h2, r * 8 + (h * 4 + mm + 1))
                    for k in range(2):
                        ins = pe.matmul(bank[mm][:, 0:HALF],
                                        W1s[e % 2][:, k, P * mm:P * mm + P],
                                        xT[:, k, bass.ds(n * NW + h * HALF, HALF)],
                                        start=(k == 0), stop=(k == 1))
                    ins.then_inc(s_h1, 1)

            def results(e, r, h):
                pe.wait_ge(s_h2, r * 8 + (h * 4 + 8))
                for b in range(2):
                    for k in range(HM):
                        ins = pe.matmul(bank[4 + h][0:NB, C * b:C * b + C], hid[h][:, k, NB * b:NB * b + NB],
                                        W2s[e % 2][:, k, :], start=(k == 0), stop=(k == HM - 1))
                ins.then_inc(s_y, 1)

            def step(e, n, with_round=True):
                r = n + e * NC
                for h in range(2):
                    hidden(e, n, r, h)
                if with_round:
                    quarter(r - 1, 0)
                for h in range(2):
                    pe.wait_ge(s_yt, r * 2 + (h + 1))
                    results(e, r, h)
                    if with_round and h == 0:
                        quarter(r - 1, 1)
                        quarter(r - 1, 2)
                if with_round:
                    quarter(r - 1, 3)

            for e in range(NEXP - 1):
                pe.wait_ge(s_w1[e % 2], 32 * (e // 2 + 1))
                if e == 0:
                    step(0, 0, False)
                with pe.Fori(0 if e else 1, NC) as n:
                    step(e, n)
            e = NEXP - 1
            pe.wait_ge(s_w1[e % 2], 32 * (e // 2 + 1))
            step(e, 0)
            pe.wait_ge(s_tb, 2)
            rem = pe.value_load(celli[0:1, 2:3], min_val=1, max_val=(EC - G * ROUNDS) // G + 1)
            with pe.Fori(0, rem) as i:
                for t in range(G):
                    tile_sums(i + ROUNDS, t)
            pe.wait_ge(s_vc, 1)
            for b in range(BW):
                ins = pe.transpose(bank[7][0:NB, DH * TS * b:DH * TS * b + DH * TS],
                                   vsum[0:DH * TS, NB * b:NB * b + NB], ident[0:DH * TS, 0:DH * TS])
            ins.then_inc(s_vt, 1)
            with pe.Fori(1, NC) as n:
                for h in range(2):
                    hidden(e, n, n + ROUNDS, h)
                for h in range(2):
                    pe.wait_ge(s_yc, n * 2 + (h - 1))
                    results(e, n + ROUNDS, h)

        @block.scalar
        def _(act):
            act.sem_inc(s_linf, 2)
            act.sem_inc(s_lin, 2)
            act.sem_inc(s_split, 2)
            act.sem_inc(s_scat, DEPTH)
            act.sem_inc(s_wcp, 2)
            act.sem_inc(s_acc, 2)
            act.sem_inc(s_wt, 2)
            act.sem_inc(s_sc, 2)
            act.sem_inc(s_cs, 2)
            act.sem_inc(s_yt, 2)
            act.sem_inc(s_y, 2)
            act.sem_inc(s_h2, 4)
            act.sem_inc(s_da, 4)
            act.sem_inc(s_ct, 2)
            act.sem_inc(s_cp, 2)
            act.sem_inc(s_nb, 1)
            act.sem_inc(s_at, 2)
            act.sem_inc(s_mix, 2)
            act.sem_inc(s_nr, 2)

            def deviation(k, g):
                b = slice(BW * g, BW * g + BW)
                act.wait_ge(s_st, NC * k + g + 1)
                act.activation(sd[0:NB, b], mv[0:NB, b, 1], ACT.Sqrt, bias=epsc[0:NB, :]).then_inc(s_sd, 1)

            act.wait_ge(s_fold, 1)
            act.wait_ge(s_fz, 1)
            act.copy(wraw[0:54, :], bank[0][0:54, 0:C])
            act.copy(wraw[64:118, :], bank[0][0:54, 0:C]).then_inc(s_foldc, 1)
            act.wait_ge(s_fold, 3)
            for w in range(4):
                ins = act.copy(fw[:, w, :, :].rearrange("p a b -> p (a b)"), bank[1 + w])
            ins.then_inc(s_foldc, 1)

            def turned(g, used, banks):
                for k in range(2):
                    act.wait_ge(s_tp, used + 2 * g + k + 1)
                    act.copy(xT[:, k, NW * g:NW * g + NW],
                             banks[(2 * g + k) % len(banks)][:, 0:NW]).then_inc(s_tc, 1)

            deviation(0, 0)
            for g in range(NC):
                if g + 1 < NC:
                    deviation(0, g + 1)
                turned(g, 0, bank[0:4])
            for t in range(T):
                act.wait_ge(s_km, t + 1)
                act.activation(kexp[0:NB, t % KV, :], kraw[0:NB, t % KV, :], ACT.Exp)
                act.activation(kraw[0:NB, t % KV, :], kraw[0:NB, t % KV, :], ACT.Relu).then_inc(s_ke, 1)
            act.wait_ge(s_xnd, 16 * NC)

            def query_parts(n):
                for c in range(2):
                    act.wait_ge(s_q, n * 2 + (c + 1))
                    act.wait_ge(s_pq, n * 2 + c)
                    act.activation(qexp[:, c, :], bank[c][:, 0:NW], ACT.Exp, bias=col(CBQ, c))
                    act.activation(qrel[:, c, :], bank[c][:, 0:NW], ACT.Relu, bias=col(CBQ, c)).then_inc(s_qe, 1)

            def normaliser(n):
                for c in range(2):
                    act.wait_ge(s_qn, n * 2 + (c + 1))
                    act.wait_ge(s_at, n * 2 + (c + 1))
                    act.activation(nrm[:, c, :], bank[3 + 2 * c][:, 0:NW], ACT.Identity,
                                   bias=tinyc[:, :]).then_inc(s_nr, 1)

            def mixed(n):
                for mm in range(2):
                    act.wait_ge(s_wo, n * 2 + (mm + 1))
                    act.activation(mixT[:, mm, bass.ds(n * NW, NW)], bank[6 + mm][:, 0:NW], ACT.Identity,
                                   bias=col(CBO, mm)).then_inc(s_mix, 1)

            for c in range(2):
                act.wait_ge(s_q, c + 1)
                act.activation(qexp[:, c, :], bank[c][:, 0:NW], ACT.Exp, bias=col(CBQ, c))
                act.activation(qrel[:, c, :], bank[c][:, 0:NW], ACT.Relu, bias=col(CBQ, c)).then_inc(s_qe, 1)
            with act.Fori(0, NC - 1) as n:
                normaliser(n)
                query_parts(n + 1)
                mixed(n)
            normaliser(NC - 1)
            mixed(NC - 1)
            act.wait_ge(s_base, 1)
            npass = act.value_load(celli[0:1, 0:1], min_val=1, max_val=N // WIN + 1)

            def select(p, c, j):
                q = p * NCH + c
                act.wait_ge(s_scat, q + 2)
                for t in range(CT):
                    ins = act.activation(sel[j][:, t, :], iota[:, 0:WIN], ACT.Abs,
                                         bias=nrel[:, bass.ds(c, 1), t:t + 1].rearrange("p o t -> p (o t)"))
                ins.then_inc(s_act, 1)
                act.wait_ge(s_act, q + 1)
                act.activation(sel[j], sel[j], ACT.Relu, bias=onec[:, :], scale=-1.0).then_inc(s_sel, 1)

            def upper_parts(p, w, b):
                q = p * NCH + w * 2 + b
                act.wait_ge(s_feat[b], (p * NWIN + w) * 32 + 32)
                act.wait_ge(s_lin, q * 2 + 2)
                act.wait_ge(s_split, q + 2)
                act.copy(upper, feat[b]).then_inc(s_upper, 1)

            def copy_window(p, w, b):
                act.wait_ge(s_scat, p * NCH + w * 2 + (2 + DEPTH))
                act.wait_ge(s_wt, p * NWIN + w + 1)
                act.copy(wsum[b], bank[b]).then_inc(s_wcp, 1)

            with act.Fori(0, npass) as p:
                act.wait_ge(s_nb, p + 1)
                upper_parts(p, 0, 0)
                select(p, 0, 0)
                upper_parts(p, 0, 1)
                select(p, 1, 1)
                upper_parts(p, 1, 0)
                with act.Fori(0, NWIN // 2 - 1) as i:
                    for b in range(2):
                        w = i * 2 + b
                        select(p, w * 2 + 2, 0)
                        upper_parts(p, w + 1, 1)
                        copy_window(p, w, b)
                        select(p, w * 2 + 3, 1)
                        upper_parts(p, w + 2, 0)
                select(p, NCH - 2, 0)
                upper_parts(p, NWIN - 1, 1)
                copy_window(p, NWIN - 2, 0)
                select(p, NCH - 1, 1)
                copy_window(p, NWIN - 1, 1)
            act.wait_ge(s_scat, npass * NCH + DEPTH)
            with act.Fori(0, NC) as n:
                act.wait_ge(s_cp, n * 2 + 2)
                for u in range(4):
                    act.wait_ge(s_de, n * 4 + (u + 1))
                    act.activation(L[:, u, :], bank[u][:, 0:NW], ACT.Identity,
                                   bias=fbias[:, u:u + 1]).then_inc(s_da, 1)
                for mm in range(2):
                    act.wait_ge(s_cp, n * 2 + (mm + 3))
                    act.activation(HT[:, mm, bass.ds(n * NW, NW)], bank[4 + mm][:, 0:NW], ACT.Identity,
                                   bias=col(CCAT, mm)).then_inc(s_ct, 1)
            act.wait_ge(s_gv, 1)
            act.activation(cols[:, 2 * CVAR:2 * CVAR + 2], cols[:, 2 * CVAR:2 * CVAR + 2], ACT.Sqrt,
                           bias=epsc[:, :]).then_inc(s_gq, 1)
            act.wait_ge(s_gc, 1)
            for g in range(NC):
                for mm in range(2):
                    v = HT[:, mm, NW * g:NW * g + NW]
                    ins = act.activation(v, v, ACT.Identity, bias=col(CBB, mm), scale=col(CA, mm))
                ins.then_inc(s_gn, 1)
            deviation(1, 0)
            for g in range(NC):
                if g + 1 < NC:
                    deviation(1, g + 1)
                turned(g, 2 * NC, bank[5:8])

            def exponents(r):
                act.wait_ge(s_z, r + 1)
                act.activation(ez, z, ACT.Exp).then_inc(s_ez, 1)

            def gelus(e, r, h):
                act.wait_ge(s_y, r * 2 + (h + 1))
                for mm in range(HM):
                    act.wait_ge(s_h1, r * 8 + (h * 4 + mm + 1))
                    act.activation(hid[h][:, mm, :], bank[mm][:, 0:HALF],
                                   ACT.Gelu, bias=b1c[:, e * HM + mm:e * HM + mm + 1]).then_inc(s_h2, 1)

            act.wait_ge(s_a1, 1)
            act.activation(es[0:NB], es[0:NB], ACT.Exp).then_inc(s_ow, 1)
            act.activation(el[0:NB], el[0:NB], ACT.Exp).then_inc(s_ow, 1)
            for e in range(NEXP - 1):
                with act.Fori(0, NC) as n:
                    for h in range(2):
                        gelus(e, n + e * NC, h)
                    exponents(n + e * NC)

            def last_expert(n):
                for h in range(2):
                    gelus(NEXP - 1, ROUNDS + n, h)
                for h in range(2):
                    act.wait_ge(s_y, 2 * (ROUNDS + n) + h + 3)
                    act.copy(Y[0:NB, n * BW + 2 * h:n * BW + 2 * h + 2, NEXP - 1, :],
                             bank[4 + h][0:NB, :].rearrange("p (b c) -> p b c", b=2)).then_inc(s_yc, 1)

            last_expert(0)
            exponents(ROUNDS)
            act.wait_ge(s_tb, 2)
            rem = act.value_load(celli[0:1, 2:3], min_val=1, max_val=(EC - G * ROUNDS) // G + 1)
            with act.If(rem - 1):
                with act.Fori(1, rem) as r:
                    exponents(r + ROUNDS)
            act.wait_ge(s_sc, rem * G + (G * ROUNDS + 2))
            act.copy(vsum[0:DH * TS, :], bank[6][0:DH * TS, 0:DW]).then_inc(s_vc, 1)
            last_expert(1)
            act.wait_ge(s_a1, 2)
            act.activation(sd[0:NB, :], sc[0:NB, :, 0], ACT.Sqrt, bias=epsc[0:NB, :]).then_inc(s_ow, 1)
            last_expert(2)
            act.wait_ge(s_a1, 3)
            act.activation(gg[0:NB], gg[0:NB], ACT.Exp).then_inc(s_ow, 1)
            for n in range(3, NC):
                last_expert(n)

        @block.vector
        def _(dve):
            st = Steps(dve, s_vec)
            TT, TS1, STT = dve.tensor_tensor, dve.tensor_scalar, dve.scalar_tensor_tensor
            st.did(dve.memset(epsc[:, :], EPS))
            st.did(dve.memset(tinyc[:, :], 1e-6))
            st.did(dve.memset(onec[:, :], 1.0))
            st.did(dve.memset(hmask[:, :], 0.0))
            st.did(dve.memset(vrow[:, :, :, P:P + 1], 1.0))
            st.settle()
            for g in range(4):
                st.did(dve.memset(hmask[32 * g:32 * g + 32, 32 * g:32 * g + 32], 1.0))

            st.then(dve.memset(wraw, 0.0))
            dve.sem_inc(s_fz, 1)

            dve.wait_ge(s_dl, 16)
            st.then(dve.tensor_copy(nrel[:, :, :], nrel[:, :, :].bitcast(I32)))
            st.did(dve.tensor_reduce(small[:, 0:NWIN], nrel_w, AX, ALU.min))
            dve.tensor_reduce(small[:, NWIN:2 * NWIN], nrel_w, AX, ALU.max)
            st.settle()
            dve.tensor_scalar(small[:, 0:NWIN], small[:, 0:NWIN], -1.0, None, ALU.mult).then_inc(s_dm, 1)

            def measure(rows, g):
                for t in range(BW * g, BW * g + BW):
                    st.did(dve.bn_stats(stats[0:NB, t, :], rows[0:NB, t, :]))
                st.settle()
                for t in range(BW * g, BW * g + BW):
                    ins = dve.bn_aggr(mv[0:NB, t, :], stats[0:NB, t, :])
                ins.then_inc(s_st, 1)

            def normalise(rows, out_rows, k, g):
                b = slice(BW * g, BW * g + BW)
                dve.wait_ge(s_sd, NC * k + g + 1)
                st.then(dve.reciprocal(rs[0:NB, b], sd[0:NB, b]))
                for t in range(BW * g, BW * g + BW):
                    TS1(out_rows[0:NB, t, :], rows[0:NB, t, :], mv[0:NB, t, 0:1], rs[0:NB, t:t + 1],
                        ALU.subtract, ALU.mult).then_inc(s_xn, 1)

            for g in range(NC):
                dve.wait_ge(s_x[g], 16)
                measure(x_rows, g)
                if g:
                    normalise(x_rows, rows_n, 0, g - 1)
            normalise(x_rows, rows_n, 0, NC - 1)
            dve.wait_ge(s_foldc, 1)
            st.did(dve.tensor_copy(wf[0:64, :], wraw[0:64, :]))
            st.then(dve.tensor_copy(wupper[64:P, :], wraw[64:P, :]))
            st.then(TT(wf[64:P, :], wraw[64:P, :], wupper[64:P, :].bitcast(F32), ALU.subtract))
            dve.wait_ge(s_fold, 3)
            st.did(dve.memset(fraw, 0.0))
            TT(fbias[:, :], bank[5][:, 0:4], cols[:, 2 * CLB1:2 * CLB1 + 4], ALU.add).then_inc(s_foldc, 1)

            dve.wait_ge(s_ar, 1)
            st.did(TT(nrel_w, nrel_w, over(ared[:, 0:NWIN], P, NWIN, 2 * CT), ALU.add))
            st.then(TT(small[:, 0:NWIN], ared[:, NWIN:2 * NWIN], ared[:, 0:NWIN], ALU.add))
            st.then(dve.tensor_reduce(cellf[:, 0:1], small[:, 0:NWIN], AX, ALU.max))
            st.then(dve.tensor_copy(celli[:, 0:1], cellf[:, 0:1]))
            st.then(TS1(celli[:, 1:2], celli[:, 0:1], WIN.bit_length() - 1, None, ALU.arith_shift_right))
            st.did(TS1(celli[:, 0:1], celli[:, 1:2], 1.0, None, ALU.add))
            st.did(TS1(nrel[:, :, :], nrel[:, :, :], -1.0, None, ALU.mult))
            st.did(TS1(basef[:, :], ared[0:1, 0:NWIN], -1.0, None, ALU.mult))
            st.settle()
            dve.tensor_copy(basei[:, :], basef[:, :]).then_inc(s_base, 1)

            dve.wait_ge(s_w[1], 16 * 5)

            def key_map(t):
                dve.wait_ge(s_ke, t + 1)
                STT(kexp[0:NB, t % KV, :], kexp[0:NB, t % KV, :], 1.0, kraw[0:NB, t % KV, :],
                    ALU.min, ALU.add).then_inc(s_pk, 1)

            for t in range(T):
                dve.wait_ge(s_kv, t + 1)
                if t >= KV:
                    dve.wait_ge(s_kvs, t - KV + 1)
                i = (4, 5, 2, 3)[t % KV]
                TT(kraw[0:NB, t % KV, :], bank[i][0:NB, 0:C], bkv_s[0:NB, 0:C], ALU.add).then_inc(s_km, 1)
                TT(vrow[0:NB, t % KV, :, 0:P], bank[i][0:NB, C:2 * C].rearrange("p (c n) -> p c n", c=2),
                   bkv_s[0:NB, C:2 * C].rearrange("p (c n) -> p c n", c=2), ALU.add).then_inc(s_kvu, 1)
                if t >= 1:
                    key_map(t - 1)
            key_map(T - 1)
            dve.wait_ge(s_kvs, T)
            st.settle()
            for c in range(2):
                st.did(TT(kvbd[:, c, 0, :], bank[6 + c][:, 0:P], hmask[:, :], ALU.mult))
                ins = TS1(kvbd[:, c, 1, :], hmask[:, :], bank[6 + c][:, P:P + 1], None, ALU.mult)
            ins.then_inc(s_bd, 1)
            dve.wait_ge(s_xnd, 16 * NC)
            v0 = st.k

            def query_map(n):
                for c in range(2):
                    dve.wait_ge(s_qe, n * 2 + (c + 1))
                    STT(qraw[:, c, :], qexp[:, c, :], 1.0, qrel[:, c, :], ALU.min, ALU.add).then_inc(s_pq, 1)

            def normalised(n):
                st.restart(n * 2 + v0)
                for c in range(2):
                    dve.wait_ge(s_nr, n * 2 + (c + 3))
                    st.then(dve.reciprocal(nrm[:, c, :], nrm[:, c, :]))
                    dve.wait_ge(s_wo, n * 2)
                    TT(att[:, c, :], bank[2 + 2 * c][:, 0:NW], nrm[:, c, :], ALU.mult).then_inc(s_at, 1)

            dve.memset(low[:, T * C:KVB], 0.0)
            query_map(0)
            st.restart(v0)
            for c in range(2):
                dve.wait_ge(s_nr, c + 3)
                st.then(dve.reciprocal(nrm[:, c, :], nrm[:, c, :]))
                TT(att[:, c, :], bank[2 + 2 * c][:, 0:NW], nrm[:, c, :], ALU.mult).then_inc(s_at, 1)
            with dve.Fori(1, NC) as n:
                dve.wait_ge(s_qn, n * 2)
                query_map(n)
                normalised(n)
            st.restart(v0 + 2 * NC)

            npass = dve.value_load(celli[0:1, 0:1], min_val=1, max_val=N // WIN + 1)
            dve.wait_ge(s_mix, 2 * NC + 2)
            st.did(TS1(low[:, 0:QB].bitcast(I32), low[:, 0:QB].bitcast(I32), 0, None, ALU.bitwise_and))
            st.did(dve.memset(low[:, QB:T * C], 0.0))
            st.did(dve.memset(low[:, KVB:4 * HTW], 0.0))
            dve.wait_ge(s_cst, 2)
            v0 = st.base + st.k
            halves = (slice(0, 4), slice(4, CT))
            banks = (psum[:, 2:4, :].rearrange("p b (t c) -> p (b t) c", c=C),
                     psum[:, 4:6, :].rearrange("p b (t c) -> p (b t) c", c=C)[:, 0:CT - 4, :])

            def split(q, b):
                dve.wait_ge(s_lin, q * 2 + 2)
                dve.wait_ge(s_upper, q + 1)
                TT(lower, feat[b], upper.bitcast(F32), ALU.subtract).then_inc(s_split, 1)

            def chunk(p, c, use, j, more=True):
                d, q = j % DEPTH, p * NCH + c
                dve.wait_ge(s_gate[d], use * 16)
                dve.wait_ge(s_gath[d], use * (16 * CT))
                for h, ts in enumerate(halves):
                    dve.wait_ge(s_lin, q * 2 + (h + 3))
                    TT(gath[d][:, ts, :], banks[h], gath[d][:, ts, :], ALU.mult).then_inc(s_linf, 1)
                if more:
                    split(q + 1, (j + 1) % 2)
                for h, ts in enumerate(halves):
                    dve.wait_ge(s_linf, q * 2 + (h + 3))
                    TT(gath[d][:, ts, :], gath[d][:, ts, :], gate[d][:, ts, :], ALU.mult).then_inc(s_m1, 1)
                for h, ts in enumerate(halves):
                    dve.wait_ge(s_m1, q * 2 + (h + 1))
                    TT(gate[d][:, ts, :], gath[d][:, ts, :], gate[d][:, ts, :], ALU.mult).then_inc(s_msg, 1)

            def add_window(p, c, w):
                v = p * NWIN + c
                dve.wait_ge(s_wt, v + 3)
                dve.wait_ge(s_acc, v + 2)
                dve.sem_inc(s_mark, 1)
                at = dve.value_load(basei[0:1, bass.ds(c, 1)], min_val=0, max_val=N)
                TT(hT[:, :, bass.ds(at, WIN)], hT[:, :, bass.ds(at, WIN)],
                   bank[6 + w % 2].rearrange("p (f w) -> p f w", f=4), ALU.add).then_inc(s_acc, 1)

            U3 = NCH // DEPTH
            with dve.Fori(0, npass) as p:
                split(p * NCH, 0)
                for j in range(BODY):
                    chunk(p, j, p * U3 + (j // DEPTH + 1), j)
                    if j % 2 and j > 1:
                        add_window(p, j // 2 - 1, j // 2 - 1)
                with dve.Fori(1, NCH // BODY - 1) as i:
                    for j in range(BODY):
                        chunk(p, i * BODY + j, p * U3 + i * (BODY // DEPTH) + (j // DEPTH + 1), j)
                        if j % 2:
                            add_window(p, i * (BODY // 2) + (j // 2 - 1), j // 2 - 1)
                for j in range(BODY):
                    c = NCH - BODY + j
                    chunk(p, c, p * U3 + (c // DEPTH + 1), j, c + 1 < NCH)
                    if j % 2:
                        add_window(p, c // 2 - 1, j // 2 - 1)
                add_window(p, NWIN - 1, NWIN - 1)
                st.restart(v0 + p * 2)
                st.did(TS1(nrel[:, :, :], nrel[:, :, :], float(WIN), None, ALU.add))
                st.then(TS1(basef[:, :], basef[:, :], float(WIN), float(N), ALU.add, ALU.min))
                st.settle()
                dve.tensor_copy(basei[:, :], basef[:, :]).then_inc(s_nb, 1)
                dve.wait_ge(s_nb, p + 2)
            v0 = npass * 2 + v0

            st.restart(v0)
            dve.wait_ge(s_el, 32)
            st.did(dve.memset(shared[:, :], 0.0))
            st.then(TS1(emask, edst, float(N), None, ALU.is_lt))
            A, B = cnt_a[:, 0:EC], cnt_b[:, 0:EC]
            st.then(STT(A, esrc, float(N - 1), emask, ALU.is_ge, ALU.mult))
            st.did(TT(emask, emask, A, ALU.subtract))
            st.then(STT(ekey, edst, 4096.0, esrc, ALU.mult, ALU.add))
            st.did(STT(ekey, ekey, 1.0, emask, ALU.add, ALU.mult))
            dve.tensor_reduce(small[:, 0:1], emask, AX, ALU.add).then_inc(s_dm, 1)
            st.then(STT(B, edst, 1.0, A, ALU.add, ALU.mult))
            dve.sem_inc(s_dm, 1)
            st.then(TS1(cnt_a, cnt_b, -0.5, 1.0 / RB, ALU.add, ALU.mult))
            st.then(TS1(cnt_a, cnt_a, -0.5, MAGIC, ALU.add, ALU.add))
            st.then(TS1(cnt_a, cnt_a, -MAGIC, None, ALU.add))
            st.then(STT(cnt_b, cnt_a, -float(RB), cnt_b, ALU.mult, ALU.add))
            st.then(TS1(cnt_b, cnt_b, -1.0, None, ALU.add))
            dve.wait_ge(s_ar, 2)
            S0 = 8 * SORTS * NC
            st.did(TS1(cellf[:, 1:2], ared[:, 0:1], 1.0 / 8, -(S0 - 7.5) / 8 - 0.5, ALU.mult, ALU.add))
            st.then(TS1(cellf[:, 2:3], ared[:, 0:1], 1.0 / G, -(G * ROUNDS - G + 0.5) / G - 0.5, ALU.mult, ALU.add))
            st.then(TS1(cellf[:, 1:3], cellf[:, 1:3], MAGIC, None, ALU.add))
            st.then(TS1(cellf[:, 1:3], cellf[:, 1:3], -MAGIC, 1.0, ALU.add, ALU.max))
            st.then(dve.tensor_copy(celli[:, 1:3], cellf[:, 1:3]))
            dve.sem_inc(s_mark, 1)
            srem = dve.value_load(celli[0:1, 1:2], min_val=1, max_val=EC // 8 - SORTS * NC)
            v0 = v0 + st.k

            def sort_step(st, s):
                st.did(dve.max(srt[:, :], ekey))
                st.settle()
                dve.sem_inc(s_mark, 1)
                st.did(dve.match_replace(ekey, srt[:, :], ekey, 0.0))
                st.then(dve.tensor_copy(kbuf[:, bass.ds(s * 8, 8)], srt[:, :]))
                dve.sem_inc(s_mark, 1)

            with dve.Fori(0, NC) as n:
                st.restart(n * (3 * SORTS + 2) + v0)
                for u in range(4):
                    dve.wait_ge(s_da, n * 4 + (u + 5))
                    STT(L[:, u, :], L[:, u, :], 0.1, L[:, u, :], ALU.mult, ALU.max).then_inc(s_dL, 1)
                for s in range(SORTS):
                    sort_step(st, n * SORTS + s)
                dve.wait_ge(s_ct, n * 2 + 4)
                for mm in range(2):
                    st.did(dve.bn_stats(gstat[:, mm, bass.ds(n, 1), :].rearrange("p o s -> p (o s)"),
                                        HT[:, mm, bass.ds(n * NW, NW)]))
            v0 = v0 + (3 * SORTS + 2) * NC
            st.restart(v0)
            st.settle()
            sk, st = st, Steps(dve, s_vec2)
            dve.sem_inc(s_mark, 1)
            for mm in range(2):
                st.did(dve.bn_aggr(gmv[:, mm, :], gstat[:, mm, :, :]))
            st.settle()
            st.then(STT(cols[:, 2 * CMU:2 * CMU + 2], gmv[:, :, 0], -1.0, cols[:, 2 * CGM:2 * CGM + 2],
                        ALU.mult, ALU.mult))
            st.then(TT(cols[:, 2 * CA:2 * CA + 2], gmv[:, :, 0], cols[:, 2 * CMU:2 * CMU + 2], ALU.add))
            st.then(TT(cols[:, 2 * CA:2 * CA + 2], cols[:, 2 * CA:2 * CA + 2], cols[:, 2 * CA:2 * CA + 2], ALU.mult))
            TT(cols[:, 2 * CVAR:2 * CVAR + 2], gmv[:, :, 1], cols[:, 2 * CA:2 * CA + 2], ALU.add).then_inc(s_gv, 1)
            dve.wait_ge(s_gv, 1)
            dve.wait_ge(s_gq, 1)
            st.then(dve.reciprocal(cols[:, 2 * CA:2 * CA + 2], cols[:, 2 * CVAR:2 * CVAR + 2]))
            st.then(TT(cols[:, 2 * CA:2 * CA + 2], cols[:, 2 * CA:2 * CA + 2], cols[:, 2 * CGW:2 * CGW + 2], ALU.mult))
            st.then(TT(cols[:, 2 * CBB:2 * CBB + 2], cols[:, 2 * CA:2 * CA + 2], cols[:, 2 * CMU:2 * CMU + 2], ALU.mult))
            TT(cols[:, 2 * CBB:2 * CBB + 2], cols[:, 2 * CBB:2 * CBB + 2], cols[:, 2 * CGB:2 * CGB + 2],
               ALU.add).then_inc(s_gc, 1)
            for g in range(NC):
                dve.wait_ge(s_gn, g + 1)
                v = slice(NW * g, NW * g + NW)
                TT(mixT[:, :, v], HT[:, :, v], mixT[:, :, v], ALU.add).then_inc(s_yT, 1)
            def fold_logits():
                dve.wait_ge(s_gl, 16 * 7)
                for i in range(2):
                    for k in range(2):
                        st.did(TT(V.rearrange("p a b -> p (a b)")[:, (2 * i + k) * HE:(2 * i + k + 1) * HE], wg[:, k, 0:HE],
                                  attb[:, HE * i:HE * i + HE], ALU.mult))
                st.settle()
                for i in range(2):
                    for k in range(2):
                        ins = dve.tensor_reduce(wg[:, k, HE + 4 * i:HE + 4 * i + 4],
                                                V.rearrange("p a b -> p (a b)")[:, (2 * i + k) * HE:(2 * i + k + 1) * HE]
                                                .rearrange("p (h e) -> p h e", h=HEADS), AX, ALU.add)
                ins.then_inc(s_wg, 1)
            for g in range(NC):
                for t in range(BW * g, BW * g + BW):
                    dve.wait_ge(s_yb, t + 1)
                    TT(x_rows[0:NB, t, :], bank[t % 4][0:NB, 0:C], x_rows[0:NB, t, :], ALU.add).then_inc(s_x1, 1)
                dve.wait_ge(s_x1, BW * (g + 1))
                measure(x_rows, g)
                if g == 0:
                    dve.wait_ge(s_yT, NC)
                if g:
                    normalise(x_rows, rows2, 1, g - 1)
                if g == 1:
                    fold_logits()
            normalise(x_rows, rows2, 1, NC - 1)
            with dve.Fori(0, srem) as s:
                sk.restart(s * 3 + v0)
                sort_step(sk, s + SORTS * NC)
            sk.restart(srem * 3 + v0)
            sk.settle()
            dve.sem_inc(s_mark, 1)
            dve.memset(zeros, 0.0).then_inc(s_zero, 1)
            dve.wait_ge(s_tt, 1)
            dve.tensor_copy(tab[0:NB], bank[4][0:NB, 0:24 * T].rearrange("p (t c) -> p t c", t=T)).then_inc(s_tb, 1)
            dve.wait_ge(s_tb, 1)
            st.then(dve.memset(mx, -3e38))
            st.did(dve.tensor_reduce(mx[0:NB, 0:4], tab[0:NB, :, HE:TS].rearrange("p t h -> p h t"), AX, ALU.max))
            st.then(dve.tensor_reduce(mx[0:NB, 4:8], tab[0:NB, :, HE:TS].rearrange("p t h -> p h t"), AX, ALU.min))
            TS1(mx[0:NB, 4:8], mx[0:NB, 4:8], -1.0, None, ALU.mult).then_inc(s_tm, 1)
            st.did(dve.tensor_copy(td[0:NB, :, 0:4], tab[0:NB, :, TS:24]))
            dve.wait_ge(s_ar, 3)
            st.then(TT(td[0:NB, :, 4:8], tab[0:NB, :, TS:24],
                       mall[0:NB, 0:4].unsqueeze(1).broadcast_to((NB, T, 4)), ALU.add))
            st.then(TT(mx[:, 8:12], mall[:, 0:4], mall[:, 4:8], ALU.add))
            st.then(dve.tensor_reduce(cellf[:, 3:4], mx[:, 8:12], AX, ALU.max))
            st.then(TS1(cellf[:, 3:4], cellf[:, 3:4], SAFE, None, ALU.is_gt))
            dve.tensor_copy(celli[:, 3:4], cellf[:, 3:4]).then_inc(s_wide, 1)
            dve.wait_ge(s_wide, 1)
            dve.sem_inc(s_mark, 1)
            wide = dve.value_load(celli[0:1, 3:4], min_val=0, max_val=1)
            with dve.If(wide):
                sv = Steps(dve, s_sv)
                sv.did(dve.memset(smf, 0.0))
                sv.did(dve.tensor_scalar(niota[:, 0:P], iota[:, 0:P], 0.0, None, ALU.add))
                sv.settle()
                for b in range(1, -(-N // P)):
                    w = min(P, N - P * b)
                    sv.did(TS1(niota[:, P * b:P * b + w], iota[:, 0:w], float(P * b), None, ALU.add))
                dve.wait_ge(s_se, 32)
                sv.settle()
                with dve.Fori(0, EC) as c:
                    sv.restart(c * (4 + 2 * HEADS) + (1 + -(-N // P)))
                    sv.settle()
                    sv.did(dve.tensor_copy(sdf, sdst[:, bass.ds(c, 1)]))
                    sv.then(dve.tensor_copy(srel[:, 0:1], ssrc[:, bass.ds(c, 1)]))
                    sv.then(TS1(srel[:, 0:1], srel[:, 0:1], float(N - 1), None, ALU.min))
                    dve.tensor_copy(sidx, srel[:, 0:1]).then_inc(s_si, 1)
                    dve.wait_ge(s_sg, c * 16 + 16)
                    sv.then(TT(srel, srow[:, HE:TS], mall[:, 4:8], ALU.add))
                    for h in range(HEADS):
                        sv.then(TS1(smo, niota, sdf, srel[:, h:h + 1], ALU.is_equal, ALU.mult))
                        sv.then(TT(smt[:, :, h], smt[:, :, h], smo, ALU.max))
                dve.sem_inc(s_sm, 1)
                dve.wait_ge(s_sl, 16)
                sv.restart(EC * (4 + 2 * HEADS) + (1 + -(-N // P)))
                sv.then(TT(smx[0:NB], smx[0:NB], mall[0:NB, 4:8].unsqueeze(1).broadcast_to((NB, T, 4)), ALU.subtract))
                sv.then(TT(smx[0:NB], smx[0:NB], tab[0:NB, :, HE:TS], ALU.max))
                sv.then(TT(td[0:NB, :, 4:8], tab[0:NB, :, TS:24], smx[0:NB], ALU.add))
            STT(td[0:NB, :, 4:8], td[0:NB, :, 4:8], 0.2, td[0:NB, :, 4:8], ALU.mult, ALU.max).then_inc(s_tb, 1)
            dve.wait_ge(s_tb, 2)
            rem = dve.value_load(celli[0:1, 2:3], min_val=1, max_val=(EC - G * ROUNDS) // G + 1)

            def prepare(r):
                st.then(TS1(kI, kbuf[:, bass.ds(r * G, G)], -1.0, None, ALU.add))
                st.did(TS1(nindex[:, 0], kI, 4095, None, ALU.bitwise_and))
                st.then(TS1(dI, kI, 12, None, ALU.arith_shift_right))
                st.did(TS1(nindex[:, 0], nindex[:, 0], float(N - 1), None, ALU.min))
                st.did(TS1(ndigits[:, 0], dI, 0.5, 1.0 / DW, ALU.add, ALU.mult))
                st.then(TS1(nindex[:, 1], dI, 0.0, None, ALU.max))
                st.then(TS1(ndigits[:, 0], ndigits[:, 0], -0.5, MAGIC, ALU.add, ALU.add))
                st.then(TS1(ndigits[:, 0], ndigits[:, 0], -MAGIC, None, ALU.add))
                st.did(STT(ndigits[:, 1], ndigits[:, 0], -float(DW), dI, ALU.mult, ALU.add))

            def begin(r, v):
                st.restart(v)
                st.settle()
                dve.wait_ge(s_gg, r * (32 * G) + 32 * G)
                st.did(dve.tensor_copy(WA, GA))
                st.did(dve.tensor_copy(WB, GB))
                dve.tensor_copy(index, nindex).then_inc(s_ki, 1)
                st.settle()
                st.then(TT(z, WA[:, :, HE:TS], WB[:, :, 0:4], ALU.add))
                st.then(STT(z, z, 0.2, z, ALU.mult, ALU.max))
                TT(z, z, WB[:, :, 4:8], ALU.subtract).then_inc(s_z, 1)
                st.did(TT(OH, over(digits[:, 0], P, G, DH), iota[:, 0:DH].unsqueeze(1).broadcast_to((P, G, DH)), ALU.is_equal))
                st.then(dve.tensor_copy(lcur, digits[:, 1]))
                st.then(dve.tensor_copy(digits, ndigits))
                dve.wait_ge(s_ki, r + 2)
                prepare(r + 2)
                dve.wait_ge(s_ez, r + 1)
                st.did(TT(V[:, :, 0:HE].rearrange("p t (h e) -> p t h e", h=HEADS),
                          WA[:, :, 0:HE].rearrange("p t (h e) -> p t h e", h=HEADS),
                          over(ez, P, G, HEADS, NEXP), ALU.mult))
                st.then(dve.tensor_copy(V[:, :, HE:TS], ez))
                st.then(dve.tensor_copy(VP[:, :, 0, :].bitcast(F22), V))
                st.then(TT(VP[:, :, 1, :].bitcast(F22), V, VP[:, :, 0, :], ALU.subtract))

            def tile(r, i):
                dve.wait_ge(s_sc, r * G + (i + 1))
                TS1(digit[i % 2], iota[:, :], lcur[:, i:i + 1], None, ALU.is_equal)
                TT(values[i % 2], OH[:, i:i + 1, :].unsqueeze(3).broadcast_to((P, 2, DH, TS)),
                   VP[:, i, :, :].unsqueeze(2).broadcast_to((P, 2, DH, TS)), ALU.mult).then_inc(s_out, 1)

            def quarter(r, k):
                dve.wait_ge(s_cs, r * 4 + (k + 1))
                for buf, of in ((oa[k % 2], cnt_a), (ob[k % 2], cnt_b)):
                    ins = TT(buf, over(of[:, bass.ds(r * (4 * QT) + k * QT, QT)], P, QT, RB),
                             iota[:, 0:RB].unsqueeze(1).broadcast_to((P, QT, RB)), ALU.is_equal)
                ins.then_inc(s_cnt, 1)
                tile(r, 2 * k)
                tile(r, 2 * k + 1)

            prepare(0)
            st.settle()
            st.did(dve.tensor_copy(digits, ndigits))
            dve.tensor_copy(index, nindex).then_inc(s_ki, 1)
            dve.wait_ge(s_ki, 1)
            st.settle()
            prepare(1)
            dve.wait_ge(s_last, 16)
            R = slice(0, NB)
            st.did(TT(es[R], tab[R, :, HE:TS], tab[R, :, TS:24], ALU.add))
            st.then(TT(el[R], tab[R, :, TS:24], last[R, HE:TS].unsqueeze(1).broadcast_to((NB, T, 4)), ALU.add))
            st.did(STT(es[R], es[R], 0.2, es[R], ALU.mult, ALU.max))
            st.then(STT(el[R], el[R], 0.2, el[R], ALU.mult, ALU.max))
            st.did(TT(es[R], es[R], td[R, :, 4:8], ALU.subtract))
            TT(el[R], el[R], td[R, :, 4:8], ALU.subtract).then_inc(s_a1, 1)

            def take(e, n):
                r = n + e * NC
                for h in range(2):
                    dve.wait_ge(s_y, r * 2 + (h + 3))
                    TT(Y[0:NB, bass.ds(n * BW + 2 * h, 2), e, :], bank[4 + h][0:NB, :].rearrange("p (b c) -> p b c", b=2),
                       b2b[0:NB, C * e:C * e + C].unsqueeze(1).broadcast_to((NB, 2, C)), ALU.add).then_inc(s_yt, 1)

            take(0, 0)
            v0 = st.k
            begin(0, v0)
            per = st.k
            for e in range(NEXP - 1):
                with dve.Fori(0 if e else 1, NC) as n:
                    r = n + (e * NC - 1)
                    for k in range(4):
                        quarter(r, k)
                    begin(r + 1, n * per + (v0 + e * NC * per))
                    assert st.k == per
                    take(e, n)
            for k in range(4):
                quarter(ROUNDS - 1, k)
            begin(ROUNDS, v0 + ROUNDS * per)
            dve.wait_ge(s_cs, 4 * ROUNDS + 2)
            dve.tensor_copy(cc[0:RB, 0:RB], bank[7][0:RB, 0:RB]).then_inc(s_cst2, 1)
            v0 = v0 + (ROUNDS + 1) * per
            for t in range(G):
                tile(ROUNDS, t)
            with dve.If(rem - 1):
                with dve.Fori(1, rem) as r:
                    begin(r + ROUNDS, r * per + (v0 - per))
                    for t in range(G):
                        tile(r + ROUNDS, t)
            st.restart(rem * per + (v0 - per))

            dve.wait_ge(s_ow, 2)
            dve.wait_ge(s_cl, 16)
            st.did(TT(el[R], el[R], over(cn[R], NB, T, 4), ALU.mult))
            h4 = lambda v: v.rearrange("p t (h e) -> p t h e", h=HEADS)
            st.then(TT(h4(f1[R]), h4(tab[R, :, 0:HE]), over(es[R], NB, T, HEADS, NEXP), ALU.mult))
            st.did(TT(es[R], es[R], el[R], ALU.add))
            st.then(TT(h4(f2[R]), last[R, 0:HE].unsqueeze(1).broadcast_to((NB, T, HE)).rearrange("p t (h e) -> p t h e", h=HEADS),
                       over(el[R], NB, T, HEADS, NEXP), ALU.mult))
            dve.wait_ge(s_vt, 1)
            st.then(dve.tensor_copy(agg[R].rearrange("p (d b) v -> p d b v", d=DH),
                                    bank[7][R, 0:T * TS].rearrange("p (b d v) -> p d b v", b=BW, d=DH)))
            st.did(TT(agg[R, :, 0:HE], agg[R, :, 0:HE], f1[R], ALU.add))
            st.then(TT(agg[R, :, HE:TS], agg[R, :, HE:TS], es[R], ALU.add))
            st.did(TT(agg[R, :, 0:HE], agg[R, :, 0:HE], f2[R], ALU.add))
            st.then(TS1(es[R], agg[R, :, HE:TS], 1e-16, None, ALU.add))
            st.then(dve.reciprocal(es[R], es[R]))
            st.then(TT(h4(f1[R]), h4(agg[R, :, 0:HE]), over(es[R], NB, T, HEADS, NEXP), ALU.mult))

            def by_value(i):
                return bgb[R, HE * i:HE * i + HE].unsqueeze(1).broadcast_to((NB, T, HE))

            st.then(TT(f1[R], f1[R], by_value(0), ALU.add))
            st.then(dve.tensor_reduce(t1[R], f1[R], AX, ALU.add))
            st.then(TS1(t1[R], t1[R], -1.0 / HE, None, ALU.mult))
            st.then(TT(f1[R], f1[R], over(t1[R], NB, T, HE), ALU.add))
            st.then(TT(f2[R], f1[R], f1[R], ALU.mult))
            st.then(dve.tensor_reduce(t2[R], f2[R], AX, ALU.add))
            TS1(sc[R, :, 0], t2[R], 1.0 / HE, None, ALU.mult).then_inc(s_a1, 1)
            dve.wait_ge(s_ow, 3)
            st.then(dve.reciprocal(t1[R], sd[R, :]))
            st.then(TT(f1[R], f1[R], over(t1[R], NB, T, HE), ALU.mult))
            st.then(TT(f1[R], f1[R], by_value(1), ALU.mult))
            st.then(TT(f1[R], f1[R], by_value(2), ALU.add))
            st.then(dve.tensor_reduce(sc[R], f1[R].rearrange("p t (h e) -> p t e h", h=HEADS), AX, ALU.add))
            st.did(TS1(sc[R], sc[R], 1.0 / HEADS, None, ALU.mult))
            st.then(dve.memset(rk[R], 0.0))
            for i in range(4):
                for j in range(i + 1, 4):
                    st.then(TT(t2[R], sc[R, :, i], sc[R, :, j], ALU.is_ge))
                    st.did(TT(rk[R, :, j], rk[R, :, j], t2[R], ALU.add))
                    st.did(TT(rk[R, :, i], rk[R, :, i], t2[R], ALU.subtract))
                    st.settle()
            for i in range(4):
                st.did(TS1(rk[R, :, i], rk[R, :, i], float(3 - i), None, ALU.add))
            st.then(dve.tensor_reduce(t1[R], sc[R], AX, ALU.max))
            TT(gg[R], sc[R], over(t1[R], NB, T, 4), ALU.subtract).then_inc(s_a1, 1)
            dve.wait_ge(s_ow, 4)
            st.then(STT(gg[R], rk[R], 1.5, gg[R], ALU.is_lt, ALU.mult))
            st.then(dve.tensor_reduce(t1[R], gg[R], AX, ALU.add))
            st.then(dve.reciprocal(t1[R], t1[R]))
            st.then(TT(gg[R], gg[R], over(t1[R], NB, T, 4), ALU.mult))
            for g in range(NC):
                for e in range(NEXP):
                    if e == NEXP - 1:
                        dve.wait_ge(s_yl, 2 * g + 2)
                    for b in range(BW):
                        t = g * BW + b
                        ins = STT(x_rows[R, t, :], Y[R, t, e, :], gg[R, t, e:e + 1], x_rows[R, t, :], ALU.mult, ALU.add)
                        if e == NEXP - 1 and b == BW - 1:
                            ins.then_inc(s_fin, 1)
                        else:
                            st.did(ins)
                    if e < NEXP - 1:
                        st.settle()


def kernel(**a):
    import concourse.bacc as _bacc
    from concourse.bass_utils import run_bass_kernel_spmd as _run

    a = {k: np.asarray(v) for k, v in a.items()}
    EP = NCH * CH

    def pad(v, fill):
        return np.concatenate([v, np.full((EP - E1,) + v.shape[1:], fill, v.dtype)])

    src = pad(a["src"], 0).reshape(NCH, P, CT)
    src = np.concatenate([src, src[:AHEAD]])

    arrays = {
        "x": a["x"],
        "src": src,
        "dst": pad(a["dst"], N - 1).reshape(NCH, P, CT),
        "ea54": pad(a["edge_attr_54"], 0).reshape(NCH, P, CT, 54).transpose(0, 3, 2, 1),
        "ea256": pad(a["edge_attr_256"], 0).reshape(NCH, P, CT * C),
        "edges": a["L0_ffn_edge_index"],
        "wf1aT": a["L0_gnn_w_f1a"].T,
        "wf1b": a["L0_gnn_w_f1b"],
        "wlrT": np.stack([a[f"L0_gnn_{k}"].T for k in ("c1_wl", "c1_wr", "c2_wl", "c2_wr")]),
        "lin": np.stack([a["L0_gnn_lin1_w"], a["L0_gnn_lin2_w"]]),
        "catw": a["L0_gnn_cat_w"],
        "vecs": np.concatenate([a[f"L0_{k}"].reshape(2, P) for k in (
            "gnn_c1_bl", "gnn_c2_bl", "gnn_lin1_b", "gnn_lin2_b", "gnn_cat_b", "gnn_gn_w", "gnn_gn_b",
            "gnn_gn_ms", "mix_bq", "mix_bo")]).T,
        "wkv": np.concatenate([a["L0_mix_wk"], a["L0_mix_wv"]], axis=1),
        "bkv": np.concatenate([a["L0_mix_bk"], a["L0_mix_bv"]]),
        "wq": a["L0_mix_wq"], "wo": a["L0_mix_wo"],
        "wgat": a["L0_ffn_W_gat"], "atts": a["L0_ffn_att_src"].reshape(HE), "attd": a["L0_ffn_att_dst"].reshape(HE),
        "bgat": a["L0_ffn_b_gat"], "lng": a["L0_ffn_ln_gamma"], "lnb": a["L0_ffn_ln_beta"],
        "w1": a["L0_ffn_W1"], "b1": a["L0_ffn_b1"].reshape(NEXP * HM, P).T, "w2": a["L0_ffn_W2"], "b2": a["L0_ffn_b2"],
    }
    arrays = {f"in_{k}": np.ascontiguousarray(v) for k, v in arrays.items()}
    nc = _bacc.Bacc("TRN2", target_bir_lowering=False, num_devices=1)
    aps = {k[3:]: nc.dram_tensor(k, v.shape, mybir.dt.from_np(v.dtype), kind="ExternalInput").ap()
           for k, v in arrays.items()}
    out = nc.dram_tensor("out_rows", (N, C), F32, kind="ExternalOutput").ap()
    build(nc, out=out, **aps)
    r = _run(nc, [arrays], core_ids=[0])
    return r.results[0]["out_rows"]
```

```python
from contextlib import ExitStack

import numpy as np
import concourse.bass as bass
from concourse import mybir

ALU = mybir.AluOpType
ACT = mybir.ActivationFunctionType
F32 = mybir.dt.float32
BF16 = mybir.dt.bfloat16
I32 = mybir.dt.int32
F22 = mybir.dt.float32r
AX = mybir.AxisListType.X
RMAX = bass.bass_isa.ReduceOp.max

P = 128
N = 2500
C = 256
NB = 125
T = N // NB
NW = 500
NC = N // NW
BW = NW // NB

E1 = 42500
CT = 7
CH = P * CT
NCH = 48
WIN = 128
NWIN = NCH // 2
DEPTH = 3
KV = 4
IDX = 6
AHEAD = 2
BODY = 12

E2 = 131072
EC = E2 // P
HEADS, NEXP = 4, 4
HE = HEADS * NEXP
TS = HE + HEADS
TD = 2 * HEADS
G = 8
ROUNDS = NC * (NEXP - 1)
DW = 500
DH = N // DW
QT = 18
SAFE = 16.0
SORTS = 4
SORTED = SORTS * (NC - 1)
KCAP = EC + 4 * G
RB = 50
CCOLS = 4 * QT * ROUNDS
HID = 512
HM = HID // P
HALF = NW // 2
MAGIC = 12582912.0
EPS = 1e-5


class Steps:

    def __init__(self, eng, sem):
        self.eng, self.sem, self.base, self.k = eng, sem, 0, 0

    def did(self, ins):
        ins.then_inc(self.sem, 1)
        self.k += 1

    def settle(self):
        self.eng.wait_ge(self.sem, self.base + self.k)

    def then(self, ins):
        self.did(ins)
        self.settle()

    def restart(self, base):
        self.base, self.k = base, 0


def build(nc, x, src, dst, ea54, ea256, edges, wf1aT, wf1b, wlrT, lin, catw, vecs,
          wkv, bkv, wq, wo, wgat, atts, attd, bgat, lng, lnb,
          w1, b1, w2, b2, out):
    with ExitStack() as ctx:
        def sb(name, shape, dt=F32):
            return ctx.enter_context(nc.sbuf_tensor(name, shape, dt))

        def sem(name):
            return ctx.enter_context(nc.semaphore(name))

        psum = ctx.enter_context(nc.psum_tensor("psum", [P, 8, 512], F32))
        bank = [psum[:, i, :] for i in range(8)]

        xn_rows_d = nc.dram_tensor("xn_rows", [N, C], F32).ap()
        source_rows_d = nc.dram_tensor("source_rows", [N, TS], F32).ap()
        dest_rows_d = nc.dram_tensor("dest_rows", [N, TD], F32).ap()
        counts_d = nc.dram_tensor("counts", [RB, RB], F32).ap()
        segment_maxima_d = nc.dram_tensor("segment_maxima", [N, HEADS], F32).ap()

        x_rows = sb("x_rows", [P, T, C])
        xT = sb("xT", [P, 2, N])
        ident = sb("ident", [P, P])
        iota = sb("iota", [P, DW])
        hmask = sb("hmask", [P, P])
        stats = sb("stats", [P, T, 6])
        mv = sb("mv", [P, T, 2])
        sd = sb("sd", [P, T])
        rs = sb("rs", [P, T])
        epsc = sb("epsc", [P, 1])
        tinyc = sb("tinyc", [P, 1])
        onec = sb("onec", [P, 1])
        gstat = sb("gstat", [P, 2, NC, 6])
        gmv = sb("gmv", [P, 2, 2])
        NCOL = 14
        cols = sb("cols", [P, 2 * NCOL])
        b1c = sb("b1c", [P, NEXP * HM])
        fbias = sb("fbias", [P, 4])
        srt = sb("srt", [P, 8])
        small = sb("small", [P, 2 * NWIN])
        ared = sb("ared", [P, 2 * NWIN])
        cellf = sb("cellf", [P, 8])
        celli = sb("celli", [P, 8], I32)
        basei = sb("basei", [1, NWIN], I32)
        basef = sb("basef", [1, NWIN])
        nrel = sb("nrel", [P, NCH, CT])
        nrel_w = nrel[:, :, :].rearrange("p (w s) t -> p w (s t)", s=2)
        srci = sb("srci", [P, IDX, CT], I32)
        shared = sb("shared", [P, KCAP + 2 * CCOLS])
        wlr = shared[:, 0:2048].rearrange("p (w k n) -> p w k n", w=4, k=2)
        linw = shared[:, 2048:3072].rearrange("p (b k n) -> p b k n", b=2, k=2)
        kbuf = shared[:, 0:KCAP]
        cnt_a = shared[:, KCAP:KCAP + CCOLS]
        cnt_b = shared[:, KCAP + CCOLS:KCAP + 2 * CCOLS]
        wsum = [shared[:, 4 * P * i:4 * P * i + 4 * P] for i in range(2)]
        fraw = shared[:, 8 * P:8 * P + 2 * CH]
        feat = [fraw[:, CH * i:CH * i + CH].rearrange("p (t e) -> p t e", t=CT) for i in range(2)]
        parts = sb("parts", [P, 2 * CH], F22)
        upper, lower = (parts[:, CH * i:CH * i + CH].rearrange("p (t e) -> p t e", t=CT) for i in range(2))
        wf = sb("filter_parts", [P, C], F22)
        TU = 2 * DH * TS + DW
        values = [parts[:, TU * i:TU * i + 2 * DH * TS].rearrange("p (k d v) -> p k d v", k=2, d=DH) for i in range(2)]
        digit = [parts[:, TU * i + 2 * DH * TS:TU * i + TU] for i in range(2)]

        LOW = 20608
        low = sb("low", [P, LOW])
        HIGH = 13440
        high = sb("high", [P, HIGH])

        def cut(buf, off, *shape, dt=None):
            n = int(np.prod(shape))
            v = buf[:, off:off + n]
            if dt is not None:
                v = v.bitcast(dt)
                if dt == BF16:
                    shape = shape[:-1] + (shape[-1] * 2,)
            if len(shape) == 1:
                return v
            names = "abcd"[:len(shape)]
            return v.rearrange(f"p ({' '.join(names)}) -> p {' '.join(names)}",
                               **{c: s for c, s in zip(names[1:], shape[1:])})

        HTW = N + WIN
        hT = cut(low, 0, 4, HTW)
        o = 4 * HTW
        mixT = cut(low, o, 2, N); o += 2 * N
        folded = cut(low, o, 4, 2, C); o += 4 * 2 * C
        cat_s = cut(low, o, 4, C); o += 4 * C
        wo_s = cut(low, o, 2, C); o += 2 * C
        wq_s = cut(low, o, 2, C); o += 2 * C
        assert o <= LOW
        rows_n = cut(low, 0, T, C)
        m = T * C
        wkv_s = cut(low, m, 2, 512); m += 1024
        bkv_s = cut(low, m, 512); m += 512
        kraw = cut(low, m, KV, C); m += KV * C
        kexp = cut(low, m, KV, C); m += KV * C
        vrow = cut(low, m, KV, 2, P + 1); m += KV * 2 * (P + 1)
        KVB = m
        kvbd = cut(low, m, 2, 2, P); m += 512
        assert m <= 4 * HTW
        m = 0
        qraw = cut(low, m, 2, NW); m += 2 * NW
        qrel = cut(low, m, 2, NW); m += 2 * NW
        qexp = cut(low, m, 2, NW); m += 2 * NW
        nrm = cut(low, m, 2, NW); m += 2 * NW
        att = cut(low, m, 2, NW); m += 2 * NW
        QB = m
        assert m <= T * C
        Y = cut(low, 0, T, NEXP, C)
        max_table = cut(low, 0, N, HEADS)
        max_table_flat = cut(low, 0, N * HEADS)
        max_reduced = cut(low, N * HEADS, N * HEADS)
        max_candidate = cut(low, N * HEADS, N)
        niota = cut(low, N * HEADS + N, N)
        o = 0
        msgs = [cut(high, o + i * CT * 2 * C, CT, 2 * C) for i in range(DEPTH)]; o += DEPTH * CT * 2 * C
        gath = [m[:, :, 0:C] for m in msgs]
        gate = [m[:, :, C:2 * C] for m in msgs]
        sel = [cut(high, o + i * CT * WIN, CT, WIN) for i in range(2)]; o += 2 * CT * WIN
        wraw, wupper = cut(high, 1024, C), cut(high, 2048, C).bitcast(F22)
        assert o <= HIGH, o
        W1s = [cut(high, i * 2048, 2, HID) for i in range(2)]
        W2s = [cut(high, i * 2048 + 1024, HM, C) for i in range(2)]
        o = 4096
        HT = cut(high, o, 2, N)
        rows2 = cut(high, o, T, C); o += T * C
        L = cut(high, o, 4, NW); o += 4 * NW
        KEYS = HIGH - EC
        assert o <= KEYS
        esrc = cut(high, KEYS, EC, dt=I32); ekey = cut(high, KEYS, EC)
        edst = cut(high, 2048, EC, dt=I32)
        emask = cut(high, 2048 + EC, EC)
        assert o <= HIGH, o
        o = 4096 + T * C
        tab = cut(high, o, T, 24); o += T * 24
        td = cut(high, o, T, TD); o += T * TD
        b2b = cut(high, o, NEXP * C); o += NEXP * C
        key_int = cut(high, o, G, dt=I32); o += G
        dest_int = cut(high, o, G, dt=I32); o += G
        index = cut(high, o, 2, G, dt=I32); o += 2 * G
        nindex = cut(high, o, 2, G, dt=I32); o += 2 * G
        digits = cut(high, o, 2, G); o += 2 * G
        ndigits = cut(high, o, 2, G); o += 2 * G
        lower_digit = cut(high, o, G); o += G
        sources = cut(high, o, G, TS); o += G * TS
        dests = cut(high, o, G, TD); o += G * TD
        got_sources = cut(high, o, G, TS); o += G * TS
        got_dests = cut(high, o, G, TD); o += G * TD
        edge_logit = cut(high, o, G, HEADS); o += G * HEADS
        edge_exp = cut(high, o, G, HEADS); o += G * HEADS
        weighted = cut(high, o, G, TS); o += G * TS
        weighted_parts = cut(high, o, G, 2, TS); o += G * 2 * TS
        upper_digit_hot = cut(high, o, G, DH); o += G * DH
        own_exp = cut(high, o, T, HEADS); o += T * HEADS
        last_exp = cut(high, o, T, HEADS); o += T * HEADS
        last = cut(high, o, 24); o += 24
        bgb = cut(high, o, 3 * HE); o += 3 * HE
        wg = cut(high, o, 2, 24); o += 48
        attb = cut(high, o, 2 * HE); o += 2 * HE
        logit_ends = cut(high, o, 16); o += 16
        logit_ends_all = cut(high, o, 16); o += 16
        GATS = o
        assert GATS <= KEYS
        o = 4096
        ssrc = cut(high, o, EC, dt=I32); o += EC
        sdst = cut(high, o, EC, dt=I32); o += EC
        sidx = cut(high, o, 1, dt=I32); o += 1
        sdf = cut(high, o, 1); o += 1
        srow = cut(high, o, TS); o += TS
        srel = cut(high, o, HEADS); o += HEADS
        segment_max = cut(high, o, T, HEADS); o += T * HEADS
        o = 4096
        hid = [cut(high, o + i * HM * HALF, HM, HALF) for i in range(2)]; o += 2 * HM * HALF
        upper_hot = [cut(high, o + i * QT * RB // 2, QT, RB // 2, dt=BF16) for i in range(2)]; o += QT * RB
        lower_hot = [cut(high, o + i * QT * RB // 2, QT, RB // 2, dt=BF16) for i in range(2)]; o += QT * RB
        assert o <= 4096 + T * C, o
        o = GATS
        zeros = cut(high, o, DW); o += DW
        assert o <= HIGH, o
        o = 0
        agg = cut(high, o, T, TS); o += T * TS
        f1 = cut(high, o, T, HE); o += T * HE
        f2 = cut(high, o, T, HE); o += T * HE
        vsum = cut(high, o, DW); o += DW
        node_counts = cut(high, o, T); o += T
        scores = cut(high, o, T, 4); o += T * 4
        rank = cut(high, o, T, 4); o += T * 4
        gates = cut(high, o, T, 4); o += T * 4
        pair_counts = cut(high, o, 64); o += 64
        t1 = cut(high, o, T); o += T
        t2 = cut(high, o, T); o += T
        assert o <= 2048

        def col(i, mm):
            return cols[:, 2 * i + mm:2 * i + mm + 1]

        (CBL1, CBL2, CLB1, CLB2, CCAT, CGW, CGB, CGM, CBQ, CBO, CMU, CA, CBB, CVAR) = range(NCOL)

        x_loaded = [sem(f"x_loaded{g}") for g in range(NC)]
        weights_loaded = [sem(f"weights_loaded{i}") for i in range(3)]
        constants_made = sem("constants_made")
        pool_steps = sem("pool_steps")
        vector_steps = sem("vector_steps")
        vector_steps_second_half = sem("vector_steps_second_half")
        waits_passed = sem("waits_passed")
        scalar_steps = sem("scalar_steps")
        folds_multiplied = sem("folds_multiplied")
        folds_copied = sem("folds_copied")
        stats_ready = sem("stats_ready")
        deviation_ready = sem("deviation_ready")
        rows_normalised = sem("rows_normalised")
        rows_stored = sem("rows_stored")
        rows_transposed = sem("rows_transposed")
        transposes_copied = sem("transposes_copied")
        kv_multiplied = sem("kv_multiplied")
        kv_taken = sem("kv_taken")
        k_biased = sem("k_biased")
        k_exponent = sem("k_exponent")
        k_feature_ready = sem("k_feature_ready")
        kv_summed = sem("kv_summed")
        kv_masked = sem("kv_masked")
        q_multiplied = sem("q_multiplied")
        q_exponent = sem("q_exponent")
        q_feature_ready = sem("q_feature_ready")
        attention_multiplied = sem("attention_multiplied")
        normaliser_taken = sem("normaliser_taken")
        attention_normalised = sem("attention_normalised")
        mix_multiplied = sem("mix_multiplied")
        mix_taken = sem("mix_taken")
        destinations_loaded = sem("destinations_loaded")
        windows_measured = sem("windows_measured")
        reduced_over_partitions = sem("reduced_over_partitions")
        window_bases_ready = sem("window_bases_ready")
        gate_loaded = [sem(f"gate_loaded{i}") for i in range(DEPTH)]
        indices_loaded = [sem(f"indices_loaded{i}") for i in range(IDX)]
        features_loaded = [sem(f"features_loaded{i}") for i in range(2)]
        sources_gathered = [sem(f"sources_gathered{i}") for i in range(DEPTH)]
        upper_parts_ready = sem("upper_parts_ready")
        features_split = sem("features_split")
        windows_selected = sem("windows_selected")
        filters_multiplied = sem("filters_multiplied")
        filters_taken = sem("filters_taken")
        first_messages_ready = sem("first_messages_ready")
        messages_ready = sem("messages_ready")
        windows_moved = sem("windows_moved")
        messages_summed = sem("messages_summed")
        window_copied = sem("window_copied")
        window_transposed = sem("window_transposed")
        window_added = sem("window_added")
        padding_cleared = sem("padding_cleared")
        second_edges_loaded = sem("second_edges_loaded")
        dense_multiplied = sem("dense_multiplied")
        dense_biased = sem("dense_biased")
        dense_leaky = sem("dense_leaky")
        cat_multiplied = sem("cat_multiplied")
        cat_taken = sem("cat_taken")
        graphnorm_steps = sem("graphnorm_steps")
        graphnorm_root = sem("graphnorm_root")
        graphnorm_applied = sem("graphnorm_applied")
        graphnorm_coefficients = sem("graphnorm_coefficients")
        sum_by_feature_ready = sem("sum_by_feature_ready")
        sum_transposed = sem("sum_transposed")
        sum_rows_ready = sem("sum_rows_ready")
        expert_weights_loaded = [sem(f"expert_weights_loaded{i}") for i in range(2)]
        gat_vectors_loaded = sem("gat_vectors_loaded")
        gat_weights_ready = sem("gat_weights_ready")
        tables_multiplied = sem("tables_multiplied")
        logits_reduced = sem("logits_reduced")
        tables_ready = sem("tables_ready")
        tables_stored = sem("tables_stored")
        span_compared = sem("span_compared")
        slow_edges_loaded = sem("slow_edges_loaded")
        slow_vector_steps = sem("slow_vector_steps")
        slow_sources_ready = sem("slow_sources_ready")
        slow_sources_gathered = sem("slow_sources_gathered")
        slow_maxima_by_partition = sem("slow_maxima_by_partition")
        slow_maxima_reduced = sem("slow_maxima_reduced")
        slow_maxima_stored = sem("slow_maxima_stored")
        slow_maxima_loaded = sem("slow_maxima_loaded")
        last_source_loaded = sem("last_source_loaded")
        round_indices_ready = sem("round_indices_ready")
        round_gathered = sem("round_gathered")
        logits_ready = sem("logits_ready")
        exponents_ready = sem("exponents_ready")
        outer_ready = sem("outer_ready")
        outer_summed = sem("outer_summed")
        counts_ready = sem("counts_ready")
        counts_summed = sem("counts_summed")
        sums_cleared = sem("sums_cleared")
        hidden_multiplied = sem("hidden_multiplied")
        hidden_ready = sem("hidden_ready")
        expert_multiplied = sem("expert_multiplied")
        expert_taken = sem("expert_taken")
        last_expert_taken = sem("last_expert_taken")
        last_expert_biased = sem("last_expert_biased")
        value_sums_copied = sem("value_sums_copied")
        value_sums_transposed = sem("value_sums_transposed")
        counts_copied = sem("counts_copied")
        counts_stored = sem("counts_stored")
        counts_loaded = sem("counts_loaded")
        last_arguments = sem("last_arguments")
        last_functions = sem("last_functions")
        rows_finished = sem("rows_finished")
        output_stored = sem("output_stored")

        x_v = x.rearrange("(t p) c -> p t c", p=NB)
        out_v = out.rearrange("(t p) c -> p t c", p=NB)
        xn_v = xn_rows_d.rearrange("(t p) c -> p t c", p=NB)

        block = ctx.enter_context(nc.Block())

        def over(v, *shape):
            return v.unsqueeze(len(shape) - 1).broadcast_to(shape)

        @block.sync
        def _(sp):
            for g in range(NC):
                sp.dma_start(x_rows[0:NB, BW * g:BW * g + BW, :], x_v[:, BW * g:BW * g + BW, :]).then_inc(x_loaded[g], 16)
            sp.dma_start(nrel[:, :, :].bitcast(I32), dst.rearrange("c p t -> p c t")).then_inc(destinations_loaded, 16)
            sp.dma_start(wkv_s, wkv.rearrange("(k p) n -> p k n", p=P)).then_inc(weights_loaded[0], 16)
            sp.dma_start(bkv_s, bkv.partition_broadcast(P)).then_inc(weights_loaded[0], 16)
            sp.dma_start(cols[:, 0:2 * CMU], vecs).then_inc(weights_loaded[1], 16)
            sp.dma_start(wq_s, wq.rearrange("(k p) n -> p k n", p=P)).then_inc(weights_loaded[1], 16)
            sp.dma_start(wo_s, wo.rearrange("(k p) n -> p k n", p=P)).then_inc(weights_loaded[1], 16)
            sp.dma_start(wlr, wlrT.rearrange("w (k p) n -> p w k n", p=P)).then_inc(weights_loaded[2], 16)
            sp.dma_start(linw, lin.rearrange("b (k p) n -> p b k n", p=P)).then_inc(weights_loaded[2], 16)
            sp.dma_start(high[0:64, 0:54], wf1aT).then_inc(weights_loaded[2], 16)
            sp.dma_start(high[0:64, 64:64 + C], wf1b).then_inc(weights_loaded[2], 16)
            sp.dma_start(cat_s, catw.rearrange("(k p) n -> p k n", p=P)).then_inc(weights_loaded[2], 16)
            sp.dma_start(b1c[:, :], b1).then_inc(weights_loaded[2], 16)
            for g in range(NC):
                sp.wait_ge(rows_normalised, BW * (g + 1))
                sp.dma_start(xn_v[:, BW * g:BW * g + BW, :], rows_n[0:NB, BW * g:BW * g + BW, :]).then_inc(rows_stored, 16)
            sp.wait_ge(window_bases_ready, 1)
            npass = sp.value_load(celli[0:1, 0:1], min_val=1, max_val=N // WIN + 1)
            sp.wait_ge(folds_multiplied, 3)
            sp.wait_ge(padding_cleared, 2)
            for j in range(AHEAD):
                sp.dma_start(srci[:, j, :], src[j]).then_inc(indices_loaded[j], 16)
            with sp.Fori(0, npass) as p:
                with sp.Fori(0, NCH // IDX) as i:
                    for j in range(IDX):
                        q = p * NCH + i * IDX + j
                        c = i * IDX + j
                        sp.wait_ge(features_split, q + 1)
                        for at in (0, 64):
                            sp.dma_start(feat[j % 2][at:at + 54],
                                         ea54[bass.ds(c, 1)].rearrange("o f t p -> (o f) t p")
                                         ).then_inc(features_loaded[j % 2], 16)
                        sp.wait_ge(messages_summed, q + 1)
                        a = (j + AHEAD) % IDX
                        sp.dma_start(srci[:, a, :], src[bass.ds(c + AHEAD, 1)].rearrange("o p t -> (o p) t")
                                     ).then_inc(indices_loaded[a], 16)
                        sp.dma_start(gate[j % DEPTH], ea256[bass.ds(c, 1)].rearrange("o p (t c) -> (o p) t c", t=CT)
                                     ).then_inc(gate_loaded[j % DEPTH], 16)
            sp.wait_ge(messages_summed, npass * NCH + DEPTH)
            sp.dma_start(esrc, edges[0].rearrange("(p c) -> p c", p=P)).then_inc(second_edges_loaded, 16)
            sp.dma_start(edst, edges[1].rearrange("(p c) -> p c", p=P)).then_inc(second_edges_loaded, 16)
            for e in range(2):
                if e == 1:
                    sp.wait_ge(windows_measured, 3)
                sp.dma_start(W1s[e], w1[e].rearrange("(k p) n -> p k n", p=P)).then_inc(expert_weights_loaded[e], 16)
                sp.dma_start(W2s[e], w2[e].rearrange("(k p) n -> p k n", p=P)).then_inc(expert_weights_loaded[e], 16)
            sp.wait_ge(sum_by_feature_ready, NC)
            sp.dma_start(wg[:, :, 0:HE], wgat.rearrange("(k p) n -> p k n", p=P)).then_inc(gat_vectors_loaded, 16)
            sp.dma_start(attb[:, 0:HE], atts.partition_broadcast(P)).then_inc(gat_vectors_loaded, 16)
            sp.dma_start(attb[:, HE:2 * HE], attd.partition_broadcast(P)).then_inc(gat_vectors_loaded, 16)
            for i, v in enumerate((bgat, lng, lnb)):
                sp.dma_start(bgb[:, HE * i:HE * i + HE], v.partition_broadcast(P)).then_inc(gat_vectors_loaded, 16)
            sp.dma_start(b2b, b2.rearrange("e c -> (e c)").partition_broadcast(P)).then_inc(gat_vectors_loaded, 16)
            sp.wait_ge(tables_ready, 1)
            sp.dma_start(source_rows_d.rearrange("(t p) c -> p t c", p=NB), tab[0:NB, :, 0:TS]).then_inc(tables_stored, 16)
            sp.wait_ge(span_compared, 1)
            wide = sp.value_load(celli[0:1, 3:4], min_val=0, max_val=1)
            with sp.If(wide):
                sp.dma_start(ssrc, edges[0].rearrange("(p c) -> p c", p=P)).then_inc(slow_edges_loaded, 16)
                sp.dma_start(sdst, edges[1].rearrange("(p c) -> p c", p=P)).then_inc(slow_edges_loaded, 16)
                sp.wait_ge(slow_maxima_reduced, 1)
                sp.dma_start(segment_maxima_d.rearrange("n h -> (n h)").unsqueeze(0), max_reduced[0:1, :]).then_inc(slow_maxima_stored, 16)
                sp.wait_ge(slow_maxima_stored, 16)
                sp.dma_start(segment_max[0:NB], segment_maxima_d.rearrange("(t p) h -> p t h", p=NB)).then_inc(slow_maxima_loaded, 16)
            sp.wait_ge(tables_ready, 2)
            sp.dma_start(dest_rows_d.rearrange("(t p) c -> p t c", p=NB), td[0:NB]).then_inc(tables_stored, 16)
            sp.wait_ge(tables_stored, 32)
            sp.dma_start(last[:, 0:TS], source_rows_d[N - 1, :].partition_broadcast(P)).then_inc(last_source_loaded, 16)
            for e in range(2, NEXP):
                sp.wait_ge(expert_multiplied, 2 + 2 * NC * (e - 1))
                sp.dma_start(W1s[e % 2], w1[e].rearrange("(k p) n -> p k n", p=P)).then_inc(expert_weights_loaded[e % 2], 16)
                sp.dma_start(W2s[e % 2], w2[e].rearrange("(k p) n -> p k n", p=P)).then_inc(expert_weights_loaded[e % 2], 16)
            sp.wait_ge(counts_copied, 1)
            sp.dma_start(counts_d, pair_counts[0:RB, 0:RB]).then_inc(counts_stored, 16)
            sp.wait_ge(counts_stored, 16)
            sp.dma_start(node_counts[0:NB], counts_d.rearrange("a b -> (a b)").rearrange("(t p) -> p t", p=NB),
                         allow_slow_non_contiguous=True).then_inc(counts_loaded, 16)
            for g in range(NC):
                sp.wait_ge(rows_finished, g + 1)
                sp.dma_start(out_v[:, BW * g:BW * g + BW, :], x_rows[0:NB, BW * g:BW * g + BW, :]).then_inc(output_stored, 16)
            sp.wait_ge(output_stored, 16 * NC)

        @block.gpsimd
        def _(pool):
            pool.memset(ident[:, :], 0.0).then_inc(pool_steps, 1)
            pool.wait_ge(pool_steps, 1)
            pool.affine_select(out=ident[:, :], in_=ident[:, :], compare_op=ALU.not_equal, fill=1.0, base=0,
                               pattern=[[-1, P]], channel_multiplier=1).then_inc(constants_made, 1)
            pool.iota(iota[:, :], pattern=[[1, DW]], base=0, channel_multiplier=0,
                      allow_small_or_imprecise_dtypes=True).then_inc(constants_made, 1)
            pool.wait_ge(windows_measured, 1)
            pool.partition_all_reduce(ared[:, :], small[:, :], P, RMAX).then_inc(reduced_over_partitions, 1)
            pool.wait_ge(rows_stored, 16 * NC)
            pool.wait_ge(window_bases_ready, 1)
            npass = pool.value_load(celli[0:1, 0:1], min_val=1, max_val=N // WIN + 1)
            with pool.Fori(0, npass) as p:
                with pool.Fori(0, NCH // IDX) as i:
                    for j in range(IDX):
                        pool.wait_ge(indices_loaded[j], (p * (NCH // IDX) + i) * 16 + 16)
                        pool.wait_ge(messages_summed, p * NCH + i * IDX + (j + 1))
                        pool.sem_inc(waits_passed, 1)
                        for t in range(CT):
                            pool.indirect_dma_start(
                                gath[j % DEPTH][:, t, :], None, xn_rows_d,
                                bass.IndirectOffsetOnAxis(ap=srci[:, j, t:t + 1], axis=0)
                            ).then_inc(sources_gathered[j % DEPTH], 16)
            pool.wait_ge(windows_measured, 2)
            pool.partition_all_reduce(ared[:, 0:1], small[:, 0:1], P, RMAX).then_inc(reduced_over_partitions, 1)
            pool.wait_ge(logits_reduced, 1)
            pool.partition_all_reduce(logit_ends_all[:, 0:8], logit_ends[:, 0:8], P, RMAX).then_inc(reduced_over_partitions, 1)
            pool.wait_ge(span_compared, 1)
            wide = pool.value_load(celli[0:1, 3:4], min_val=0, max_val=1)
            with pool.If(wide):
                pool.wait_ge(tables_stored, 16)
                with pool.Fori(0, EC) as c:
                    pool.wait_ge(slow_sources_ready, c + 1)
                    pool.sem_inc(waits_passed, 1)
                    pool.indirect_dma_start(srow, None, source_rows_d,
                                            bass.IndirectOffsetOnAxis(ap=sidx, axis=0)).then_inc(slow_sources_gathered, 16)
                pool.wait_ge(slow_maxima_by_partition, 1)
                pool.partition_all_reduce(max_reduced, max_table_flat, P, RMAX).then_inc(slow_maxima_reduced, 1)
            pool.wait_ge(tables_stored, 32)
            rem = pool.value_load(celli[0:1, 2:3], min_val=1, max_val=(EC - G * ROUNDS) // G + 1)

            def gathers(r):
                pool.wait_ge(round_indices_ready, r + 1)
                pool.sem_inc(waits_passed, 1)
                for t in range(G):
                    pool.indirect_dma_start(got_sources[:, t, :], None, source_rows_d,
                                            bass.IndirectOffsetOnAxis(ap=index[:, 0, t:t + 1], axis=0)).then_inc(round_gathered, 16)
                    pool.indirect_dma_start(got_dests[:, t, :], None, dest_rows_d,
                                            bass.IndirectOffsetOnAxis(ap=index[:, 1, t:t + 1], axis=0)).then_inc(round_gathered, 16)

            with pool.Fori(0, ROUNDS) as r:
                gathers(r)
            with pool.Fori(0, rem) as r:
                gathers(r + ROUNDS)
            with pool.Fori(0, NC) as n:
                for h in range(2):
                    pool.wait_ge(last_expert_taken, n * 2 + (h + 1))
                    v = Y[0:NB, bass.ds(n * BW + 2 * h, 2), NEXP - 1, :]
                    pool.tensor_tensor(v, v, b2b[0:NB, C * (NEXP - 1):].unsqueeze(1).broadcast_to((NB, 2, C)),
                                       ALU.add).then_inc(last_expert_biased, 1)

        @block.tensor
        def _(pe):
            pe.wait_ge(constants_made, 1)

            def turn_rows(rows, g, ready, used, banks):
                pe.wait_ge(rows_normalised, ready + BW * (g + 1))
                for k in range(2):
                    u = used + 2 * g + k
                    if 2 * g + k >= len(banks):
                        pe.wait_ge(transposes_copied, u - len(banks) + 1)
                    for b in range(BW):
                        ins = pe.transpose(banks[(2 * g + k) % len(banks)][:, NB * b:NB * b + NB],
                                           rows[0:NB, BW * g + b, P * k:P * k + P], ident[0:NB, 0:NB])
                    ins.then_inc(rows_transposed, 1)

            for g in range(NC):
                turn_rows(rows_n, g, 0, 0, bank[0:4])
            pe.wait_ge(weights_loaded[0], 16 * 2)

            def kv_sum(t):
                pe.wait_ge(k_feature_ready, t + 1)
                for c in range(2):
                    ins = pe.matmul(bank[6 + c][:, 0:P + 1], kexp[0:NB, t % KV, P * c:P * c + P],
                                    vrow[0:NB, t % KV, c, :], start=(t == 0), stop=(t == T - 1))
                ins.then_inc(kv_summed, 1)

            for t in range(T):
                pe.wait_ge(transposes_copied, 2 * NC if t >= 2 else 2)
                if t >= KV:
                    pe.wait_ge(kv_taken, t - KV + 1)
                for k in range(2):
                    ins = pe.matmul(bank[(4, 5, 2, 3)[t % KV]][0:NB, :], xT[:, k, NB * t:NB * t + NB], wkv_s[:, k, :],
                                    start=(k == 0), stop=(k == 1))
                ins.then_inc(kv_multiplied, 1)
                if t >= 2:
                    kv_sum(t - 2)
            kv_sum(T - 2)
            kv_sum(T - 1)
            pe.wait_ge(weights_loaded[1], 16 * 3)
            pe.wait_ge(weights_loaded[2], 16 * 6)
            pe.wait_ge(kv_taken, T)
            pe.matmul(bank[0][0:54, 0:C], high[0:64, 0:54], high[0:64, 64:64 + C],
                      start=True, stop=True).then_inc(folds_multiplied, 1)
            for w in range(4):
                for mm in range(2):
                    for k in range(2):
                        ins = pe.matmul(bank[1 + w][:, C * mm:C * mm + C], wlr[:, w, k, P * mm:P * mm + P],
                                        linw[:, w // 2, k, :], start=(k == 0), stop=(k == 1))
            ins.then_inc(folds_multiplied, 1)
            for b in range(2):
                for mm in range(2):
                    for k in range(2):
                        ins = pe.matmul(bank[5][:, 2 * b + mm:2 * b + mm + 1], linw[:, b, k, P * mm:P * mm + P],
                                        col(CBL1 + b, k), start=(k == 0), stop=(k == 1))
            ins.then_inc(folds_multiplied, 1)
            pe.wait_ge(folds_copied, 3)

            def queries(n):
                for c in range(2):
                    for k in range(2):
                        ins = pe.matmul(bank[c][:, 0:NW], wq_s[:, k, P * c:P * c + P], xT[:, k, bass.ds(n * NW, NW)],
                                        start=(k == 0), stop=(k == 1))
                    ins.then_inc(q_multiplied, 1)

            def attend(n):
                for c in range(2):
                    pe.wait_ge(q_feature_ready, n * 2 + (c + 1))
                    pe.wait_ge(attention_normalised, n * 2 + (c + 1))
                    pe.matmul(bank[2 + 2 * c][:, 0:NW], kvbd[:, c, 0, :], qraw[:, c, :], start=True, stop=True)
                    pe.matmul(bank[3 + 2 * c][:, 0:NW], kvbd[:, c, 1, :], qraw[:, c, :],
                              start=True, stop=True).then_inc(attention_multiplied, 1)

            def mix(n):
                pe.wait_ge(attention_normalised, n * 2 + 4)
                pe.wait_ge(mix_taken, n * 2 + 2)
                for mm in range(2):
                    for k in range(2):
                        ins = pe.matmul(bank[6 + mm][:, 0:NW], wo_s[:, k, P * mm:P * mm + P], att[:, k, :],
                                        start=(k == 0), stop=(k == 1))
                    ins.then_inc(mix_multiplied, 1)

            queries(0)
            pe.wait_ge(kv_masked, 1)
            with pe.Fori(0, NC - 1) as n:
                attend(n)
                queries(n + 1)
                mix(n)
            attend(NC - 1)
            mix(NC - 1)
            pe.wait_ge(mix_taken, 2 * NC + 2)

            pe.wait_ge(window_bases_ready, 1)
            npass = pe.value_load(celli[0:1, 0:1], min_val=1, max_val=N // WIN + 1)

            def filters(q, j):
                pe.wait_ge(features_split, q + 3)
                for h, tiles in enumerate((range(0, 4), range(4, CT))):
                    pe.wait_ge(filters_taken, q * 2 + (h + 1))
                    for t in tiles:
                        for k, part in enumerate((upper, lower)):
                            ins = pe.matmul(bank[2 + t // 2][:, C * (t % 2):C * (t % 2) + C],
                                            part[:, t, :], wf[:, :],
                                            start=(k == 0), stop=(k == 1))
                    ins.then_inc(filters_multiplied, 1)

            def sums(q, j):
                w = j // 2
                if j % 2 == 0:
                    pe.wait_ge(window_copied, (q >> 1) + 1)
                pe.wait_ge(windows_selected, q + 1)
                for h, tiles in enumerate((range(0, 4), range(4, CT))):
                    pe.wait_ge(messages_ready, q * 2 + (h + 1))
                    for t in tiles:
                        ins = pe.matmul(bank[w % 2], sel[j % 2][:, t, :], msgs[j % DEPTH][:, t, :],
                                        start=(j % 2 == 0 and t == 0), stop=(j % 2 == 1 and t == CT - 1),
                                        skip_group_check=True)
                ins.then_inc(messages_summed, 1)

            def turn_window(v, w):
                pe.wait_ge(window_copied, v + 3)
                pe.wait_ge(window_added, v + 1)
                for f in range(4):
                    ins = pe.transpose(bank[6 + w % 2][:, P * f:P * f + P], wsum[w % 2][:, P * f:P * f + P],
                                       ident[:, :])
                ins.then_inc(window_transposed, 1)

            with pe.Fori(0, npass) as p:
                for j in range(2):
                    filters(p * NCH + j, j)
                with pe.Fori(0, NCH // BODY - 1) as i:
                    for j in range(BODY):
                        sums(p * NCH + i * BODY + j, j)
                        filters(p * NCH + i * BODY + (j + 2), j)
                        if j % 2:
                            turn_window(p * NWIN + i * (BODY // 2) + j // 2, j // 2)
                for j in range(BODY):
                    c = NCH - BODY + j
                    sums(p * NCH + c, j)
                    if c + 2 < NCH:
                        filters(p * NCH + (c + 2), j)
                    if j % 2:
                        turn_window(p * NWIN + c // 2, j // 2)

            with pe.Fori(0, NC) as n:
                for u in range(4):
                    pe.wait_ge(dense_biased, n * 4 + (u + 1))
                    for k in range(2):
                        pe.matmul(bank[u][:, 0:NW], folded[:, u - u % 2 + 1, k, P * (u % 2):P * (u % 2) + P],
                                  xT[:, k, bass.ds(n * NW, NW)], start=(k == 0), stop=False)
                pe.wait_ge(window_added, npass * NWIN + 2)
                pe.sem_inc(waits_passed, 1)
                for u in range(4):
                    for k in range(2):
                        ins = pe.matmul(bank[u][:, 0:NW], folded[:, u - u % 2, k, P * (u % 2):P * (u % 2) + P],
                                        hT[:, u - u % 2 + k, bass.ds(n * NW, NW)], start=False, stop=(k == 1))
                    ins.then_inc(dense_multiplied, 1)
                pe.wait_ge(cat_taken, n * 2 + 2)
                for k in range(4):
                    pe.wait_ge(dense_leaky, n * 4 + (k + 1))
                    for mm in range(2):
                        ins = pe.matmul(bank[4 + mm][:, 0:NW], cat_s[:, k, P * mm:P * mm + P], L[:, k, :],
                                        start=(k == 0), stop=(k == 3))
                        if k == 3:
                            ins.then_inc(cat_multiplied, 1)
            def turn_back(g):
                pe.wait_ge(sum_by_feature_ready, g + 1)
                for t in range(BW * g, BW * g + BW):
                    if t >= 4:
                        pe.wait_ge(sum_rows_ready, t - 3)
                    for k in range(2):
                        ins = pe.transpose(bank[t % 4][0:NB, P * k:P * k + P], mixT[:, k, NB * t:NB * t + NB],
                                           ident[:, :])
                    ins.then_inc(sum_transposed, 1)

            def table(g):
                pe.wait_ge(transposes_copied, 2 * NC + 2 * g + 2)
                for t in range(BW * g, BW * g + BW):
                    for k in range(2):
                        ins = pe.matmul(bank[4][0:NB, 24 * t:24 * t + 24], xT[:, k, NB * t:NB * t + NB], wg[:, k, :],
                                        start=(k == 0), stop=(k == 1))
                return ins

            pe.wait_ge(cat_taken, 2 * NC + 2)
            turn_back(0)
            turn_back(1)
            for g in range(1, NC + 1):
                if g + 1 < NC:
                    turn_back(g + 1)
                turn_rows(rows2, g - 1, T, 2 * NC, bank[5:8])
                if g == 2:
                    pe.wait_ge(gat_weights_ready, 1)
                if g >= 2:
                    table(g - 2)
            table(NC - 1).then_inc(tables_multiplied, 1)
            pe.wait_ge(sums_cleared, 1)
            pe.matmul(bank[6][0:DH * TS, 0:DW], zeros[:, 0:DH * TS], zeros, start=True, stop=True,
                      skip_group_check=True)
            pe.matmul(bank[7][0:RB, 0:RB], zeros[:, 0:RB], zeros[:, 0:RB], start=True, stop=True,
                      skip_group_check=True)

            def tile_sums(r, i):
                pe.wait_ge(outer_ready, r * G + (i + 1))
                for k in range(2):
                    ins = pe.matmul(bank[6][0:DH * TS, 0:DW], values[i % 2][:, k].rearrange("p d v -> p (d v)"),
                                    digit[i % 2], start=False, stop=True, skip_group_check=True)
                ins.then_inc(outer_summed, 1)

            def quarter(r, k):
                pe.wait_ge(counts_ready, r * 4 + (k + 1))
                for t in range(QT):
                    ins = pe.matmul(bank[7][0:RB, 0:RB], upper_hot[k % 2][:, t, :], lower_hot[k % 2][:, t, :],
                                    start=False, stop=True, skip_group_check=True)
                ins.then_inc(counts_summed, 1)
                tile_sums(r, 2 * k)
                tile_sums(r, 2 * k + 1)

            def hidden(e, n, r, h):
                for mm in range(HM):
                    pe.wait_ge(hidden_ready, r * 8 + (h * 4 + mm + 1))
                    for k in range(2):
                        ins = pe.matmul(bank[mm][:, 0:HALF],
                                        W1s[e % 2][:, k, P * mm:P * mm + P],
                                        xT[:, k, bass.ds(n * NW + h * HALF, HALF)],
                                        start=(k == 0), stop=(k == 1))
                    ins.then_inc(hidden_multiplied, 1)

            def results(e, r, h):
                pe.wait_ge(hidden_ready, r * 8 + (h * 4 + 8))
                for b in range(2):
                    for k in range(HM):
                        ins = pe.matmul(bank[4 + h][0:NB, C * b:C * b + C], hid[h][:, k, NB * b:NB * b + NB],
                                        W2s[e % 2][:, k, :], start=(k == 0), stop=(k == HM - 1))
                ins.then_inc(expert_multiplied, 1)

            def step(e, n, with_round=True):
                r = n + e * NC
                for h in range(2):
                    hidden(e, n, r, h)
                if with_round:
                    quarter(r - 1, 0)
                for h in range(2):
                    pe.wait_ge(expert_taken, r * 2 + (h + 1))
                    results(e, r, h)
                    if with_round and h == 0:
                        quarter(r - 1, 1)
                        quarter(r - 1, 2)
                if with_round:
                    quarter(r - 1, 3)

            for e in range(NEXP - 1):
                pe.wait_ge(expert_weights_loaded[e % 2], 32 * (e // 2 + 1))
                if e == 0:
                    step(0, 0, False)
                with pe.Fori(0 if e else 1, NC) as n:
                    step(e, n)
            e = NEXP - 1
            pe.wait_ge(expert_weights_loaded[e % 2], 32 * (e // 2 + 1))
            step(e, 0)
            pe.wait_ge(tables_ready, 2)
            rem = pe.value_load(celli[0:1, 2:3], min_val=1, max_val=(EC - G * ROUNDS) // G + 1)
            with pe.Fori(0, rem) as i:
                for t in range(G):
                    tile_sums(i + ROUNDS, t)
            pe.wait_ge(value_sums_copied, 1)
            for b in range(BW):
                ins = pe.transpose(bank[7][0:NB, DH * TS * b:DH * TS * b + DH * TS],
                                   vsum[0:DH * TS, NB * b:NB * b + NB], ident[0:DH * TS, 0:DH * TS])
            ins.then_inc(value_sums_transposed, 1)
            with pe.Fori(1, NC) as n:
                for h in range(2):
                    hidden(e, n, n + ROUNDS, h)
                for h in range(2):
                    pe.wait_ge(last_expert_taken, n * 2 + (h - 1))
                    results(e, n + ROUNDS, h)

        @block.scalar
        def _(act):
            act.sem_inc(filters_taken, 2)
            act.sem_inc(filters_multiplied, 2)
            act.sem_inc(features_split, 2)
            act.sem_inc(messages_summed, DEPTH)
            act.sem_inc(window_copied, 2)
            act.sem_inc(window_added, 2)
            act.sem_inc(window_transposed, 2)
            act.sem_inc(outer_summed, 2)
            act.sem_inc(counts_summed, 2)
            act.sem_inc(expert_taken, 2)
            act.sem_inc(expert_multiplied, 2)
            act.sem_inc(hidden_ready, 4)
            act.sem_inc(dense_biased, 4)
            act.sem_inc(cat_taken, 2)
            act.sem_inc(cat_multiplied, 2)
            act.sem_inc(windows_moved, 1)
            act.sem_inc(attention_normalised, 2)
            act.sem_inc(mix_taken, 2)
            act.sem_inc(normaliser_taken, 2)

            def deviation(k, g):
                b = slice(BW * g, BW * g + BW)
                act.wait_ge(stats_ready, NC * k + g + 1)
                act.activation(sd[0:NB, b], mv[0:NB, b, 1], ACT.Sqrt, bias=epsc[0:NB, :]).then_inc(deviation_ready, 1)

            def turned(g, used, banks):
                for k in range(2):
                    act.wait_ge(rows_transposed, used + 2 * g + k + 1)
                    act.copy(xT[:, k, NW * g:NW * g + NW],
                             banks[(2 * g + k) % len(banks)][:, 0:NW]).then_inc(transposes_copied, 1)

            deviation(0, 0)
            for g in range(NC):
                if g + 1 < NC:
                    deviation(0, g + 1)
                turned(g, 0, bank[0:4])
            for t in range(T):
                act.wait_ge(k_biased, t + 1)
                act.activation(kexp[0:NB, t % KV, :], kraw[0:NB, t % KV, :], ACT.Exp)
                act.activation(kraw[0:NB, t % KV, :], kraw[0:NB, t % KV, :], ACT.Relu).then_inc(k_exponent, 1)
            act.wait_ge(folds_multiplied, 1)
            act.wait_ge(padding_cleared, 1)
            act.copy(wraw[0:54, :], bank[0][0:54, 0:C])
            act.copy(wraw[64:118, :], bank[0][0:54, 0:C]).then_inc(folds_copied, 1)
            act.wait_ge(folds_multiplied, 3)
            for w in range(4):
                ins = act.copy(folded[:, w, :, :].rearrange("p a b -> p (a b)"), bank[1 + w])
            ins.then_inc(folds_copied, 1)
            act.wait_ge(rows_stored, 16 * NC)

            def query_parts(n):
                for c in range(2):
                    act.wait_ge(q_multiplied, n * 2 + (c + 1))
                    act.wait_ge(q_feature_ready, n * 2 + c)
                    act.activation(qexp[:, c, :], bank[c][:, 0:NW], ACT.Exp, bias=col(CBQ, c))
                    act.activation(qrel[:, c, :], bank[c][:, 0:NW], ACT.Relu, bias=col(CBQ, c)).then_inc(q_exponent, 1)

            def normaliser(n):
                for c in range(2):
                    act.wait_ge(attention_multiplied, n * 2 + (c + 1))
                    act.wait_ge(attention_normalised, n * 2 + (c + 1))
                    act.activation(nrm[:, c, :], bank[3 + 2 * c][:, 0:NW], ACT.Identity,
                                   bias=tinyc[:, :]).then_inc(normaliser_taken, 1)

            def mixed(n):
                for mm in range(2):
                    act.wait_ge(mix_multiplied, n * 2 + (mm + 1))
                    act.activation(mixT[:, mm, bass.ds(n * NW, NW)], bank[6 + mm][:, 0:NW], ACT.Identity,
                                   bias=col(CBO, mm)).then_inc(mix_taken, 1)

            for c in range(2):
                act.wait_ge(q_multiplied, c + 1)
                act.activation(qexp[:, c, :], bank[c][:, 0:NW], ACT.Exp, bias=col(CBQ, c))
                act.activation(qrel[:, c, :], bank[c][:, 0:NW], ACT.Relu, bias=col(CBQ, c)).then_inc(q_exponent, 1)
            with act.Fori(0, NC - 1) as n:
                normaliser(n)
                query_parts(n + 1)
                mixed(n)
            normaliser(NC - 1)
            mixed(NC - 1)
            act.wait_ge(window_bases_ready, 1)
            npass = act.value_load(celli[0:1, 0:1], min_val=1, max_val=N // WIN + 1)

            def select(p, c, j):
                q = p * NCH + c
                act.wait_ge(messages_summed, q + 2)
                for t in range(CT):
                    ins = act.activation(sel[j][:, t, :], iota[:, 0:WIN], ACT.Abs,
                                         bias=nrel[:, bass.ds(c, 1), t:t + 1].rearrange("p o t -> p (o t)"))
                ins.then_inc(scalar_steps, 1)
                act.wait_ge(scalar_steps, q + 1)
                act.activation(sel[j], sel[j], ACT.Relu, bias=onec[:, :], scale=-1.0).then_inc(windows_selected, 1)

            def upper_parts(p, w, b):
                q = p * NCH + w * 2 + b
                act.wait_ge(features_loaded[b], (p * NWIN + w) * 32 + 32)
                act.wait_ge(filters_multiplied, q * 2 + 2)
                act.wait_ge(features_split, q + 2)
                act.copy(upper, feat[b]).then_inc(upper_parts_ready, 1)

            def copy_window(p, w, b):
                act.wait_ge(messages_summed, p * NCH + w * 2 + (2 + DEPTH))
                act.wait_ge(window_transposed, p * NWIN + w + 1)
                act.copy(wsum[b], bank[b]).then_inc(window_copied, 1)

            with act.Fori(0, npass) as p:
                act.wait_ge(windows_moved, p + 1)
                upper_parts(p, 0, 0)
                select(p, 0, 0)
                upper_parts(p, 0, 1)
                select(p, 1, 1)
                upper_parts(p, 1, 0)
                with act.Fori(0, NWIN // 2 - 1) as i:
                    for b in range(2):
                        w = i * 2 + b
                        select(p, w * 2 + 2, 0)
                        upper_parts(p, w + 1, 1)
                        copy_window(p, w, b)
                        select(p, w * 2 + 3, 1)
                        upper_parts(p, w + 2, 0)
                select(p, NCH - 2, 0)
                upper_parts(p, NWIN - 1, 1)
                copy_window(p, NWIN - 2, 0)
                select(p, NCH - 1, 1)
                copy_window(p, NWIN - 1, 1)
            act.wait_ge(messages_summed, npass * NCH + DEPTH)
            with act.Fori(0, NC) as n:
                act.wait_ge(cat_multiplied, n * 2 + 2)
                for u in range(4):
                    act.wait_ge(dense_multiplied, n * 4 + (u + 1))
                    act.activation(L[:, u, :], bank[u][:, 0:NW], ACT.Identity,
                                   bias=fbias[:, u:u + 1]).then_inc(dense_biased, 1)
                for mm in range(2):
                    act.wait_ge(cat_multiplied, n * 2 + (mm + 3))
                    act.activation(HT[:, mm, bass.ds(n * NW, NW)], bank[4 + mm][:, 0:NW], ACT.Identity,
                                   bias=col(CCAT, mm)).then_inc(cat_taken, 1)
            act.wait_ge(graphnorm_steps, 1)
            act.activation(cols[:, 2 * CVAR:2 * CVAR + 2], cols[:, 2 * CVAR:2 * CVAR + 2], ACT.Sqrt,
                           bias=epsc[:, :]).then_inc(graphnorm_root, 1)
            act.wait_ge(graphnorm_coefficients, 1)
            for g in range(NC):
                for mm in range(2):
                    v = HT[:, mm, NW * g:NW * g + NW]
                    ins = act.activation(v, v, ACT.Identity, bias=col(CBB, mm), scale=col(CA, mm))
                ins.then_inc(graphnorm_applied, 1)
            deviation(1, 0)
            for g in range(NC):
                if g + 1 < NC:
                    deviation(1, g + 1)
                turned(g, 2 * NC, bank[5:8])

            def exponents(r):
                act.wait_ge(logits_ready, r + 1)
                act.activation(edge_exp, edge_logit, ACT.Exp).then_inc(exponents_ready, 1)

            def gelus(e, r, h):
                act.wait_ge(expert_multiplied, r * 2 + (h + 1))
                for mm in range(HM):
                    act.wait_ge(hidden_multiplied, r * 8 + (h * 4 + mm + 1))
                    act.activation(hid[h][:, mm, :], bank[mm][:, 0:HALF],
                                   ACT.Gelu, bias=b1c[:, e * HM + mm:e * HM + mm + 1]).then_inc(hidden_ready, 1)

            act.wait_ge(last_arguments, 1)
            act.activation(own_exp[0:NB], own_exp[0:NB], ACT.Exp).then_inc(last_functions, 1)
            act.activation(last_exp[0:NB], last_exp[0:NB], ACT.Exp).then_inc(last_functions, 1)
            for e in range(NEXP - 1):
                with act.Fori(0, NC) as n:
                    for h in range(2):
                        gelus(e, n + e * NC, h)
                    exponents(n + e * NC)

            def last_gelus(n):
                for h in range(2):
                    gelus(NEXP - 1, ROUNDS + n, h)

            def last_results(n):
                for h in range(2):
                    act.wait_ge(expert_multiplied, 2 * (ROUNDS + n) + h + 3)
                    act.copy(Y[0:NB, n * BW + 2 * h:n * BW + 2 * h + 2, NEXP - 1, :],
                             bank[4 + h][0:NB, :].rearrange("p (b c) -> p b c", b=2)).then_inc(last_expert_taken, 1)

            last_gelus(0)
            last_results(0)
            exponents(ROUNDS)
            act.wait_ge(tables_ready, 2)
            rem = act.value_load(celli[0:1, 2:3], min_val=1, max_val=(EC - G * ROUNDS) // G + 1)
            with act.If(rem - 1):
                with act.Fori(1, rem) as r:
                    exponents(r + ROUNDS)
            act.wait_ge(outer_summed, rem * G + (G * ROUNDS + 2))
            act.copy(vsum[0:DH * TS, :], bank[6][0:DH * TS, 0:DW]).then_inc(value_sums_copied, 1)
            last_gelus(1)
            act.wait_ge(last_arguments, 2)
            act.activation(sd[0:NB, :], scores[0:NB, :, 0], ACT.Sqrt, bias=epsc[0:NB, :]).then_inc(last_functions, 1)
            last_results(1)
            last_gelus(2)
            act.wait_ge(last_arguments, 3)
            act.activation(gates[0:NB], gates[0:NB], ACT.Exp).then_inc(last_functions, 1)
            last_results(2)
            for n in range(3, NC):
                last_gelus(n)
                last_results(n)

        @block.vector
        def _(dve):
            st = Steps(dve, vector_steps)
            TT, TS1, STT = dve.tensor_tensor, dve.tensor_scalar, dve.scalar_tensor_tensor
            st.did(dve.memset(epsc[:, :], EPS))
            st.did(dve.memset(tinyc[:, :], 1e-6))
            st.did(dve.memset(onec[:, :], 1.0))
            st.did(dve.memset(hmask[:, :], 0.0))
            st.did(dve.memset(vrow[:, :, :, P:P + 1], 1.0))
            st.settle()
            for g in range(4):
                st.did(dve.memset(hmask[32 * g:32 * g + 32, 32 * g:32 * g + 32], 1.0))

            st.then(dve.memset(wraw, 0.0))
            dve.sem_inc(padding_cleared, 1)

            dve.wait_ge(destinations_loaded, 16)
            st.then(dve.tensor_copy(nrel[:, :, :], nrel[:, :, :].bitcast(I32)))
            st.did(dve.tensor_reduce(small[:, 0:NWIN], nrel_w, AX, ALU.min))
            dve.tensor_reduce(small[:, NWIN:2 * NWIN], nrel_w, AX, ALU.max)
            st.settle()
            dve.tensor_scalar(small[:, 0:NWIN], small[:, 0:NWIN], -1.0, None, ALU.mult).then_inc(windows_measured, 1)

            def measure(rows, g):
                for t in range(BW * g, BW * g + BW):
                    st.did(dve.bn_stats(stats[0:NB, t, :], rows[0:NB, t, :]))
                st.settle()
                for t in range(BW * g, BW * g + BW):
                    ins = dve.bn_aggr(mv[0:NB, t, :], stats[0:NB, t, :])
                ins.then_inc(stats_ready, 1)

            def normalise(rows, out_rows, k, g):
                b = slice(BW * g, BW * g + BW)
                dve.wait_ge(deviation_ready, NC * k + g + 1)
                st.then(dve.reciprocal(rs[0:NB, b], sd[0:NB, b]))
                for t in range(BW * g, BW * g + BW):
                    TS1(out_rows[0:NB, t, :], rows[0:NB, t, :], mv[0:NB, t, 0:1], rs[0:NB, t:t + 1],
                        ALU.subtract, ALU.mult).then_inc(rows_normalised, 1)

            for g in range(NC):
                dve.wait_ge(x_loaded[g], 16)
                measure(x_rows, g)
                if g:
                    normalise(x_rows, rows_n, 0, g - 1)
            normalise(x_rows, rows_n, 0, NC - 1)
            dve.wait_ge(reduced_over_partitions, 1)
            st.did(TT(nrel_w, nrel_w, over(ared[:, 0:NWIN], P, NWIN, 2 * CT), ALU.add))
            st.then(TT(small[:, 0:NWIN], ared[:, NWIN:2 * NWIN], ared[:, 0:NWIN], ALU.add))
            st.then(dve.tensor_reduce(cellf[:, 0:1], small[:, 0:NWIN], AX, ALU.max))
            st.then(dve.tensor_copy(celli[:, 0:1], cellf[:, 0:1]))
            st.then(TS1(celli[:, 1:2], celli[:, 0:1], WIN.bit_length() - 1, None, ALU.arith_shift_right))
            st.did(TS1(celli[:, 0:1], celli[:, 1:2], 1.0, None, ALU.add))
            st.did(TS1(nrel[:, :, :], nrel[:, :, :], -1.0, None, ALU.mult))
            st.did(TS1(basef[:, :], ared[0:1, 0:NWIN], -1.0, None, ALU.mult))
            st.settle()
            dve.tensor_copy(basei[:, :], basef[:, :]).then_inc(window_bases_ready, 1)

            dve.wait_ge(weights_loaded[0], 16 * 2)

            def key_map(t):
                dve.wait_ge(k_exponent, t + 1)
                STT(kexp[0:NB, t % KV, :], kexp[0:NB, t % KV, :], 1.0, kraw[0:NB, t % KV, :],
                    ALU.min, ALU.add).then_inc(k_feature_ready, 1)

            for t in range(T):
                dve.wait_ge(kv_multiplied, t + 1)
                if t >= KV:
                    dve.wait_ge(kv_summed, t - KV + 1)
                i = (4, 5, 2, 3)[t % KV]
                TT(kraw[0:NB, t % KV, :], bank[i][0:NB, 0:C], bkv_s[0:NB, 0:C], ALU.add).then_inc(k_biased, 1)
                TT(vrow[0:NB, t % KV, :, 0:P], bank[i][0:NB, C:2 * C].rearrange("p (c n) -> p c n", c=2),
                   bkv_s[0:NB, C:2 * C].rearrange("p (c n) -> p c n", c=2), ALU.add).then_inc(kv_taken, 1)
                if t >= 1:
                    key_map(t - 1)
            key_map(T - 1)
            dve.wait_ge(kv_summed, T)
            st.settle()
            for c in range(2):
                st.did(TT(kvbd[:, c, 0, :], bank[6 + c][:, 0:P], hmask[:, :], ALU.mult))
                ins = TS1(kvbd[:, c, 1, :], hmask[:, :], bank[6 + c][:, P:P + 1], None, ALU.mult)
            ins.then_inc(kv_masked, 1)
            dve.wait_ge(folds_copied, 1)
            st.did(dve.tensor_copy(wf[0:64, :], wraw[0:64, :]))
            st.then(dve.tensor_copy(wupper[64:P, :], wraw[64:P, :]))
            st.then(TT(wf[64:P, :], wraw[64:P, :], wupper[64:P, :].bitcast(F32), ALU.subtract))
            dve.wait_ge(folds_multiplied, 3)
            dve.memset(fraw, 0.0).then_inc(padding_cleared, 1)
            TT(fbias[:, :], bank[5][:, 0:4], cols[:, 2 * CLB1:2 * CLB1 + 4], ALU.add).then_inc(folds_copied, 1)
            dve.wait_ge(rows_stored, 16 * NC)
            v0 = st.k

            def query_map(n):
                for c in range(2):
                    dve.wait_ge(q_exponent, n * 2 + (c + 1))
                    STT(qraw[:, c, :], qexp[:, c, :], 1.0, qrel[:, c, :], ALU.min, ALU.add).then_inc(q_feature_ready, 1)

            def normalised(n):
                st.restart(n * 2 + v0)
                for c in range(2):
                    dve.wait_ge(normaliser_taken, n * 2 + (c + 3))
                    st.then(dve.reciprocal(nrm[:, c, :], nrm[:, c, :]))
                    dve.wait_ge(mix_multiplied, n * 2)
                    TT(att[:, c, :], bank[2 + 2 * c][:, 0:NW], nrm[:, c, :], ALU.mult).then_inc(attention_normalised, 1)

            dve.memset(low[:, T * C:KVB], 0.0)
            query_map(0)
            st.restart(v0)
            for c in range(2):
                dve.wait_ge(normaliser_taken, c + 3)
                st.then(dve.reciprocal(nrm[:, c, :], nrm[:, c, :]))
                TT(att[:, c, :], bank[2 + 2 * c][:, 0:NW], nrm[:, c, :], ALU.mult).then_inc(attention_normalised, 1)
            with dve.Fori(1, NC) as n:
                dve.wait_ge(attention_multiplied, n * 2)
                query_map(n)
                normalised(n)
            st.restart(v0 + 2 * NC)

            npass = dve.value_load(celli[0:1, 0:1], min_val=1, max_val=N // WIN + 1)
            dve.wait_ge(mix_taken, 2 * NC + 2)
            st.did(TS1(low[:, 0:QB].bitcast(I32), low[:, 0:QB].bitcast(I32), 0, None, ALU.bitwise_and))
            st.did(dve.memset(low[:, QB:T * C], 0.0))
            st.did(dve.memset(low[:, KVB:4 * HTW], 0.0))
            dve.wait_ge(constants_made, 2)
            v0 = st.base + st.k
            halves = (slice(0, 4), slice(4, CT))
            banks = (psum[:, 2:4, :].rearrange("p b (t c) -> p (b t) c", c=C),
                     psum[:, 4:6, :].rearrange("p b (t c) -> p (b t) c", c=C)[:, 0:CT - 4, :])

            def split(q, b):
                dve.wait_ge(filters_multiplied, q * 2 + 2)
                dve.wait_ge(upper_parts_ready, q + 1)
                TT(lower, feat[b], upper.bitcast(F32), ALU.subtract).then_inc(features_split, 1)

            def chunk(p, c, use, j, more=True):
                d, q = j % DEPTH, p * NCH + c
                dve.wait_ge(gate_loaded[d], use * 16)
                dve.wait_ge(sources_gathered[d], use * (16 * CT))
                for h, ts in enumerate(halves):
                    dve.wait_ge(filters_multiplied, q * 2 + (h + 3))
                    TT(gath[d][:, ts, :], banks[h], gath[d][:, ts, :], ALU.mult).then_inc(filters_taken, 1)
                if more:
                    split(q + 1, (j + 1) % 2)
                for h, ts in enumerate(halves):
                    dve.wait_ge(filters_taken, q * 2 + (h + 3))
                    TT(gath[d][:, ts, :], gath[d][:, ts, :], gate[d][:, ts, :], ALU.mult).then_inc(first_messages_ready, 1)
                for h, ts in enumerate(halves):
                    dve.wait_ge(first_messages_ready, q * 2 + (h + 1))
                    TT(gate[d][:, ts, :], gath[d][:, ts, :], gate[d][:, ts, :], ALU.mult).then_inc(messages_ready, 1)

            def add_window(p, c, w):
                v = p * NWIN + c
                dve.wait_ge(window_transposed, v + 3)
                dve.wait_ge(window_added, v + 2)
                dve.sem_inc(waits_passed, 1)
                at = dve.value_load(basei[0:1, bass.ds(c, 1)], min_val=0, max_val=N)
                TT(hT[:, :, bass.ds(at, WIN)], hT[:, :, bass.ds(at, WIN)],
                   bank[6 + w % 2].rearrange("p (f w) -> p f w", f=4), ALU.add).then_inc(window_added, 1)

            U3 = NCH // DEPTH
            with dve.Fori(0, npass) as p:
                split(p * NCH, 0)
                for j in range(BODY):
                    chunk(p, j, p * U3 + (j // DEPTH + 1), j)
                    if j % 2 and j > 1:
                        add_window(p, j // 2 - 1, j // 2 - 1)
                with dve.Fori(1, NCH // BODY - 1) as i:
                    for j in range(BODY):
                        chunk(p, i * BODY + j, p * U3 + i * (BODY // DEPTH) + (j // DEPTH + 1), j)
                        if j % 2:
                            add_window(p, i * (BODY // 2) + (j // 2 - 1), j // 2 - 1)
                for j in range(BODY):
                    c = NCH - BODY + j
                    chunk(p, c, p * U3 + (c // DEPTH + 1), j, c + 1 < NCH)
                    if j % 2:
                        add_window(p, c // 2 - 1, j // 2 - 1)
                add_window(p, NWIN - 1, NWIN - 1)
                st.restart(v0 + p * 2)
                st.did(TS1(nrel[:, :, :], nrel[:, :, :], float(WIN), None, ALU.add))
                st.then(TS1(basef[:, :], basef[:, :], float(WIN), float(N), ALU.add, ALU.min))
                st.settle()
                dve.tensor_copy(basei[:, :], basef[:, :]).then_inc(windows_moved, 1)
                dve.wait_ge(windows_moved, p + 2)
            v0 = npass * 2 + v0

            st.restart(v0)
            dve.wait_ge(second_edges_loaded, 32)
            st.did(dve.memset(shared[:, :], 0.0))
            st.then(TS1(emask, edst, float(N), None, ALU.is_lt))
            A, B = cnt_a[:, 0:EC], cnt_b[:, 0:EC]
            st.then(STT(A, esrc, float(N - 1), emask, ALU.is_ge, ALU.mult))
            st.did(TT(emask, emask, A, ALU.subtract))
            st.then(STT(ekey, edst, 4096.0, esrc, ALU.mult, ALU.add))
            st.did(STT(ekey, ekey, 1.0, emask, ALU.add, ALU.mult))
            dve.tensor_reduce(small[:, 0:1], emask, AX, ALU.add).then_inc(windows_measured, 1)
            st.then(STT(B, edst, 1.0, A, ALU.add, ALU.mult))
            dve.sem_inc(windows_measured, 1)
            st.then(TS1(cnt_a, cnt_b, -0.5, 1.0 / RB, ALU.add, ALU.mult))
            st.then(TS1(cnt_a, cnt_a, -0.5, MAGIC, ALU.add, ALU.add))
            st.then(TS1(cnt_a, cnt_a, -MAGIC, None, ALU.add))
            st.then(STT(cnt_b, cnt_a, -float(RB), cnt_b, ALU.mult, ALU.add))
            st.then(TS1(cnt_b, cnt_b, -1.0, None, ALU.add))
            dve.wait_ge(reduced_over_partitions, 2)
            S0 = 8 * SORTED
            st.did(TS1(cellf[:, 1:2], ared[:, 0:1], 1.0 / 8, -(S0 - 7.5) / 8 - 0.5, ALU.mult, ALU.add))
            st.then(TS1(cellf[:, 2:3], ared[:, 0:1], 1.0 / G, -(G * ROUNDS - G + 0.5) / G - 0.5, ALU.mult, ALU.add))
            st.then(TS1(cellf[:, 1:3], cellf[:, 1:3], MAGIC, None, ALU.add))
            st.then(TS1(cellf[:, 1:3], cellf[:, 1:3], -MAGIC, 1.0, ALU.add, ALU.max))
            st.then(dve.tensor_copy(celli[:, 1:3], cellf[:, 1:3]))
            dve.sem_inc(waits_passed, 1)
            srem = dve.value_load(celli[0:1, 1:2], min_val=1, max_val=EC // 8 - SORTED)
            v0 = v0 + st.k

            def sort_step(st, s):
                st.did(dve.max(srt[:, :], ekey))
                st.settle()
                dve.sem_inc(waits_passed, 1)
                st.did(dve.match_replace(ekey, srt[:, :], ekey, 0.0))
                st.then(dve.tensor_copy(kbuf[:, bass.ds(s * 8, 8)], srt[:, :]))
                dve.sem_inc(waits_passed, 1)

            def leaky(n):
                for u in range(4):
                    dve.wait_ge(dense_biased, n * 4 + (u + 5))
                    STT(L[:, u, :], L[:, u, :], 0.1, L[:, u, :], ALU.mult, ALU.max).then_inc(dense_leaky, 1)

            def measure_features(n):
                dve.wait_ge(cat_taken, n * 2 + 4)
                for mm in range(2):
                    st.did(dve.bn_stats(gstat[:, mm, bass.ds(n, 1), :].rearrange("p o s -> p (o s)"),
                                        HT[:, mm, bass.ds(n * NW, NW)]))

            with dve.Fori(0, NC - 1) as n:
                st.restart(n * (3 * SORTS + 2) + v0)
                leaky(n)
                for s in range(SORTS):
                    sort_step(st, n * SORTS + s)
                measure_features(n)
            st.restart(v0 + (3 * SORTS + 2) * (NC - 1))
            leaky(NC - 1)
            measure_features(NC - 1)
            v0 = v0 + (3 * SORTS + 2) * (NC - 1) + 2
            st.restart(v0)
            st.settle()
            sort_steps, st = st, Steps(dve, vector_steps_second_half)
            dve.sem_inc(waits_passed, 1)
            for mm in range(2):
                st.did(dve.bn_aggr(gmv[:, mm, :], gstat[:, mm, :, :]))
            st.settle()
            st.then(STT(cols[:, 2 * CMU:2 * CMU + 2], gmv[:, :, 0], -1.0, cols[:, 2 * CGM:2 * CGM + 2],
                        ALU.mult, ALU.mult))
            st.then(TT(cols[:, 2 * CA:2 * CA + 2], gmv[:, :, 0], cols[:, 2 * CMU:2 * CMU + 2], ALU.add))
            st.then(TT(cols[:, 2 * CA:2 * CA + 2], cols[:, 2 * CA:2 * CA + 2], cols[:, 2 * CA:2 * CA + 2], ALU.mult))
            TT(cols[:, 2 * CVAR:2 * CVAR + 2], gmv[:, :, 1], cols[:, 2 * CA:2 * CA + 2], ALU.add).then_inc(graphnorm_steps, 1)
            dve.wait_ge(graphnorm_steps, 1)
            dve.wait_ge(graphnorm_root, 1)
            st.then(dve.reciprocal(cols[:, 2 * CA:2 * CA + 2], cols[:, 2 * CVAR:2 * CVAR + 2]))
            st.then(TT(cols[:, 2 * CA:2 * CA + 2], cols[:, 2 * CA:2 * CA + 2], cols[:, 2 * CGW:2 * CGW + 2], ALU.mult))
            st.then(TT(cols[:, 2 * CBB:2 * CBB + 2], cols[:, 2 * CA:2 * CA + 2], cols[:, 2 * CMU:2 * CMU + 2], ALU.mult))
            TT(cols[:, 2 * CBB:2 * CBB + 2], cols[:, 2 * CBB:2 * CBB + 2], cols[:, 2 * CGB:2 * CGB + 2],
               ALU.add).then_inc(graphnorm_coefficients, 1)
            for g in range(NC):
                dve.wait_ge(graphnorm_applied, g + 1)
                v = slice(NW * g, NW * g + NW)
                TT(mixT[:, :, v], HT[:, :, v], mixT[:, :, v], ALU.add).then_inc(sum_by_feature_ready, 1)
            def fold_logits():
                dve.wait_ge(gat_vectors_loaded, 16 * 7)
                for i in range(2):
                    for k in range(2):
                        st.did(TT(weighted.rearrange("p a b -> p (a b)")[:, (2 * i + k) * HE:(2 * i + k + 1) * HE], wg[:, k, 0:HE],
                                  attb[:, HE * i:HE * i + HE], ALU.mult))
                st.settle()
                for i in range(2):
                    for k in range(2):
                        ins = dve.tensor_reduce(wg[:, k, HE + 4 * i:HE + 4 * i + 4],
                                                weighted.rearrange("p a b -> p (a b)")[:, (2 * i + k) * HE:(2 * i + k + 1) * HE]
                                                .rearrange("p (h e) -> p h e", h=HEADS), AX, ALU.add)
                ins.then_inc(gat_weights_ready, 1)
            for g in range(NC):
                for t in range(BW * g, BW * g + BW):
                    dve.wait_ge(sum_transposed, t + 1)
                    TT(x_rows[0:NB, t, :], bank[t % 4][0:NB, 0:C], x_rows[0:NB, t, :], ALU.add).then_inc(sum_rows_ready, 1)
                dve.wait_ge(sum_rows_ready, BW * (g + 1))
                measure(x_rows, g)
                if g == 0:
                    dve.wait_ge(sum_by_feature_ready, NC)
                if g:
                    normalise(x_rows, rows2, 1, g - 1)
                if g == 1:
                    fold_logits()
            normalise(x_rows, rows2, 1, NC - 1)
            with dve.Fori(0, srem) as s:
                sort_steps.restart(s * 3 + v0)
                sort_step(sort_steps, s + SORTED)
            sort_steps.restart(srem * 3 + v0)
            sort_steps.settle()
            dve.sem_inc(waits_passed, 1)
            dve.memset(zeros, 0.0).then_inc(sums_cleared, 1)
            dve.wait_ge(tables_multiplied, 1)
            dve.tensor_copy(tab[0:NB], bank[4][0:NB, 0:24 * T].rearrange("p (t c) -> p t c", t=T)).then_inc(tables_ready, 1)
            dve.wait_ge(tables_ready, 1)
            st.then(dve.memset(logit_ends, -3e38))
            st.did(dve.tensor_reduce(logit_ends[0:NB, 0:4], tab[0:NB, :, HE:TS].rearrange("p t h -> p h t"), AX, ALU.max))
            st.then(dve.tensor_reduce(logit_ends[0:NB, 4:8], tab[0:NB, :, HE:TS].rearrange("p t h -> p h t"), AX, ALU.min))
            TS1(logit_ends[0:NB, 4:8], logit_ends[0:NB, 4:8], -1.0, None, ALU.mult).then_inc(logits_reduced, 1)
            st.did(dve.tensor_copy(td[0:NB, :, 0:4], tab[0:NB, :, TS:24]))
            dve.wait_ge(reduced_over_partitions, 3)
            st.then(TT(td[0:NB, :, 4:8], tab[0:NB, :, TS:24],
                       logit_ends_all[0:NB, 0:4].unsqueeze(1).broadcast_to((NB, T, 4)), ALU.add))
            st.then(TT(logit_ends[:, 8:12], logit_ends_all[:, 0:4], logit_ends_all[:, 4:8], ALU.add))
            st.then(dve.tensor_reduce(cellf[:, 3:4], logit_ends[:, 8:12], AX, ALU.max))
            st.then(TS1(cellf[:, 3:4], cellf[:, 3:4], SAFE, None, ALU.is_gt))
            dve.tensor_copy(celli[:, 3:4], cellf[:, 3:4]).then_inc(span_compared, 1)
            dve.wait_ge(span_compared, 1)
            dve.sem_inc(waits_passed, 1)
            wide = dve.value_load(celli[0:1, 3:4], min_val=0, max_val=1)
            with dve.If(wide):
                slow_steps = Steps(dve, slow_vector_steps)
                slow_steps.did(dve.memset(max_table_flat, 0.0))
                slow_steps.did(dve.tensor_scalar(niota[:, 0:P], iota[:, 0:P], 0.0, None, ALU.add))
                slow_steps.settle()
                for b in range(1, -(-N // P)):
                    w = min(P, N - P * b)
                    slow_steps.did(TS1(niota[:, P * b:P * b + w], iota[:, 0:w], float(P * b), None, ALU.add))
                dve.wait_ge(slow_edges_loaded, 32)
                slow_steps.settle()
                with dve.Fori(0, EC) as c:
                    slow_steps.restart(c * (4 + 2 * HEADS) + (1 + -(-N // P)))
                    slow_steps.settle()
                    slow_steps.did(dve.tensor_copy(sdf, sdst[:, bass.ds(c, 1)]))
                    slow_steps.then(dve.tensor_copy(srel[:, 0:1], ssrc[:, bass.ds(c, 1)]))
                    slow_steps.then(TS1(srel[:, 0:1], srel[:, 0:1], float(N - 1), None, ALU.min))
                    dve.tensor_copy(sidx, srel[:, 0:1]).then_inc(slow_sources_ready, 1)
                    dve.wait_ge(slow_sources_gathered, c * 16 + 16)
                    slow_steps.then(TT(srel, srow[:, HE:TS], logit_ends_all[:, 4:8], ALU.add))
                    for h in range(HEADS):
                        slow_steps.then(TS1(max_candidate, niota, sdf, srel[:, h:h + 1], ALU.is_equal, ALU.mult))
                        slow_steps.then(TT(max_table[:, :, h], max_table[:, :, h], max_candidate, ALU.max))
                dve.sem_inc(slow_maxima_by_partition, 1)
                dve.wait_ge(slow_maxima_loaded, 16)
                slow_steps.restart(EC * (4 + 2 * HEADS) + (1 + -(-N // P)))
                slow_steps.then(TT(segment_max[0:NB], segment_max[0:NB], logit_ends_all[0:NB, 4:8].unsqueeze(1).broadcast_to((NB, T, 4)), ALU.subtract))
                slow_steps.then(TT(segment_max[0:NB], segment_max[0:NB], tab[0:NB, :, HE:TS], ALU.max))
                slow_steps.then(TT(td[0:NB, :, 4:8], tab[0:NB, :, TS:24], segment_max[0:NB], ALU.add))
            STT(td[0:NB, :, 4:8], td[0:NB, :, 4:8], 0.2, td[0:NB, :, 4:8], ALU.mult, ALU.max).then_inc(tables_ready, 1)
            dve.wait_ge(tables_ready, 2)
            rem = dve.value_load(celli[0:1, 2:3], min_val=1, max_val=(EC - G * ROUNDS) // G + 1)

            def prepare(r):
                st.then(TS1(key_int, kbuf[:, bass.ds(r * G, G)], -1.0, None, ALU.add))
                st.did(TS1(nindex[:, 0], key_int, 4095, None, ALU.bitwise_and))
                st.then(TS1(dest_int, key_int, 12, None, ALU.arith_shift_right))
                st.did(TS1(nindex[:, 0], nindex[:, 0], float(N - 1), None, ALU.min))
                st.did(TS1(ndigits[:, 0], dest_int, 0.5, 1.0 / DW, ALU.add, ALU.mult))
                st.then(TS1(nindex[:, 1], dest_int, 0.0, None, ALU.max))
                st.then(TS1(ndigits[:, 0], ndigits[:, 0], -0.5, MAGIC, ALU.add, ALU.add))
                st.then(TS1(ndigits[:, 0], ndigits[:, 0], -MAGIC, None, ALU.add))
                st.did(STT(ndigits[:, 1], ndigits[:, 0], -float(DW), dest_int, ALU.mult, ALU.add))

            def begin(r, v):
                st.restart(v)
                st.settle()
                dve.wait_ge(round_gathered, r * (32 * G) + 32 * G)
                st.did(dve.tensor_copy(sources, got_sources))
                st.did(dve.tensor_copy(dests, got_dests))
                dve.tensor_copy(index, nindex).then_inc(round_indices_ready, 1)
                st.settle()
                st.then(TT(edge_logit, sources[:, :, HE:TS], dests[:, :, 0:4], ALU.add))
                st.then(STT(edge_logit, edge_logit, 0.2, edge_logit, ALU.mult, ALU.max))
                TT(edge_logit, edge_logit, dests[:, :, 4:8], ALU.subtract).then_inc(logits_ready, 1)
                st.did(TT(upper_digit_hot, over(digits[:, 0], P, G, DH), iota[:, 0:DH].unsqueeze(1).broadcast_to((P, G, DH)), ALU.is_equal))
                st.then(dve.tensor_copy(lower_digit, digits[:, 1]))
                st.then(dve.tensor_copy(digits, ndigits))
                dve.wait_ge(round_indices_ready, r + 2)
                prepare(r + 2)
                dve.wait_ge(exponents_ready, r + 1)
                st.did(TT(weighted[:, :, 0:HE].rearrange("p t (h e) -> p t h e", h=HEADS),
                          sources[:, :, 0:HE].rearrange("p t (h e) -> p t h e", h=HEADS),
                          over(edge_exp, P, G, HEADS, NEXP), ALU.mult))
                st.then(dve.tensor_copy(weighted[:, :, HE:TS], edge_exp))
                st.then(dve.tensor_copy(weighted_parts[:, :, 0, :].bitcast(F22), weighted))
                st.then(TT(weighted_parts[:, :, 1, :].bitcast(F22), weighted, weighted_parts[:, :, 0, :], ALU.subtract))

            def tile(r, i):
                dve.wait_ge(outer_summed, r * G + (i + 1))
                TS1(digit[i % 2], iota[:, :], lower_digit[:, i:i + 1], None, ALU.is_equal)
                TT(values[i % 2], upper_digit_hot[:, i:i + 1, :].unsqueeze(3).broadcast_to((P, 2, DH, TS)),
                   weighted_parts[:, i, :, :].unsqueeze(2).broadcast_to((P, 2, DH, TS)), ALU.mult).then_inc(outer_ready, 1)

            def quarter(r, k):
                dve.wait_ge(counts_summed, r * 4 + (k + 1))
                for buf, of in ((upper_hot[k % 2], cnt_a), (lower_hot[k % 2], cnt_b)):
                    ins = TT(buf, over(of[:, bass.ds(r * (4 * QT) + k * QT, QT)], P, QT, RB),
                             iota[:, 0:RB].unsqueeze(1).broadcast_to((P, QT, RB)), ALU.is_equal)
                ins.then_inc(counts_ready, 1)
                tile(r, 2 * k)
                tile(r, 2 * k + 1)

            prepare(0)
            st.settle()
            st.did(dve.tensor_copy(digits, ndigits))
            dve.tensor_copy(index, nindex).then_inc(round_indices_ready, 1)
            dve.wait_ge(round_indices_ready, 1)
            st.settle()
            prepare(1)
            dve.wait_ge(last_source_loaded, 16)
            R = slice(0, NB)
            st.did(TT(own_exp[R], tab[R, :, HE:TS], tab[R, :, TS:24], ALU.add))
            st.then(TT(last_exp[R], tab[R, :, TS:24], last[R, HE:TS].unsqueeze(1).broadcast_to((NB, T, 4)), ALU.add))
            st.did(STT(own_exp[R], own_exp[R], 0.2, own_exp[R], ALU.mult, ALU.max))
            st.then(STT(last_exp[R], last_exp[R], 0.2, last_exp[R], ALU.mult, ALU.max))
            st.did(TT(own_exp[R], own_exp[R], td[R, :, 4:8], ALU.subtract))
            TT(last_exp[R], last_exp[R], td[R, :, 4:8], ALU.subtract).then_inc(last_arguments, 1)

            def take(e, n):
                r = n + e * NC
                for h in range(2):
                    dve.wait_ge(expert_multiplied, r * 2 + (h + 3))
                    TT(Y[0:NB, bass.ds(n * BW + 2 * h, 2), e, :], bank[4 + h][0:NB, :].rearrange("p (b c) -> p b c", b=2),
                       b2b[0:NB, C * e:C * e + C].unsqueeze(1).broadcast_to((NB, 2, C)), ALU.add).then_inc(expert_taken, 1)

            take(0, 0)
            v0 = st.k
            begin(0, v0)
            per = st.k
            for e in range(NEXP - 1):
                with dve.Fori(0 if e else 1, NC) as n:
                    r = n + (e * NC - 1)
                    for k in range(4):
                        quarter(r, k)
                    begin(r + 1, n * per + (v0 + e * NC * per))
                    assert st.k == per
                    take(e, n)
            for k in range(4):
                quarter(ROUNDS - 1, k)
            begin(ROUNDS, v0 + ROUNDS * per)
            dve.wait_ge(counts_summed, 4 * ROUNDS + 2)
            dve.tensor_copy(pair_counts[0:RB, 0:RB], bank[7][0:RB, 0:RB]).then_inc(counts_copied, 1)
            v0 = v0 + (ROUNDS + 1) * per
            for t in range(G):
                tile(ROUNDS, t)
            with dve.If(rem - 1):
                with dve.Fori(1, rem) as r:
                    begin(r + ROUNDS, r * per + (v0 - per))
                    for t in range(G):
                        tile(r + ROUNDS, t)
            st.restart(rem * per + (v0 - per))

            dve.wait_ge(last_functions, 2)
            dve.wait_ge(counts_loaded, 16)
            st.did(TT(last_exp[R], last_exp[R], over(node_counts[R], NB, T, 4), ALU.mult))
            h4 = lambda v: v.rearrange("p t (h e) -> p t h e", h=HEADS)
            st.then(TT(h4(f1[R]), h4(tab[R, :, 0:HE]), over(own_exp[R], NB, T, HEADS, NEXP), ALU.mult))
            st.did(TT(own_exp[R], own_exp[R], last_exp[R], ALU.add))
            st.then(TT(h4(f2[R]), last[R, 0:HE].unsqueeze(1).broadcast_to((NB, T, HE)).rearrange("p t (h e) -> p t h e", h=HEADS),
                       over(last_exp[R], NB, T, HEADS, NEXP), ALU.mult))
            dve.wait_ge(value_sums_transposed, 1)
            st.then(dve.tensor_copy(agg[R].rearrange("p (d b) v -> p d b v", d=DH),
                                    bank[7][R, 0:T * TS].rearrange("p (b d v) -> p d b v", b=BW, d=DH)))
            st.did(TT(agg[R, :, 0:HE], agg[R, :, 0:HE], f1[R], ALU.add))
            st.then(TT(agg[R, :, HE:TS], agg[R, :, HE:TS], own_exp[R], ALU.add))
            st.did(TT(agg[R, :, 0:HE], agg[R, :, 0:HE], f2[R], ALU.add))
            st.then(TS1(own_exp[R], agg[R, :, HE:TS], 1e-16, None, ALU.add))
            st.then(dve.reciprocal(own_exp[R], own_exp[R]))
            st.then(TT(h4(f1[R]), h4(agg[R, :, 0:HE]), over(own_exp[R], NB, T, HEADS, NEXP), ALU.mult))

            def by_value(i):
                return bgb[R, HE * i:HE * i + HE].unsqueeze(1).broadcast_to((NB, T, HE))

            st.then(TT(f1[R], f1[R], by_value(0), ALU.add))
            st.then(dve.tensor_reduce(t1[R], f1[R], AX, ALU.add))
            st.then(TS1(t1[R], t1[R], -1.0 / HE, None, ALU.mult))
            st.then(TT(f1[R], f1[R], over(t1[R], NB, T, HE), ALU.add))
            st.then(TT(f2[R], f1[R], f1[R], ALU.mult))
            st.then(dve.tensor_reduce(t2[R], f2[R], AX, ALU.add))
            TS1(scores[R, :, 0], t2[R], 1.0 / HE, None, ALU.mult).then_inc(last_arguments, 1)
            dve.wait_ge(last_functions, 3)
            st.then(dve.reciprocal(t1[R], sd[R, :]))
            st.then(TT(f1[R], f1[R], over(t1[R], NB, T, HE), ALU.mult))
            st.then(TT(f1[R], f1[R], by_value(1), ALU.mult))
            st.then(TT(f1[R], f1[R], by_value(2), ALU.add))
            st.then(dve.tensor_reduce(scores[R], f1[R].rearrange("p t (h e) -> p t e h", h=HEADS), AX, ALU.add))
            st.did(TS1(scores[R], scores[R], 1.0 / HEADS, None, ALU.mult))
            st.then(dve.memset(rank[R], 0.0))
            for i in range(4):
                for j in range(i + 1, 4):
                    st.then(TT(t2[R], scores[R, :, i], scores[R, :, j], ALU.is_ge))
                    st.did(TT(rank[R, :, j], rank[R, :, j], t2[R], ALU.add))
                    st.did(TT(rank[R, :, i], rank[R, :, i], t2[R], ALU.subtract))
                    st.settle()
            for i in range(4):
                st.did(TS1(rank[R, :, i], rank[R, :, i], float(3 - i), None, ALU.add))
            st.then(dve.tensor_reduce(t1[R], scores[R], AX, ALU.max))
            TT(gates[R], scores[R], over(t1[R], NB, T, 4), ALU.subtract).then_inc(last_arguments, 1)
            dve.wait_ge(last_functions, 4)
            st.then(STT(gates[R], rank[R], 1.5, gates[R], ALU.is_lt, ALU.mult))
            st.then(dve.tensor_reduce(t1[R], gates[R], AX, ALU.add))
            st.then(dve.reciprocal(t1[R], t1[R]))
            st.then(TT(gates[R], gates[R], over(t1[R], NB, T, 4), ALU.mult))
            for g in range(NC):
                for e in range(NEXP):
                    if e == NEXP - 1:
                        dve.wait_ge(last_expert_biased, 2 * g + 2)
                    for b in range(BW):
                        t = g * BW + b
                        ins = STT(x_rows[R, t, :], Y[R, t, e, :], gates[R, t, e:e + 1], x_rows[R, t, :], ALU.mult, ALU.add)
                        if e == NEXP - 1 and b == BW - 1:
                            ins.then_inc(rows_finished, 1)
                        else:
                            st.did(ins)
                    if e < NEXP - 1:
                        st.settle()


def kernel(**a):
    import concourse.bacc as _bacc
    from concourse.bass_utils import run_bass_kernel_spmd as _run

    a = {k: np.asarray(v) for k, v in a.items()}
    EP = NCH * CH

    def pad(v, fill):
        return np.concatenate([v, np.full((EP - E1,) + v.shape[1:], fill, v.dtype)])

    src = pad(a["src"], 0).reshape(NCH, P, CT)
    src = np.concatenate([src, src[:AHEAD]])

    arrays = {
        "x": a["x"],
        "src": src,
        "dst": pad(a["dst"], N - 1).reshape(NCH, P, CT),
        "ea54": pad(a["edge_attr_54"], 0).reshape(NCH, P, CT, 54).transpose(0, 3, 2, 1),
        "ea256": pad(a["edge_attr_256"], 0).reshape(NCH, P, CT * C),
        "edges": a["L0_ffn_edge_index"],
        "wf1aT": a["L0_gnn_w_f1a"].T,
        "wf1b": a["L0_gnn_w_f1b"],
        "wlrT": np.stack([a[f"L0_gnn_{k}"].T for k in ("c1_wl", "c1_wr", "c2_wl", "c2_wr")]),
        "lin": np.stack([a["L0_gnn_lin1_w"], a["L0_gnn_lin2_w"]]),
        "catw": a["L0_gnn_cat_w"],
        "vecs": np.concatenate([a[f"L0_{k}"].reshape(2, P) for k in (
            "gnn_c1_bl", "gnn_c2_bl", "gnn_lin1_b", "gnn_lin2_b", "gnn_cat_b", "gnn_gn_w", "gnn_gn_b",
            "gnn_gn_ms", "mix_bq", "mix_bo")]).T,
        "wkv": np.concatenate([a["L0_mix_wk"], a["L0_mix_wv"]], axis=1),
        "bkv": np.concatenate([a["L0_mix_bk"], a["L0_mix_bv"]]),
        "wq": a["L0_mix_wq"], "wo": a["L0_mix_wo"],
        "wgat": a["L0_ffn_W_gat"], "atts": a["L0_ffn_att_src"].reshape(HE), "attd": a["L0_ffn_att_dst"].reshape(HE),
        "bgat": a["L0_ffn_b_gat"], "lng": a["L0_ffn_ln_gamma"], "lnb": a["L0_ffn_ln_beta"],
        "w1": a["L0_ffn_W1"], "b1": a["L0_ffn_b1"].reshape(NEXP * HM, P).T, "w2": a["L0_ffn_W2"], "b2": a["L0_ffn_b2"],
    }
    arrays = {f"in_{k}": np.ascontiguousarray(v) for k, v in arrays.items()}
    nc = _bacc.Bacc("TRN2", target_bir_lowering=False, num_devices=1)
    aps = {k[3:]: nc.dram_tensor(k, v.shape, mybir.dt.from_np(v.dtype), kind="ExternalInput").ap()
           for k, v in arrays.items()}
    out = nc.dram_tensor("out_rows", (N, C), F32, kind="ExternalOutput").ap()
    build(nc, out=out, **aps)
    r = _run(nc, [arrays], core_ids=[0])
    return r.results[0]["out_rows"]
```
